# Optimizing a Trainium2 kernel written in Bass

```python
import numpy as np
import jax
import jax.numpy as jnp

def _softmax(x, axis=-1):
    return jax.nn.softmax(x, axis=axis)

def _gelu(x):
    return jax.nn.gelu(x, approximate=True)

def _silu(x):
    return jax.nn.silu(x)

def _sigmoid(x):
    return jax.nn.sigmoid(x)

def _layernorm(x, axis=-1, eps=1e-05):
    m = jnp.mean(x, axis=axis, keepdims=True)
    v = jnp.var(x, axis=axis, keepdims=True)
    return (x - m) / jnp.sqrt(v + eps)

def _scatter_add(tgt, idx, src, axis=0):
    return tgt.at[idx].add(src)

def _segment_sum(src, seg, n):
    return jax.ops.segment_sum(src, seg, n)
kernel_name = 'mk_flamingo_gated_d2_seqx_r8_ee9be9'

def setup_inputs(seed: int=0):
    np.random.seed(seed)
    _w = jnp.asarray

    def _rec_inputs():
        import jax
        import jax.numpy as jnp
        _rk = jax.random.key(seed)
        x = 7.22e-05 + 1 * jax.random.normal(jax.random.fold_in(_rk, 1), (32, 64, 128), jnp.float32)
        _lenS = 64 - jax.random.randint(jax.random.fold_in(_rk, 7), (32,), 0, max(1, 64 // 4) + 1, jnp.int32)
        _lenS2 = 64 - jax.random.randint(jax.random.fold_in(_rk, 8), (32,), 0, max(1, 64 // 4) + 1, jnp.int32)
        _ctx_1024P = jax.random.normal(jax.random.fold_in(_rk, 11), (32, 16, 128), jnp.float32)
        _ctx_1024c = jax.random.dirichlet(jax.random.fold_in(_rk, 511), 0.3 * jnp.ones((16,), jnp.float32), (32, 64))
        _ctx_1024t = jnp.einsum('bsk,bkd->bsd', _ctx_1024c, _ctx_1024P)
        _ctx_1024t = _ctx_1024t * jax.lax.rsqrt(jnp.mean(jnp.square(_ctx_1024t)) + 1e-12) * 0.953939
        ctx_1024 = 4.13588e-05 + 0.999923 * (_ctx_1024t + 0.3 * jax.random.normal(jax.random.fold_in(_rk, 611), (32, 64, 128), jnp.float32))
        _validS = jnp.arange(64)[None, :] < _lenS[:, None]
        _validS2 = jnp.arange(64)[None, :] < _lenS2[:, None]
        _causal = jnp.tril(jnp.ones((64, 64), dtype=bool))
        mask_BxSxS2_if1 = jnp.where(jnp.ones((32, 64, 64), dtype=bool), 1, 0).astype(jnp.int32)
        _g = jax.random.normal(jax.random.fold_in(_rk, 9001), (2, 2), jnp.float32)
        _g = jnp.sign(_g) * jnp.maximum(jnp.abs(_g), 1.0) + (_g == 0) * 1.0
        g_xattn = _g[0]
        g_ffn = _g[1]
        return (x, ctx_1024, mask_BxSxS2_if1, g_xattn, g_ffn)
    x, ctx_1024, mask_BxSxS2_if1, g_xattn, g_ffn = _rec_inputs()

    def _L0_xattn_setup():
        import jax, jax.numpy as jnp
        import numpy as np
        B, SQ, SKV, E, H = (4, 256, 256, 128, 16)
        D = E // H
        key = jax.random.key(seed)
        ks = jax.random.split(key, 8)
        s = 1.0 / np.sqrt(D)
        return {'query': jax.random.normal(ks[0], (B, SQ, E), jnp.float32), 'key_value': jax.random.normal(ks[1], (B, SKV, E), jnp.float32), 'wq': jax.random.normal(ks[2], (H, D, D), jnp.float32) * s, 'bq': jnp.zeros((H, D), jnp.float32), 'wk': jax.random.normal(ks[3], (H, D, D), jnp.float32) * s, 'bk': jnp.zeros((H, D), jnp.float32), 'wv': jax.random.normal(ks[4], (H, D, D), jnp.float32) * s, 'bv': jnp.zeros((H, D), jnp.float32), 'wo': jax.random.normal(ks[5], (E, E), jnp.float32) * (1.0 / np.sqrt(E)), 'bo': jnp.zeros((E,), jnp.float32)}
    _L0_xattn_all = _L0_xattn_setup()
    _L0_xattn_in = {k: v for k, v in _L0_xattn_all.items() if k in ('wq', 'bq', 'wk', 'bk', 'wv', 'bv', 'wo', 'bo')}
    del _L0_xattn_all

    def _L0_ffn_setup():
        import jax, jax.numpy as jnp
        import numpy as np
        DIM = 128
        INTER = 64
        E = 8
        TOP_K = 2
        ROUTE_SCALE = 1.0
        key = jax.random.key(seed)
        ks = jax.random.split(key, 8)
        s_d = 1.0 / np.sqrt(DIM)
        s_f = 1.0 / np.sqrt(INTER)
        x = jax.random.normal(ks[0], (2, 256, DIM), dtype=jnp.float32)
        gate_w = jax.random.uniform(ks[1], (E, DIM), jnp.float32, -s_d, s_d)
        wg = jax.random.uniform(ks[2], (E, INTER, DIM), jnp.float32, -s_d, s_d)
        wu = jax.random.uniform(ks[3], (E, INTER, DIM), jnp.float32, -s_d, s_d)
        wd = jax.random.uniform(ks[4], (E, DIM, INTER), jnp.float32, -s_f, s_f)
        sg = jax.random.uniform(ks[5], (INTER, DIM), jnp.float32, -s_d, s_d)
        su = jax.random.uniform(ks[6], (INTER, DIM), jnp.float32, -s_d, s_d)
        sd = jax.random.uniform(ks[7], (DIM, INTER), jnp.float32, -s_f, s_f)
        return {'x': x, 'gate_w': gate_w, 'wg': wg, 'wu': wu, 'wd': wd, 'sg': sg, 'su': su, 'sd': sd}
    _L0_ffn_all = _L0_ffn_setup()
    _L0_ffn_in = {k: v for k, v in _L0_ffn_all.items() if k in ('gate_w', 'wg', 'wu', 'wd', 'sg', 'su', 'sd')}
    del _L0_ffn_all

    def _L1_xattn_setup():
        import jax, jax.numpy as jnp
        import numpy as np
        HEAD_NUM = 16
        D_MODEL = 128
        NEG = -1000000000.0
        key = jax.random.key(seed)
        ks = jax.random.split(key, 12)
        B, S, D = (2, 256, D_MODEL)
        inp = {'query': jax.random.normal(ks[0], (B, S, D), jnp.float32), 'key': jax.random.normal(ks[1], (B, S, D), jnp.float32), 'value': jax.random.normal(ks[2], (B, S, D), jnp.float32), 'mask': jnp.ones((B, S, S), jnp.int32)}
        scale = 1.0 / np.sqrt(D)
        for i in range(4):
            inp[f'W{i}'] = jax.random.normal(ks[3 + i], (D, D), jnp.float32) * scale
            inp[f'b{i}'] = jnp.zeros((D,), jnp.float32)
        return inp
    _L1_xattn_all = _L1_xattn_setup()
    _L1_xattn_in = {k: v for k, v in _L1_xattn_all.items() if k in ('W0', 'b0', 'W1', 'b1', 'W2', 'b2', 'W3', 'b3')}
    del _L1_xattn_all

    def _L1_ffn_setup():
        import jax, jax.numpy as jnp
        import numpy as np
        S, B, D, H, DH = (512, 8, 128, 16, 64)

        def _forward(x, Wg, Wq, bq, Wkv, bkv, Wo, bo, ln_g, ln_b):
            s_len, bsz, d_model = x.shape
            n_head, _, d_head = Wq.shape
            cap = s_len // n_head
            scale = 1.0 / d_head ** 0.5
            h = jnp.transpose(x, (1, 0, 2))
            t = h
            probs = jax.nn.softmax(h @ Wg, axis=-1)
            scores = jnp.transpose(probs, (0, 2, 1))
            _, idx = jax.lax.top_k(scores, cap)
            idx = jnp.sort(idx, axis=-1)
            hg = jnp.take_along_axis(h[:, None, :, :], idx[..., None], axis=2)
            hg = jnp.transpose(hg, (1, 0, 2, 3))
            q = jnp.einsum('hbcd,hde->hbce', hg, Wq) + bq[:, None, None, :]
            kv = jnp.einsum('hbcd,hde->hbce', hg, Wkv) + bkv[:, None, None, :]
            k, v = jnp.split(kv, 2, axis=-1)
            att = jnp.einsum('hbid,hbjd->hbij', q, k) * scale
            p = jax.nn.softmax(att, axis=1)
            av = jnp.einsum('hbij,hbjd->hbid', p, v)
            ao = jnp.einsum('hbid,hde->hbie', av, Wo) + bo
            tok = jnp.transpose(idx, (1, 0, 2))
            b_ids = jnp.arange(bsz)[None, :, None]
            outs = jnp.zeros_like(t).at[b_ids, tok].add(ao)
            y = t + outs
            mu = jnp.mean(y, axis=-1, keepdims=True)
            var = jnp.var(y, axis=-1, keepdims=True)
            yn = (y - mu) * jax.lax.rsqrt(var + 1e-05) * ln_g + ln_b
            return jnp.transpose(yn, (1, 0, 2))
        key = jax.random.key(seed)
        ks = jax.random.split(key, 6)
        s = 0.02
        return {'x': jax.random.normal(ks[0], (S, B, D), jnp.float32), 'attn_mask': jnp.zeros((S, S), jnp.bool_), 'Wg': jax.random.normal(ks[1], (D, H), jnp.float32) * s, 'Wq': jax.random.normal(ks[2], (H, D, DH), jnp.float32) * s, 'bq': jnp.zeros((H, DH), jnp.float32), 'Wkv': jax.random.normal(ks[3], (H, D, 2 * DH), jnp.float32) * s, 'bkv': jnp.zeros((H, 2 * DH), jnp.float32), 'Wo': jax.random.normal(ks[4], (H, DH, D), jnp.float32) * s, 'bo': jnp.zeros((D,), jnp.float32), 'ln_g': jnp.ones((D,), jnp.float32), 'ln_b': jnp.zeros((D,), jnp.float32)}
    _L1_ffn_all = _L1_ffn_setup()
    _L1_ffn_in = {k: v for k, v in _L1_ffn_all.items() if k in ('attn_mask', 'Wg', 'Wq', 'bq', 'Wkv', 'bkv', 'Wo', 'bo', 'ln_g', 'ln_b')}
    del _L1_ffn_all
    return {'x': x, 'ctx_1024': ctx_1024, 'mask_BxSxS2_if1': mask_BxSxS2_if1, 'g_xattn': g_xattn, 'g_ffn': g_ffn, 'L0_xattn_wq': _L0_xattn_in['wq'], 'L0_xattn_bq': _L0_xattn_in['bq'], 'L0_xattn_wk': _L0_xattn_in['wk'], 'L0_xattn_bk': _L0_xattn_in['bk'], 'L0_xattn_wv': _L0_xattn_in['wv'], 'L0_xattn_bv': _L0_xattn_in['bv'], 'L0_xattn_wo': _L0_xattn_in['wo'], 'L0_xattn_bo': _L0_xattn_in['bo'], 'L0_ffn_gate_w': _L0_ffn_in['gate_w'], 'L0_ffn_wg': _L0_ffn_in['wg'], 'L0_ffn_wu': _L0_ffn_in['wu'], 'L0_ffn_wd': _L0_ffn_in['wd'], 'L0_ffn_sg': _L0_ffn_in['sg'], 'L0_ffn_su': _L0_ffn_in['su'], 'L0_ffn_sd': _L0_ffn_in['sd'], 'L1_xattn_W0': _L1_xattn_in['W0'], 'L1_xattn_b0': _L1_xattn_in['b0'], 'L1_xattn_W1': _L1_xattn_in['W1'], 'L1_xattn_b1': _L1_xattn_in['b1'], 'L1_xattn_W2': _L1_xattn_in['W2'], 'L1_xattn_b2': _L1_xattn_in['b2'], 'L1_xattn_W3': _L1_xattn_in['W3'], 'L1_xattn_b3': _L1_xattn_in['b3'], 'L1_ffn_attn_mask': _L1_ffn_in['attn_mask'], 'L1_ffn_Wg': _L1_ffn_in['Wg'], 'L1_ffn_Wq': _L1_ffn_in['Wq'], 'L1_ffn_bq': _L1_ffn_in['bq'], 'L1_ffn_Wkv': _L1_ffn_in['Wkv'], 'L1_ffn_bkv': _L1_ffn_in['bkv'], 'L1_ffn_Wo': _L1_ffn_in['Wo'], 'L1_ffn_bo': _L1_ffn_in['bo'], 'L1_ffn_ln_g': _L1_ffn_in['ln_g'], 'L1_ffn_ln_b': _L1_ffn_in['ln_b']}

def reference(x, ctx_1024, mask_BxSxS2_if1, g_xattn, g_ffn, L0_xattn_wq, L0_xattn_bq, L0_xattn_wk, L0_xattn_bk, L0_xattn_wv, L0_xattn_bv, L0_xattn_wo, L0_xattn_bo, L0_ffn_gate_w, L0_ffn_wg, L0_ffn_wu, L0_ffn_wd, L0_ffn_sg, L0_ffn_su, L0_ffn_sd, L1_xattn_W0, L1_xattn_b0, L1_xattn_W1, L1_xattn_b1, L1_xattn_W2, L1_xattn_b2, L1_xattn_W3, L1_xattn_b3, L1_ffn_attn_mask, L1_ffn_Wg, L1_ffn_Wq, L1_ffn_bq, L1_ffn_Wkv, L1_ffn_bkv, L1_ffn_Wo, L1_ffn_bo, L1_ffn_ln_g, L1_ffn_ln_b):
    import jax
    import jax.numpy as jnp

    def _L0_xattn_ref(query, key_value, wq, bq, wk, bk, wv, bv, wo, bo):
        import jax, jax.numpy as jnp
        import numpy as np
        B, SQ, SKV, E, H = (4, 256, 256, 128, 16)
        D = E // H
        b, sq, e = query.shape
        skv = key_value.shape[1]
        h, d = (wq.shape[0], wq.shape[1])
        q = query.reshape(b, sq, h, d)
        kv = key_value.reshape(b, skv, h, d)
        qh = jnp.einsum('bshd,hed->bshe', q, wq) + bq
        kh = jnp.einsum('bthd,hed->bthe', kv, wk) + bk
        vh = jnp.einsum('bthd,hed->bthe', kv, wv) + bv
        scores = jnp.einsum('bshd,bthd->bhst', qh, kh) / jnp.sqrt(jnp.asarray(d, qh.dtype))
        attn = jax.nn.softmax(scores, axis=-1)
        ctx = jnp.einsum('bhst,bthd->bshd', attn, vh)
        out = ctx.reshape(b, sq, e)
        return out @ wo.T + bo

    def _L0_ffn_ref(x, gate_w, wg, wu, wd, sg, su, sd):
        import jax, jax.numpy as jnp
        import numpy as np
        DIM = 128
        INTER = 64
        E = 8
        TOP_K = 2
        ROUTE_SCALE = 1.0
        B, S, D = x.shape
        xf = x.reshape(-1, D)
        N = xf.shape[0]
        scores = jax.nn.softmax(xf @ gate_w.T, axis=-1)
        _, idx = jax.lax.top_k(scores, TOP_K)
        weights = jnp.take_along_axis(scores, idx, axis=-1) * ROUTE_SCALE
        cw = jnp.zeros((N, E), dtype=xf.dtype)
        cw = cw.at[jnp.arange(N)[:, None], idx].add(weights)
        g = jnp.einsum('nd,efd->nef', xf, wg)
        u = jnp.einsum('nd,efd->nef', xf, wu)
        h = jax.nn.silu(g) * u
        y = jnp.einsum('nef,edf->ned', h, wd)
        routed = jnp.einsum('ned,ne->nd', y, cw)
        shared = jax.nn.silu(xf @ sg.T) * (xf @ su.T) @ sd.T
        return (routed + shared).reshape(B, S, D)

    def _L1_xattn_ref(query, key, value, mask, W0, b0, W1, b1, W2, b2, W3, b3):
        import jax, jax.numpy as jnp
        import numpy as np
        HEAD_NUM = 16
        D_MODEL = 128
        NEG = -1000000000.0
        B, Sq, D = query.shape
        Sk = key.shape[1]
        H, dk = (HEAD_NUM, D // HEAD_NUM)
        q = (query @ W0.T + b0).reshape(B, Sq, H, dk).transpose(0, 2, 1, 3)
        k = (key @ W1.T + b1).reshape(B, Sk, H, dk).transpose(0, 2, 1, 3)
        v = (value @ W2.T + b2).reshape(B, Sk, H, dk).transpose(0, 2, 1, 3)
        scores = jnp.einsum('bhqd,bhkd->bhqk', q, k) / jnp.sqrt(jnp.float32(dk))
        scores = jnp.where(mask[:, None, :, :] == 0, NEG, scores)
        p_attn = jax.nn.softmax(scores, axis=-1)
        x = jnp.einsum('bhqk,bhkd->bhqd', p_attn, v)
        x = x.transpose(0, 2, 1, 3).reshape(B, Sq, D)
        return x @ W3.T + b3

    def _L1_ffn_ref(x, attn_mask, Wg, Wq, bq, Wkv, bkv, Wo, bo, ln_g, ln_b):
        import jax, jax.numpy as jnp
        import numpy as np
        S, B, D, H, DH = (512, 8, 128, 16, 64)

        def _forward(x, Wg, Wq, bq, Wkv, bkv, Wo, bo, ln_g, ln_b):
            s_len, bsz, d_model = x.shape
            n_head, _, d_head = Wq.shape
            cap = s_len // n_head
            scale = 1.0 / d_head ** 0.5
            h = jnp.transpose(x, (1, 0, 2))
            t = h
            probs = jax.nn.softmax(h @ Wg, axis=-1)
            scores = jnp.transpose(probs, (0, 2, 1))
            _, idx = jax.lax.top_k(scores, cap)
            idx = jnp.sort(idx, axis=-1)
            hg = jnp.take_along_axis(h[:, None, :, :], idx[..., None], axis=2)
            hg = jnp.transpose(hg, (1, 0, 2, 3))
            q = jnp.einsum('hbcd,hde->hbce', hg, Wq) + bq[:, None, None, :]
            kv = jnp.einsum('hbcd,hde->hbce', hg, Wkv) + bkv[:, None, None, :]
            k, v = jnp.split(kv, 2, axis=-1)
            att = jnp.einsum('hbid,hbjd->hbij', q, k) * scale
            p = jax.nn.softmax(att, axis=1)
            av = jnp.einsum('hbij,hbjd->hbid', p, v)
            ao = jnp.einsum('hbid,hde->hbie', av, Wo) + bo
            tok = jnp.transpose(idx, (1, 0, 2))
            b_ids = jnp.arange(bsz)[None, :, None]
            outs = jnp.zeros_like(t).at[b_ids, tok].add(ao)
            y = t + outs
            mu = jnp.mean(y, axis=-1, keepdims=True)
            var = jnp.var(y, axis=-1, keepdims=True)
            yn = (y - mu) * jax.lax.rsqrt(var + 1e-05) * ln_g + ln_b
            return jnp.transpose(yn, (1, 0, 2))
        return _forward(x, Wg, Wq, bq, Wkv, bkv, Wo, bo, ln_g, ln_b)
    x = x + jnp.tanh(g_xattn[0]) * _L0_xattn_ref(_layernorm(x, axis=-1), ctx_1024, L0_xattn_wq, L0_xattn_bq, L0_xattn_wk, L0_xattn_bk, L0_xattn_wv, L0_xattn_bv, L0_xattn_wo, L0_xattn_bo)
    x = x + jnp.tanh(g_ffn[0]) * _L0_ffn_ref(_layernorm(x, axis=-1), L0_ffn_gate_w, L0_ffn_wg, L0_ffn_wu, L0_ffn_wd, L0_ffn_sg, L0_ffn_su, L0_ffn_sd)
    x = x + jnp.tanh(g_xattn[1]) * _L1_xattn_ref(_layernorm(x, axis=-1), ctx_1024, ctx_1024, mask_BxSxS2_if1, L1_xattn_W0, L1_xattn_b0, L1_xattn_W1, L1_xattn_b1, L1_xattn_W2, L1_xattn_b2, L1_xattn_W3, L1_xattn_b3)
    x = x + jnp.tanh(g_ffn[1]) * _L1_ffn_ref(_layernorm(x, axis=-1), L1_ffn_attn_mask, L1_ffn_Wg, L1_ffn_Wq, L1_ffn_bq, L1_ffn_Wkv, L1_ffn_bkv, L1_ffn_Wo, L1_ffn_bo, L1_ffn_ln_g, L1_ffn_ln_b)
    return x

_drawn_inputs = setup_inputs


def setup_inputs(seed=0):
    import zlib

    import numpy as np

    out = dict(_drawn_inputs(seed))
    spreads = {'g_ffn': (-1.0, 0.2),
     'L0_xattn_bq': (0.0, 0.1),
     'L0_xattn_bk': (0.0, 0.8),
     'L0_xattn_bv': (0.0, 0.1),
     'L0_xattn_bo': (0.0, 0.1),
     'L1_xattn_b0': (0.0, 0.1),
     'L1_xattn_b1': (0.0, 0.8),
     'L1_xattn_b2': (0.0, 0.1),
     'L1_xattn_b3': (0.0, 0.1),
     'L1_ffn_bq': (0.0, 0.8),
     'L1_ffn_bkv': (0.0, 0.8),
     'L1_ffn_bo': (0.0, 0.1),
     'L1_ffn_ln_g': (1.0, 0.2),
     'L1_ffn_ln_b': (0.0, 0.1)}
    factors = {'L1_ffn_Wq': 8.0, 'L1_ffn_Wkv': 8.0, 'L1_ffn_Wo': 8.0}
    for name, (base, spread) in spreads.items():
        noise = np.random.default_rng([zlib.crc32(name.encode()), seed]).standard_normal(out[name].shape)
        drawn = base * np.exp(spread * noise) if base else spread * noise
        out[name] = jnp.asarray(drawn.astype(out[name].dtype))
    for name, factor in factors.items():
        out[name] = (out[name] * factor).astype(out[name].dtype)
    return out
```

```python
from contextlib import ExitStack

import numpy as np
import concourse.bass as bass
from concourse import mybir

ALU = mybir.AluOpType
ACT = mybir.ActivationFunctionType
AX = mybir.AxisListType
F32 = mybir.dt.float32
BF16 = mybir.dt.bfloat16
I32 = mybir.dt.int32

P = 128
B, S, D = 32, 64, 128
NG, NI, DH = 4, 4, 8
NT = B * S // P
CB = 8
CW = CB * S
CT = CW // P
NC = B // CB
NA = 2 * NC
NE, F = 8, 64
NP = NE // 2
H1, E1, CAP = 16, 64, 2
NQ, SP = 4, S // 4
SCALE = float(DH) ** -0.5
SCALE1 = float(E1) ** -0.5
BIG = -(2.0 ** 100)
EPS = 1e-5


def columns(widths):
    at, out = 0, {}
    for name, w in widths:
        out[name] = (at, w)
        at += w
    return out, at


CF, CF_N = columns([("ident", P), ("gmask", NG), ("imask", NI), ("cmask", 4), ("ones_v", 64),
                    ("first8", CT * NE), ("first32", B)])
CBF, CBF_N = columns([("ident", P), ("pick", CB * P), ("experts", NP * P), ("twice", P)])
WA, WA_N = columns([("wq0", P), ("wk0", P), ("wv0", P), ("wo0", P), ("bo0", P), ("bq0", 1), ("bk0", 1),
                    ("bv0", 1), ("gates", 4), ("gate_w", NE)])
WB, WB_N = columns([("wq1", P), ("wk1", P), ("wv1", P), ("wo1", P), ("bo1", P), ("bq1", 1), ("bk1", 1),
                    ("bv1", 1)])
WF, WF_N = columns([("wg", NE * F), ("wu", NE * F), ("shared", 2 * F), ("wd", NP * D), ("sd", D)])
WL, WL_N = columns([("Wg", H1), ("bo", 1), ("ln_g", D), ("ln_b", D), ("Wo", H1 * D),
                    ("Wqkv", H1 * 3 * E1), ("bqkv", H1 // 2 * 3 * E1)])


def general_jobs():
    jobs = [("bias", 0)]
    for n in (0, 1):
        jobs += [("xT", n), ("Q", n), ("K", n), ("V", n, 0), ("V", n, 1)]
        if n == 0:
            jobs += [("maxT", 0)]
    for n in range(NA):
        if n + 2 < NA:
            jobs += [("xT", n + 2), ("Q", n + 2), ("K", n + 2), ("V", n + 2, 0), ("V", n + 2, 1)]
        if n + 1 < NA:
            jobs += [("maxT", n + 1)]
        if n < NC:
            jobs += [("O", n)]
        if 1 <= n <= NC:
            c = n - 1
            jobs += [("logits", c)]
            for p in range(NP):
                jobs += [("G", c, p), ("U", c, p)]
            jobs += [("shared", c), ("weightT", c)]
            jobs += [("W", c, p) for p in range(NP)]
            jobs += [("Y", c)]
        if n < NC:
            jobs += [("fT", n)]
        if n == 1:
            jobs += [("bias", 1)]
    for k in range(NT // CT):
        jobs += [("O1", k)]
    for k in range(NT // CT):
        jobs += [("hT", k)]
    jobs += [("tlog",), ("probT",), ("hotT", 0), ("hotT", 1)]
    jobs += [("take", k) for k in range(NT // CT)]
    jobs += [("qkv", k) for k in range(H1 // 2)]
    jobs += [("attT",), ("attB",)]
    jobs += [("avT", k) for k in range(2)]
    jobs += [("ao", k) for k in range(NT // CT)]
    jobs += [("aoT", k) for k in range(NT // CT)]
    jobs += [("back", k) for k in range(NT // CT)]
    return jobs


def two_layers(nc, x, ctxT, maskT, const_f, const_b, w_a, w_b, w_f, w_l, out):
    jobs = {job: k for k, job in enumerate(general_jobs())}
    stack = ExitStack()
    with stack:
        def sb(name, shape, dt=F32):
            return stack.enter_context(nc.sbuf_tensor(name, shape, dt))

        def bank(name):
            return stack.enter_context(nc.psum_tensor(name, [P, 512], F32))

        def sem(name):
            return stack.enter_context(nc.semaphore(name))

        cf = sb("cf", [P, CF_N])
        cb = sb("cb", [P, CBF_N], BF16)
        wa = sb("wa", [P, WA_N])
        wb = sb("wb", [P, WB_N])
        wf = sb("wf", [P, WF_N])
        wl = sb("wl", [P, WL_N])
        xa = sb("xa", [P, NT, D])
        xn = sb("xn", [P, CT, D])
        fn = sb("fn", [P, CT, D])
        stats = sb("stats", [P, 16, 6])
        mean_var = sb("mean_var", [P, 16, 2])
        var_eps = sb("var_eps", [P, 16])
        rstd = sb("rstd", [P, 16])
        half_neg = sb("half_neg", [P, 16])
        xT = sb("xT", [P, 2, CW])
        fT = sb("fT", [P, CW])
        cT = sb("cT", [P, B * S])
        Qg = sb("Qg", [P, 2, CB, NG, S])
        Ki = sb("Ki", [P, 2, CB, NI, S])
        Qb = sb("Qb", [P, CB, NG, S], BF16)
        Kb = sb("Kb", [P, CB, NI, S], BF16)
        V2 = sb("V2", [P, 2, CB, 2, P])
        pT = sb("pT", [P, 3, 512])
        nmax = sb("nmax", [P, 2, CB * 8])
        nmax2 = sb("nmax2", [P, 2, CB * 8], BF16)
        shift = sb("shift", [P, 2, 512], BF16)
        den = sb("den", [P, 512])
        oT = sb("oT", [P, B * S])
        mask = sb("mask", [S, B * S], I32)
        maskb = sb("maskb", [P, B, 2, S], BF16)
        gated = sb("gated", [P, 4])
        bqg = sb("bqg", [P, 2, NG])
        bki = sb("bki", [P, 2, NI])
        obias = sb("obias", [P, 2, D])
        lg = sb("lg", [P, CT, NE])
        lw = sb("lw", [P, CT, NE])
        hot1 = sb("hot1", [P, CT, NE])
        hot2 = sb("hot2", [P, CT, NE])
        pr = sb("pr", [P, CT, NE])
        r4 = sb("r4", [P, 4, CT])
        cw3 = sb("cw3", [P, CT, 3, NE], BF16)
        cwT = sb("cwT", [P, CW], BF16)
        sil = sb("sil", [P, 2, CW])
        gu = sb("gu", [P, NP + 1, CW])
        hid = sb("hid", [P, NP, CW])
        xr = sb("xr", [P, SP, D])
        hn = sb("hn", [P, SP, D])
        at = Qg[:, :, :, :, :].rearrange("p a b g s -> p (a b g s)")
        hT = at[:, 0:2048].rearrange("p (h c s) -> p h c s", h=H1, c=CAP)
        avT = at[:, 2048:4096].rearrange("p (h c s) -> p h c s", h=H1, c=CAP)
        at = Ki[:, :, :, :, :].rearrange("p a b g s -> p (a b g s)")
        qkv = at[:, 0:3072].rearrange("p (h c e) -> p h c e", h=8, c=CAP)
        av = at[:, 3072:4096].rearrange("p (h c e) -> p h c e", h=8, c=CAP)
        at = V2[:, :, :, :, :].rearrange("p a b g s -> p (a b g s)")
        aoT = at[:, 0:2048].rearrange("p (s q r) -> p s q r", s=SP, q=NQ)
        ao = at[:, 2048:4096].rearrange("p (s d) -> p s d", s=SP)
        y = oT[:, :].rearrange("p (s d) -> p s d", s=SP)
        at = gu[:, :, :].rearrange("p a b -> p (a b)")
        takeT = at[:, 0:2048].rearrange("p (s q r) -> p s q r", s=SP, q=NQ)
        at = hid[:, :, :].rearrange("p a b -> p (a b)")
        putT = at[:, 0:2048].rearrange("p (s q t) -> p s q t", s=SP, q=NQ)
        xnT = cT[:, :].rearrange("p (s r) -> p s r", s=SP)
        at = fT[:, :]
        sm = at[:, 0:256].rearrange("p (s h) -> p s h", s=SP)
        smr = at[:, 256:320].rearrange("p (k s) -> p k s", k=4)
        at = xT[:, :, :].rearrange("p a b -> p (a b)")
        pt = at[:, 0:256].rearrange("p (a q t) -> p a q t", a=2, q=NQ)
        w0 = at[:, 256:512].rearrange("p (a q t) -> p a q t", a=2, q=NQ)
        o1 = at[:, 512:768].rearrange("p (a q t) -> p a q t", a=2, q=NQ)
        o2 = at[:, 768:1024].rearrange("p (a q t) -> p a q t", a=2, q=NQ)
        at = xn[:, :, :].rearrange("p a b -> p (a b)")
        tm = at[:, 0:64].rearrange("p (k a q) -> p k a q", k=8, a=2)
        hot = at[:, 64:320].rearrange("p (a q t) -> p a q t", a=2, q=NQ)
        att = at[:, 320:352]
        attn = at[:, 352:384]
        at = fn[:, :, :].rearrange("p a b -> p (a b)")
        asT = at[:, 0:128]
        aeT = at[:, 128:256]
        ar = at[:, 256:272]
        prod = pT[:, :, :].rearrange("p a b -> p (a b)")[:, 0:1024]

        bS = [bank(f"scores{i}") for i in range(2)]
        bT = [bank(f"scoresT{i}") for i in range(2)]
        bC = bank("context")
        bD = bank("denominators")
        bG = [bank(f"general{i}") for i in range(2)]

        d_cf, d_cb, d_wa, d_wb, d_wf, d_wl, d_mask = (sem(f"loaded_{k}") for k in
                                                      ("cf", "cb", "wa", "wb", "wf", "wl", "mask"))
        d_x = [sem(f"loaded_x{c}") for c in range(NC)]
        d_c = [sem(f"loaded_ctx{c}") for c in range(NC)]
        general_full = [sem(f"general_full{i}") for i in range(2)]
        general_free = [sem(f"general_free{i}") for i in range(2)]
        vector_step, scalar_step, pool_step = sem("vector_step"), sem("scalar_step"), sem("pool_step")
        gates_ready, biases_ready, pools_ready = sem("gates_ready"), sem("biases_ready"), sem("pools_ready")
        zeros_ready, mask_ready = sem("zeros_ready"), sem("mask_ready")
        normed, var_ready, rstd_ready = sem("normed"), sem("var_ready"), sem("rstd_ready")
        fnormed = sem("fnormed")
        obias_ready, bias_added = sem("obias_ready"), sem("bias_added")
        xT_ready, fT_ready = sem("xT_ready"), sem("fT_ready")
        q_ready, k_ready, v_ready = sem("q_ready"), sem("k_ready"), sem("v_ready")
        qk_low_ready = sem("qk_low_ready")
        scores_done, max_done = sem("scores_done"), sem("max_done")
        nmax_ready, shift_ready = sem("nmax_ready"), sem("shift_ready")
        scoresT_done, exp_done, pv_done = sem("scoresT_done"), sem("exp_done"), sem("pv_done")
        context_ready, residual_ready, layer_ready = (sem("context_ready"), sem("residual_ready"),
                                                      sem("layer_ready"))
        logits_ready, route_exp, cw_ready, cwT_ready = (sem("logits_ready"), sem("route_exp"),
                                                        sem("cw_ready"), sem("cwT_ready"))
        silu_done, gated_up, hidden_ready = sem("silu_done"), sem("gated_up"), sem("hidden_ready")
        spilled, d_xr, stored = sem("spilled"), sem("loaded_xr"), sem("stored")
        hn_ready, hnT_ready, tl_ready, tl_exp = (sem("hn_ready"), sem("hnT_ready"), sem("tl_ready"),
                                                 sem("tl_exp"))
        probs_ready, hot_ready, take_ready = sem("probs_ready"), sem("hot_ready"), sem("take_ready")
        put_ready, hT_ready, qkv_ready = sem("put_ready"), sem("hT_ready"), sem("qkv_ready")
        att_ready, ash_ready, aexp_ready, attn_ready = (sem("att_ready"), sem("ash_ready"),
                                                        sem("aexp_ready"), sem("attn_ready"))
        av_ready, avT_ready, aoT_ready, ao_ready = (sem("av_ready"), sem("avT_ready"),
                                                    sem("aoT_ready"), sem("ao_ready"))
        out_bias, tail_zero, out_ready = sem("out_bias"), sem("tail_zero"), sem("out_ready")
        yn_ready = sem("yn_ready")

        def col(tile, table, name):
            a, w = table[name]
            return tile[:, a:a + w]

        ident = col(cf, CF, "ident")
        identb = col(cb, CBF, "ident")

        spill = nc.dram_tensor("x_by_position", [B, S, D], F32).ap()
        spill_tiles = spill.rearrange("(j b) s d -> (b s) j d", b=2)

        def by_position(ap):
            return ap.rearrange("b (q s) d -> q b s d", q=NQ)

        def full(engine, job):
            k = jobs[job]
            engine.wait_ge(general_full[k % 2], k // 2 + 1)
            return bG[k % 2]

        def freed(job):
            return general_free[jobs[job] % 2]

        def used(engine, job):
            k = jobs[job]
            engine.wait_ge(general_free[k % 2], k // 2 + 1)

        def filled(engine, job):
            k = jobs[job]
            engine.wait_ge(general_full[k % 2], k // 2 + 1)

        block = stack.enter_context(nc.Block())

        @block.sync
        def _(sp):
            x_tiles = x.rearrange("(j b) s d -> (b s) j d", b=2)
            sp.dma_start(wa[:, :], w_a).then_inc(d_wa, 16)
            sp.dma_start(cf[:, :], const_f).then_inc(d_cf, 16)
            for c in range(NC):
                sp.dma_start(xa[:, CT * c:CT * c + CT, :], x_tiles[:, CT * c:CT * c + CT, :]).then_inc(d_x[c], 16)
                sp.dma_start(cT[:, CW * c:CW * c + CW], ctxT[:, CW * c:CW * c + CW]).then_inc(d_c[c], 16)
                if c == 0:
                    sp.dma_start(cb[:, :], const_b).then_inc(d_cb, 16)
            sp.dma_start(wf[:, :], w_f).then_inc(d_wf, 16)
            sp.dma_start(mask[:, :], maskT).then_inc(d_mask, 16)
            sp.dma_start(wb[:, :], w_b).then_inc(d_wb, 16)
            sp.dma_start(wl[:, :], w_l).then_inc(d_wl, 16)
            for c in range(NC):
                used(sp, ("Y", c))
                sp.dma_start(spill_tiles[:, CT * c:CT * c + CT, :], xa[:, CT * c:CT * c + CT, :]).then_inc(spilled, 16)
            sp.wait_ge(spilled, 16 * NC)
            for q in range(NQ):
                sp.dma_start(xr[32 * q:32 * q + 32, :, :], by_position(spill)[q]).then_inc(d_xr, 16)
            for k in range(NT // CT):
                sp.wait_ge(out_ready, k + 1)
                for q in range(NQ):
                    sp.dma_start(by_position(out)[q][:, CT * k:CT * k + CT, :],
                                 y[32 * q:32 * q + 32, CT * k:CT * k + CT, :]).then_inc(stored, 16)
            sp.wait_ge(stored, 16 * NQ * (NT // CT))

        @block.tensor
        def _(pe):
            def take(job):
                k = jobs[job]
                if k >= 2:
                    pe.wait_ge(general_free[k % 2], k // 2)
                return bG[k % 2], general_full[k % 2]

            def out_bias_product(l):
                w, table = ((wa, WA), (wb, WB))[l]
                if l:
                    pe.wait_ge(d_wb, 16)
                dst, done = take(("bias", l))
                bv = col(w, table, f"bv{l}")
                nc.tensor.matmul(dst[:, 0:D], bv.broadcast_to([P, P]), col(w, table, f"wo{l}"),
                                 start=True, stop=True).then_inc(done, 1)

            def transpose_tiles(job, tiles):
                dst, done = take(job)
                for j in range(CT):
                    last = nc.tensor.transpose(dst[:, P * j:P * j + P], tiles[:, j, :], ident)
                last.then_inc(done, 1)

            def project(n):
                l, c = divmod(n, NC)
                w, table = ((wa, WA), (wb, WB))[l]
                pe.wait_ge(normed, n + 1)
                transpose_tiles(("xT", n), xn)
                dst, done = take(("Q", n))
                used(pe, ("xT", n))
                nc.tensor.matmul(dst[:, :], col(w, table, f"wq{l}"), xT[:, n % 2, :],
                                 start=True, stop=True).then_inc(done, 1)
                if l == 0:
                    pe.wait_ge(d_c[c], 16)
                dst, done = take(("K", n))
                nc.tensor.matmul(dst[:, :], col(w, table, f"wk{l}"), cT[:, CW * c:CW * c + CW],
                                 start=True, stop=True).then_inc(done, 1)
                for half in range(2):
                    dst, done = take(("V", n, half))
                    for b in range(4):
                        first = CW * c + S * (4 * half + b)
                        for i2 in range(2):
                            last = nc.tensor.matmul(dst[S * i2:S * i2 + S, P * b:P * b + P], cT[:, first:first + S],
                                                    col(w, table, f"wv{l}"), start=True, stop=True)
                    last.then_inc(done, 1)

            def low_scores(n, b):
                k = CB * n + b
                if b == 0:
                    pe.wait_ge(qk_low_ready, 2 * (n + 1))
                if k >= 2:
                    pe.wait_ge(max_done, k - 1)
                dst = bS[k % 2]
                masked = n >= NC
                if masked:
                    if n == NC and b == 0:
                        pe.wait_ge(mask_ready, 3)
                    seq = CB * (n - NC) + b
                    nc.tensor.matmul(dst[:, :], col(cb, CBF, "twice"),
                                     maskb[:, seq, 0:1, :].broadcast_to([P, 8, S]),
                                     start=True, stop=False, skip_group_check=True)
                for gp in range(2):
                    last = nc.tensor.matmul(dst[:, 256 * gp:256 * gp + 256],
                                            Qb[:, b, 2 * gp:2 * gp + 2, :].rearrange("p g s -> p (g s)"),
                                            Kb[:, b, :, :].rearrange("p i t -> p (i t)"),
                                            start=not masked, stop=not masked or gp == 1,
                                            skip_group_check=masked)
                last.then_inc(scores_done, 1)

            def transpose_maxima(n):
                dst, done = take(("maxT", n))
                pe.wait_ge(nmax_ready, n + 1)
                nc.tensor.transpose(dst[:, :].bitcast(BF16)[:, 0:P],
                                    nmax2[:, :, :].rearrange("p a b -> p (a b)"), identb).then_inc(done, 1)

            def scores_transposed(n, b):
                k = CB * n + b
                if b == 0:
                    used(pe, ("maxT", n))
                if k >= 2:
                    pe.wait_ge(exp_done, k - 1)
                dst = bT[k % 2]
                masked = n >= NC
                pick = col(cb, CBF, "pick")[:, P * b:P * b + P]
                if masked:
                    seq = CB * (n - NC) + b
                    nc.tensor.matmul(dst[:, :], maskb[:, seq, :, :].rearrange("p a t -> p (a t)"),
                                     identb[:, 0:S].unsqueeze(1).broadcast_to([P, 8, S]),
                                     start=True, stop=False, skip_group_check=True)
                else:
                    nc.tensor.matmul(dst[:, :], pick, shift[:, n % 2, :], start=True, stop=False,
                                     skip_group_check=True)
                for ip in range(2):
                    last = nc.tensor.matmul(dst[:, 256 * ip:256 * ip + 256],
                                            Ki[:, n % 2, b, 2 * ip:2 * ip + 2, :].rearrange("p i t -> p (i t)"),
                                            Qg[:, n % 2, b, :, :].rearrange("p g s -> p (g s)"),
                                            start=False, stop=not masked and ip == 1, skip_group_check=True)
                if masked:
                    last = nc.tensor.matmul(dst[:, :], pick, shift[:, n % 2, :], start=False, stop=True,
                                            skip_group_check=True)
                last.then_inc(scoresT_done, 1)

            def values(n, b):
                k = CB * n + b
                if b == 0:
                    used(pe, ("V", n, 1))
                    pe.wait_ge(context_ready, n)
                pe.wait_ge(exp_done, k + 1)
                ones = col(cf, CF, "ones_v").rearrange("p (a r) -> p a r", a=2)
                for dst, w in ((bC, None), (bD, ones)):
                    for ip in range(2):
                        for g in range(NG):
                            lhs = V2[:, n % 2, b, ip, 32 * g:32 * g + 32] if w is None else w[:, ip, :]
                            at = 256 * ip + S * g
                            last = nc.tensor.matmul(dst[32 * g:32 * g + 32, S * b:S * b + S], lhs,
                                                    pT[:, k % 3, at:at + S],
                                                    start=ip == 0, stop=ip == 1)
                last.then_inc(pv_done, 1)

            def attention(n):
                for b in range(CB):
                    scores_transposed(n, b)
                    if n + 1 < NA:
                        low_scores(n + 1, b)
                    if b >= 1:
                        values(n, b - 1)
                values(n, CB - 1)

            def project_out(n):
                dst, done = take(("O", n))
                pe.wait_ge(context_ready, n + 1)
                for j in range(CT):
                    first = CW * n + P * j
                    last = nc.tensor.matmul(dst[:, P * j:P * j + P], oT[:, first:first + P],
                                            col(wa, WA, "wo0"), start=True, stop=True)
                last.then_inc(done, 1)

            def experts(c):
                if c == 0:
                    pe.wait_ge(d_wf, 16)
                dst, done = take(("logits", c))
                used(pe, ("fT", c))
                for j in range(CT):
                    last = nc.tensor.matmul(dst[:, NE * j:NE * j + NE], fT[:, P * j:P * j + P],
                                            col(wa, WA, "gate_w"), start=True, stop=True)
                last.then_inc(done, 1)
                for p in range(NP):
                    for job, w in (("G", "wg"), ("U", "wu")):
                        dst, done = take((job, c, p))
                        nc.tensor.matmul(dst[:, :], col(wf, WF, w)[:, P * p:P * p + P], fT[:, :],
                                         start=True, stop=True).then_inc(done, 1)
                dst, done = take(("shared", c))
                nc.tensor.matmul(dst[:, :], col(wf, WF, "shared"), fT[:, :], start=True, stop=True).then_inc(done, 1)
                dst, done = take(("weightT", c))
                pe.wait_ge(cw_ready, c + 1)
                for j in range(CT):
                    last = nc.tensor.transpose(dst[0:3 * NE, :].bitcast(BF16)[:, P * j:P * j + P],
                                               cw3[:, j, :, :].rearrange("p a b -> p (a b)"), identb)
                last.then_inc(done, 1)
                for p in range(NP):
                    dst, done = take(("W", c, p))
                    if p == 0:
                        used(pe, ("weightT", c))
                    nc.tensor.matmul(dst[:, :], col(cb, CBF, "experts")[:, P * p:P * p + P], cwT[:, :],
                                     start=True, stop=True).then_inc(done, 1)
                dst, done = take(("Y", c))
                used(pe, ("W", c, NP - 1))
                for j in range(CT):
                    for p in range(NP + 1):
                        if p < NP:
                            lhs, rhs = hid[:, p, P * j:P * j + P], col(wf, WF, "wd")[:, D * p:D * p + D]
                        else:
                            lhs, rhs = gu[0:F, NP, P * j:P * j + P], col(wf, WF, "sd")[0:F, :]
                        last = nc.tensor.matmul(dst[:, P * j:P * j + P], lhs, rhs, start=p == 0, stop=p == NP)
                last.then_inc(done, 1)

            def transpose_for_experts(n):
                pe.wait_ge(fnormed, n + 1)
                transpose_tiles(("fT", n), fn)

            pe.wait_ge(d_wa, 16)
            out_bias_product(0)
            pe.wait_ge(d_cf, 16)
            pe.wait_ge(d_cb, 16)
            project(0)
            for b in range(CB):
                low_scores(0, b)
            transpose_maxima(0)
            project(1)
            for n in range(NA):
                attention(n)
                if n + 2 < NA:
                    project(n + 2)
                if n + 1 < NA:
                    transpose_maxima(n + 1)
                if n < NC:
                    project_out(n)
                if 1 <= n <= NC:
                    experts(n - 1)
                if n < NC:
                    transpose_for_experts(n)
                if n == 1:
                    out_bias_product(1)

            pe.wait_ge(context_ready, NA)
            for k in range(NT // CT):
                dst, done = take(("O1", k))
                for j in range(CT):
                    last = nc.tensor.matmul(dst[:, P * j:P * j + P], oT[:, P * (CT * k + j):P * (CT * k + j) + P],
                                            col(wb, WB, "wo1"), start=True, stop=True)
                last.then_inc(done, 1)
            for k in range(NT // CT):
                pe.wait_ge(hn_ready, k + 1)
                transpose_tiles(("hT", k), hn[:, CT * k:CT * k + CT, :])
            dst, done = take(("tlog",))
            used(pe, ("hT", NT // CT - 1))
            for j in range(SP):
                last = nc.tensor.matmul(dst[:, H1 * j:H1 * j + H1], xnT[:, j, :], col(wl, WL, "Wg"),
                                        start=True, stop=True)
            last.then_inc(done, 1)
            dst, done = take(("probT",))
            pe.wait_ge(probs_ready, 1)
            for a in range(2):
                last = nc.tensor.transpose(dst[:, P * a:P * a + P],
                                           sm[:, 8 * a:8 * a + 8, :].rearrange("p s h -> p (s h)"), ident)
            last.then_inc(done, 1)
            for c in range(CAP):
                dst, done = take(("hotT", c))
                pe.wait_ge(hot_ready, 1)
                for a in range(2):
                    src = (o1 if c == 0 else hot)[:, a, :, :].rearrange("p q t -> p (q t)")
                    last = nc.tensor.transpose(dst[:, P * a:P * a + P], src, ident)
                last.then_inc(done, 1)
            used(pe, ("hotT", CAP - 1))
            for k in range(NT // CT):
                dst, done = take(("take", k))
                for j in range(CT):
                    s = CT * k + j
                    last = nc.tensor.matmul(dst[:, P * j:P * j + P], hn[:, s, :],
                                            takeT[:, s, :, :].rearrange("p q r -> p (q r)"),
                                            start=True, stop=True)
                last.then_inc(done, 1)
            used(pe, ("take", NT // CT - 1))
            for k in range(H1 // 2):
                dst, done = take(("qkv", k))
                for c in range(CAP):
                    for h2 in range(2):
                        h = 2 * k + h2
                        last = nc.tensor.matmul(dst[64 * h2:64 * h2 + 64, 192 * c:192 * c + 192],
                                                hT[:, h, c, :], col(wl, WL, "Wqkv")[:, 192 * h:192 * h + 192],
                                                start=True, stop=True)
                last.then_inc(done, 1)
            dst, done = take(("attT",))
            pe.wait_ge(att_ready, 4)
            nc.tensor.transpose(dst[0:32, 0:P], att, ident).then_inc(done, 1)
            dst, done = take(("attB",))
            pe.wait_ge(attn_ready, 1)
            nc.tensor.transpose(dst[:, 0:32], asT[0:32, :], ident[0:32, 0:32]).then_inc(done, 1)
            for k in range(2):
                dst, done = take(("avT", k))
                pe.wait_ge(av_ready, 2)
                for j in range(4):
                    last = nc.tensor.transpose(dst[:, P * j:P * j + P],
                                               av[:, 4 * k + j, :, :].rearrange("p c e -> p (c e)"), ident)
                last.then_inc(done, 1)
            used(pe, ("avT", 1))
            for k in range(NT // CT):
                dst, done = take(("ao", k))
                for j in range(CT):
                    h = CT * k + j
                    last = nc.tensor.matmul(dst[:, P * j:P * j + P], col(wl, WL, "Wo")[:, D * h:D * h + D],
                                            avT[:, h, :, :].rearrange("p c s -> p (c s)"), start=True, stop=True)
                last.then_inc(done, 1)
            used(pe, ("ao", NT // CT - 1))
            for k in range(NT // CT):
                dst, done = take(("aoT", k))
                for j in range(CT):
                    last = nc.tensor.transpose(dst[:, P * j:P * j + P],
                                               aoT[:, CT * k + j, :, :].rearrange("p q r -> p (q r)"), ident)
                last.then_inc(done, 1)
            pe.wait_ge(put_ready, 1)
            for k in range(NT // CT):
                dst, done = take(("back", k))
                used(pe, ("aoT", k))
                for j in range(CT):
                    s = CT * k + j
                    last = nc.tensor.matmul(dst[:, P * j:P * j + P],
                                            putT[:, s, :, :].rearrange("p q t -> p (q t)"), ao[:, s, :],
                                            start=True, stop=True)
                last.then_inc(done, 1)

        @block.vector
        def _(ve):
            V = nc.vector
            steps = [0]

            def settled(ins):
                steps[0] += 1
                ins.then_inc(vector_step, 1)
                ve.wait_ge(vector_step, steps[0])

            norms = [0]

            def normalise(src, dst, tiles, done, reader=None):
                for j in range(tiles):
                    last = V.bn_stats(stats[:, j, :], src[:, j, :])
                settled(last)
                for j in range(tiles):
                    last = V.bn_aggr(mean_var[:, j, :], stats[:, j, :])
                settled(last)
                V.tensor_scalar(var_eps[:, 0:tiles], mean_var[:, 0:tiles, 1], EPS, None, ALU.add).then_inc(var_ready, 1)
                norms[0] += 1
                ve.wait_ge(rstd_ready, norms[0])
                if reader is not None:
                    filled(ve, reader)
                for j in range(tiles):
                    ins = V.tensor_scalar(dst[:, j, :], src[:, j, :], mean_var[:, j, 0:1], rstd[:, j:j + 1],
                                          ALU.subtract, ALU.mult)
                    if j == tiles - 1:
                        ins.then_inc(done, 1)

            def norm_attention(n):
                c = n % NC
                if n < NC:
                    ve.wait_ge(d_x[c], 16)
                else:
                    used(ve, ("Y", c))
                normalise(xa[:, CT * c:CT * c + CT, :], xn, CT, normed, ("xT", n - 1) if n >= 1 else None)

            def spread_queries(n):
                l = n // NC
                ve.wait_ge(biases_ready, l + 1)
                src = full(ve, ("Q", n))
                for g in range(NG):
                    ins = V.tensor_scalar(Qg[:, n % 2, :, g, :], src[:, :].rearrange("p (b s) -> p b s", b=CB),
                                          col(cf, CF, "gmask")[:, g:g + 1], bqg[:, l, g:g + 1], ALU.mult, ALU.add)
                ins.then_inc(freed(("Q", n)), 1)

            def row_maximum(n, b):
                k = CB * n + b
                ve.wait_ge(scores_done, k + 1)
                V.tensor_reduce(nmax[:, n % 2, 8 * b:8 * b + 8], bS[k % 2][:, :].rearrange("p (r t) -> p r t", r=8),
                                AX.X, ALU.max, negate=True).then_inc(max_done, 1)

            def split_maxima(n):
                ve.wait_ge(max_done, CB * (n + 1))
                if n >= 1:
                    filled(ve, ("maxT", n - 1))
                settled(V.tensor_copy(nmax2[:, 0, :], nmax[:, n % 2, :]))
                V.tensor_tensor(nmax2[:, 1, :], nmax[:, n % 2, :], nmax2[:, 0, :], ALU.subtract).then_inc(nmax_ready, 1)

            def spread_shift(n):
                src = full(ve, ("maxT", n))
                if n >= 2:
                    ve.wait_ge(scoresT_done, CB * (n - 1))
                V.tensor_tensor(shift[:, n % 2, :].rearrange("p (a r) -> p a r", a=4),
                                src[:, :].bitcast(BF16)[:, 0:P].unsqueeze(1).broadcast_to([P, 4, P]),
                                col(cf, CF, "cmask").unsqueeze(2).broadcast_to([P, 4, P]),
                                ALU.mult).then_inc(freed(("maxT", n)), 1)

            def divide(n):
                c = n % NC
                ve.wait_ge(pv_done, CB * (n + 1))
                settled(V.reciprocal(den[:, :], bD[:, :]))
                dst, parts = oT[:, CW * c:CW * c + CW], [bC[:, :], den[:, :]]
                if n >= NC:
                    dst = oT[:, :].rearrange("p (s q b) -> p b q s", s=SP, q=NQ)[:, CB * c:CB * c + CB, :, :]
                    parts = [ap.rearrange("p (b q s) -> p b q s", b=CB, q=NQ) for ap in parts]
                V.tensor_tensor(dst, *parts, ALU.mult).then_inc(context_ready, 1)

            def add_attention(n):
                src = full(ve, ("O", n))
                ve.wait_ge(bias_added, n + 1)
                part = xa[:, CT * n:CT * n + CT, :].rearrange("p j d -> p (j d)")
                V.scalar_tensor_tensor(part, src[:, :], gated[:, 0:1], part, ALU.mult, ALU.add).then_inc(freed(("O", n)), 1)
                used(ve, ("O", n))
                normalise(xa[:, CT * n:CT * n + CT, :], fn, CT, fnormed, ("fT", n - 1) if n >= 1 else None)

            def route(c):
                def bc(ap):
                    return ap.unsqueeze(2).broadcast_to([P, CT, NE])
                src = full(ve, ("logits", c))[:, 0:CT * NE].rearrange("p (j e) -> p j e", e=NE)
                settled(V.tensor_reduce(r4[:, 0, :], src, AX.X, ALU.max))
                V.tensor_tensor(lg[:, :, :], src, bc(r4[:, 0, :]), ALU.subtract).then_inc(freed(("logits", c)), 1)
                ve.wait_ge(route_exp, c + 1)
                settled(V.tensor_reduce(r4[:, 1, :], pr[:, :, :], AX.X, ALU.add))
                settled(V.reciprocal(r4[:, 2, :], r4[:, 1, :]))
                settled(V.tensor_tensor(pr[:, :, :], pr[:, :, :], bc(r4[:, 2, :]), ALU.mult))
                order = col(cf, CF, "first8").rearrange("p (j e) -> p j e", e=NE)
                for hot_, src_ in ((hot1, pr), (hot2, lw)):
                    settled(V.tensor_reduce(r4[:, 0, :], src_[:, :, :], AX.X, ALU.max))
                    settled(V.tensor_tensor(hot_[:, :, :], src_[:, :, :], bc(r4[:, 0, :]), ALU.is_equal))
                    settled(V.tensor_tensor(hot_[:, :, :], hot_[:, :, :], order, ALU.mult))
                    settled(V.tensor_reduce(r4[:, 1, :], hot_[:, :, :], AX.X, ALU.max))
                    settled(V.tensor_tensor(hot_[:, :, :], hot_[:, :, :], bc(r4[:, 1, :]), ALU.is_equal))
                    if hot_ is hot1:
                        settled(V.scalar_tensor_tensor(lw[:, :, :], hot1[:, :, :], -4.0, pr[:, :, :], ALU.mult, ALU.add))
                settled(V.tensor_tensor(hot1[:, :, :], hot1[:, :, :], hot2[:, :, :], ALU.add))
                settled(V.tensor_tensor(lw[:, :, :], hot1[:, :, :], pr[:, :, :], ALU.mult))
                if c >= 1:
                    filled(ve, ("weightT", c - 1))
                settled(V.tensor_copy(cw3[:, :, 0, :], lw[:, :, :]))
                settled(V.tensor_tensor(lw[:, :, :], lw[:, :, :], cw3[:, :, 0, :], ALU.subtract))
                settled(V.tensor_copy(cw3[:, :, 1, :], lw[:, :, :]))
                V.tensor_tensor(cw3[:, :, 2, :], lw[:, :, :], cw3[:, :, 1, :], ALU.subtract).then_inc(cw_ready, 1)

            def gate_up(c):
                for p in range(NP):
                    src = full(ve, ("U", c, p))
                    used(ve, ("G", c, p))
                    V.tensor_tensor(gu[:, p, :], sil[:, p % 2, :], src[:, :], ALU.mult).then_inc(freed(("U", c, p)), 1)
                ve.wait_ge(silu_done, c + 1)
                src = bG[jobs[("shared", c)] % 2]
                V.tensor_tensor(gu[0:F, NP, :], sil[F:2 * F, NP % 2, :], src[F:2 * F, :], ALU.mult).then_inc(freed(("shared", c)), 1)
                used(ve, ("shared", c))

            def weigh(c):
                for p in range(NP):
                    src = full(ve, ("W", c, p))
                    V.tensor_tensor(hid[:, p, :], gu[:, p, :], src[:, :], ALU.mult).then_inc(freed(("W", c, p)), 1)

            def add_experts(c):
                src = full(ve, ("Y", c))
                part = xa[:, CT * c:CT * c + CT, :].rearrange("p j d -> p (j d)")
                V.scalar_tensor_tensor(part, src[:, :], gated[:, 1:2], part, ALU.mult, ALU.add).then_inc(freed(("Y", c)), 1)

            def biases(l):
                w, table = ((wa, WA), (wb, WB))[l]
                if l:
                    ve.wait_ge(d_wb, 16)
                V.tensor_scalar(bqg[:, l, :], col(cf, CF, "gmask"), col(w, table, f"bq{l}"), None, ALU.mult)
                V.tensor_scalar(bki[:, l, :], col(cf, CF, "imask"), col(w, table, f"bk{l}"), None,
                                ALU.mult).then_inc(biases_ready, 1)
                src = full(ve, ("bias", l))
                V.tensor_tensor(obias[:, l, :], src[:, 0:D], col(w, table, f"bo{l}"), ALU.add).then_inc(freed(("bias", l)), 1)
                used(ve, ("bias", l))
                V.tensor_scalar(obias[:, l, :], obias[:, l, :], gated[:, 2 * l:2 * l + 1], None,
                                ALU.mult).then_inc(obias_ready, 1)

            ve.wait_ge(d_wa, 16)
            ve.wait_ge(d_cf, 16)
            ve.wait_ge(gates_ready, 1)
            norm_attention(0)
            biases(0)
            spread_queries(0)
            norm_attention(1)
            for b in range(CB):
                row_maximum(0, b)
            split_maxima(0)
            spread_shift(0)
            spread_queries(1)
            norm_attention(2)
            for n in range(NA):
                if n + 1 < NA:
                    for b in range(CB):
                        row_maximum(n + 1, b)
                    split_maxima(n + 1)
                divide(n)
                if n + 2 < NA:
                    spread_queries(n + 2)
                if n + 1 < NA:
                    spread_shift(n + 1)
                if n < NC:
                    add_attention(n)
                if n == 0:
                    norm_attention(3)
                if 1 <= n <= NC:
                    route(n - 1)
                    gate_up(n - 1)
                    weigh(n - 1)
                    add_experts(n - 1)
                    norm_attention(n - 1 + NC)
                if n == 1:
                    biases(1)

            ve.wait_ge(d_xr, 16 * NQ)
            ve.wait_ge(bias_added, NC + 1)
            for k in range(NT // CT):
                part = xr[:, CT * k:CT * k + CT, :]
                src = full(ve, ("O1", k))
                flat = part.rearrange("p j d -> p (j d)")
                V.scalar_tensor_tensor(flat, src[:, :], gated[:, 2:3], flat, ALU.mult, ALU.add).then_inc(freed(("O1", k)), 1)
                used(ve, ("O1", k))
                normalise(part, hn[:, CT * k:CT * k + CT, :], CT, hn_ready)
            src = full(ve, ("tlog",))[:, 0:SP * H1].rearrange("p (s h) -> p s h", h=H1)

            def over(ap):
                return ap.unsqueeze(2).broadcast_to([P, SP, H1])
            settled(V.tensor_reduce(smr[:, 0, :], src, AX.X, ALU.max))
            V.tensor_tensor(sm, src, over(smr[:, 0, :]), ALU.subtract).then_inc(freed(("tlog",)), 1)
            ve.wait_ge(tl_exp, 1)
            settled(V.tensor_reduce(smr[:, 1, :], sm, AX.X, ALU.add))
            settled(V.reciprocal(smr[:, 2, :], smr[:, 1, :]))
            V.tensor_tensor(sm, sm, over(smr[:, 2, :]), ALU.mult).then_inc(probs_ready, 1)
            def bc(ap):
                return ap.unsqueeze(3).broadcast_to([P, 2, NQ, B])
            src = full(ve, ("probT",))[:, 0:256]

            def flat(ap):
                return ap.rearrange("p a q t -> p (a q) t")

            def bcf(k):
                return tm[:, k, :, :].rearrange("p a q -> p (a q)").unsqueeze(2).broadcast_to([P, 8, B])

            def tmf(k):
                return tm[:, k, :, :].rearrange("p a q -> p (a q)")
            V.tensor_copy(pt.rearrange("p a q t -> p (a q t)"), src).then_inc(freed(("probT",)), 1)
            used(ve, ("probT",))
            order = col(cf, CF, "first32").unsqueeze(1).broadcast_to([P, 8, B])
            for r, (hot_, src_) in enumerate(((o1, pt), (o2, w0))):
                settled(V.tensor_reduce(tmf(0), flat(src_), AX.X, ALU.max))
                settled(V.tensor_tensor(flat(hot_), flat(src_), bcf(0), ALU.is_equal))
                settled(V.tensor_tensor(flat(hot_), flat(hot_), order, ALU.mult))
                settled(V.tensor_reduce(tmf(1 + r), flat(hot_), AX.X, ALU.max))
                settled(V.tensor_tensor(flat(hot_), flat(hot_), bcf(1 + r), ALU.is_equal))
                if r == 0:
                    settled(V.scalar_tensor_tensor(flat(w0), flat(o1), -4.0, flat(pt), ALU.mult, ALU.add))
            settled(V.tensor_tensor(tmf(3), tmf(1), tmf(2), ALU.max))
            settled(V.tensor_tensor(flat(hot), flat(o1), flat(o2), ALU.add))
            settled(V.tensor_tensor(flat(o2), order, bcf(3), ALU.is_equal))
            settled(V.tensor_tensor(flat(hot), flat(hot), flat(o2), ALU.subtract))
            V.tensor_copy(flat(o1), flat(o2)).then_inc(hot_ready, 1)
            ve.wait_ge(tail_zero, 2)
            for c in range(CAP):
                src = full(ve, ("hotT", c))
                for q in range(NQ):
                    ins = V.tensor_copy(takeT[32 * q:32 * q + 32, :, q, H1 * c:H1 * c + H1],
                                        src[32 * q:32 * q + 32, 0:256].rearrange("p (s h) -> p s h", h=H1))
                ins.then_inc(freed(("hotT", c)), 1)
            used(ve, ("hotT", 0))
            used(ve, ("hotT", 1))
            for q in range(NQ):
                last = V.transpose(putT[32 * q:32 * q + 32, :, q, :], takeT[32 * q:32 * q + 32, :, q, :])
            last.then_inc(put_ready, 1)
            ve.wait_ge(d_wl, 16)
            bias = col(wl, WL, "bqkv").rearrange("p (h e) -> p h e", e=3 * E1)
            for k in range(H1 // 2):
                src = full(ve, ("qkv", k))[:, 0:2 * 192].rearrange("p (c e) -> p c e", c=CAP)
                V.tensor_tensor(qkv[:, k, :, :], src, bias[:, k:k + 1, :].broadcast_to([P, CAP, 3 * E1]),
                                ALU.add).then_inc(freed(("qkv", k)), 1)
            used(ve, ("qkv", 7))
            used(ve, ("qkv", 6))
            att_v = att.rearrange("p (h i j) -> p h i j", i=2, j=2)
            pr_v = prod[:, 0:512].rearrange("p (h e) -> p h e", h=8)
            for i in range(2):
                for j in range(2):
                    settled(V.tensor_tensor(pr_v, qkv[:, :, i, 0:E1], qkv[:, :, j, E1:2 * E1], ALU.mult))
                    V.tensor_reduce(att_v[:, :, i, j], pr_v, AX.X, ALU.add).then_inc(att_ready, 1)
                    ve.wait_ge(att_ready, 2 * i + j + 1)
            src = full(ve, ("attT",))[0:32, 0:P].rearrange("p (b s) -> p b s", b=2)
            settled(V.tensor_reduce(ar[0:32, 0:2], src, AX.X, ALU.max))
            V.tensor_tensor(asT[0:32, :].rearrange("p (b s) -> p b s", b=2), src,
                            ar[0:32, 0:2].unsqueeze(2).broadcast_to([32, 2, S]), ALU.subtract).then_inc(freed(("attT",)), 1)
            ve.wait_ge(aexp_ready, 1)
            ex = aeT[0:32, :].rearrange("p (b s) -> p b s", b=2)
            settled(V.tensor_reduce(ar[0:32, 2:4], ex, AX.X, ALU.add))
            settled(V.reciprocal(ar[0:32, 4:6], ar[0:32, 2:4]))
            V.tensor_tensor(asT[0:32, :].rearrange("p (b s) -> p b s", b=2), ex,
                            ar[0:32, 4:6].unsqueeze(2).broadcast_to([32, 2, S]), ALU.mult).then_inc(attn_ready, 1)
            src = full(ve, ("attB",))
            V.tensor_copy(attn, src[:, 0:32]).then_inc(freed(("attB",)), 1)
            used(ve, ("attB",))
            an = attn.rearrange("p (h i j) -> p h i j", i=2, j=2)
            for i in range(2):
                def w(j):
                    return an[:, :, i, j].unsqueeze(2).broadcast_to([P, 8, E1])
                settled(V.tensor_tensor(pr_v, qkv[:, :, 0, 2 * E1:3 * E1], w(0), ALU.mult))
                settled(V.tensor_tensor(av[:, :, i, :], qkv[:, :, 1, 2 * E1:3 * E1], w(1), ALU.mult))
                V.tensor_tensor(av[:, :, i, :], av[:, :, i, :], pr_v, ALU.add).then_inc(av_ready, 1)
                ve.wait_ge(av_ready, i + 1)
            ve.wait_ge(tail_zero, 3)
            for k in range(2):
                src = full(ve, ("avT", k))[:, :].rearrange("p (j h s) -> p (j h) s", j=4, h=2)
                for i in range(2):
                    ins = V.tensor_copy(avT[64 * i:64 * i + 64, 8 * k:8 * k + 8, i, :], src[64 * i:64 * i + 64, :, :])
                ins.then_inc(freed(("avT", k)), 1)
            for k in range(NT // CT):
                src = full(ve, ("ao", k))
                for c in range(CAP):
                    s_ = src[:, :].rearrange("p (h c q s) -> p c h q s", h=CT, c=CAP, q=NQ)[:, c, :, :, :]
                    d_ = aoT[:, :, :, H1 * c + CT * k:H1 * c + CT * k + CT].rearrange("p s q h -> p h q s")
                    ins = V.tensor_scalar(d_, s_, col(wl, WL, "bo"), None, ALU.add)
                ins.then_inc(freed(("ao", k)), 1)
            ve.wait_ge(out_bias, 1)
            for k in range(NT // CT):
                src = full(ve, ("back", k))
                part = slice(CT * k, CT * k + CT)
                V.tensor_tensor(y[:, part, :].rearrange("p j d -> p (j d)"), src[:, :],
                                hn[:, part, :].rearrange("p j d -> p (j d)"), ALU.add).then_inc(freed(("back", k)), 1)
                used(ve, ("back", k))
                normalise(y[:, part, :], y[:, part, :], CT, yn_ready)
                ve.wait_ge(yn_ready, k + 1)
                settled(V.tensor_tensor(y[:, part, :], y[:, part, :],
                                        col(wl, WL, "ln_g").unsqueeze(1).broadcast_to([P, CT, D]), ALU.mult))
                V.tensor_tensor(y[:, part, :], y[:, part, :], xr[:, part, :], ALU.add).then_inc(out_ready, 1)

        @block.scalar
        def _(ae):
            A = nc.scalar

            def spread_keys(n):
                l = n // NC
                ae.wait_ge(biases_ready, l + 1)
                src = full(ae, ("K", n))
                for i in range(NI):
                    ins = A.activation(Ki[:, n % 2, :, i, :], src[:, :].rearrange("p (b s) -> p b s", b=CB),
                                       ACT.Identity, bias=bki[:, l, i:i + 1], scale=col(cf, CF, "imask")[:, i:i + 1])
                ins.then_inc(freed(("K", n)), 1)

            def place_values(n):
                for half in range(2):
                    src = full(ae, ("V", n, half))[:, :].rearrange("p (b g r) -> p b g r", b=4, g=NG)
                    for ip in range(2):
                        for i2 in range(2):
                            i = 2 * ip + i2
                            rows = slice(64 * i2, 64 * i2 + 64)
                            dst = V2[rows, n % 2, 4 * half:4 * half + 4, ip, :].rearrange("p b (g r) -> p b g r", g=NG)
                            ins = A.activation(dst[:, :, :, DH * i:DH * i + DH], src[rows, :, :, DH * i:DH * i + DH], ACT.Copy)
                    ins.then_inc(freed(("V", n, half)), 1)

            def copy_xT(n):
                src = full(ae, ("xT", n))
                A.activation(xT[:, n % 2, :], src[:, :], ACT.Copy).then_inc(freed(("xT", n)), 1)

            def exponentials(n):
                for b in range(CB):
                    k = CB * n + b
                    ae.wait_ge(scoresT_done, k + 1)
                    if k >= 3:
                        ae.wait_ge(pv_done, k - 2)
                    A.activation(pT[:, k % 3, :], bT[k % 2][:, :], ACT.Exp, scale=SCALE).then_inc(exp_done, 1)

            def experts(c):
                used(ae, ("logits", c))
                A.activation(pr[:, :, :], lg[:, :, :], ACT.Exp).then_inc(route_exp, 1)
                for p in range(NP):
                    src = full(ae, ("G", c, p))
                    if p >= 2:
                        used(ae, ("U", c, p - 2))
                    A.activation(sil[:, p % 2, :], src[:, :], ACT.Silu).then_inc(freed(("G", c, p)), 1)
                src = full(ae, ("shared", c))
                used(ae, ("U", c, NP - 2))
                A.activation(sil[F:2 * F, NP % 2, :], src[0:F, :], ACT.Silu).then_inc(silu_done, 1)
                src = full(ae, ("weightT", c))
                A.activation(cwT[0:3 * NE, :], src[0:3 * NE, :].bitcast(BF16)[:, 0:CW], ACT.Copy).then_inc(freed(("weightT", c)), 1)

            def copy_fT(n):
                src = full(ae, ("fT", n))
                A.activation(fT[:, :], src[:, :], ACT.Copy).then_inc(freed(("fT", n)), 1)

            ae.wait_ge(d_wa, 16)
            A.activation(gated[:, :], col(wa, WA, "gates"), ACT.Tanh).then_inc(gates_ready, 1)
            ae.wait_ge(zeros_ready, 2)
            ae.wait_ge(pools_ready, 1)
            for n in (0, 1):
                copy_xT(n)
                spread_keys(n)
                place_values(n)
            for n in range(NA):
                exponentials(n)
                if n + 2 < NA:
                    copy_xT(n + 2)
                    spread_keys(n + 2)
                    place_values(n + 2)
                if 1 <= n <= NC:
                    experts(n - 1)
                if n < NC:
                    copy_fT(n)

            for k in range(NT // CT):
                src = full(ae, ("hT", k))
                A.activation(cT[:, CW * k:CW * k + CW], src[:, :], ACT.Copy).then_inc(freed(("hT", k)), 1)
            used(ae, ("tlog",))
            A.activation(sm, sm, ACT.Exp).then_inc(tl_exp, 1)
            for k in range(NT // CT):
                src = full(ae, ("take", k))[:, :].rearrange("p (s q c h) -> p c h q s", s=CT, q=NQ, c=CAP)
                for c in range(CAP):
                    dst = hT[:, :, c, :].rearrange("p h (q s) -> p h q s", q=NQ)[:, :, :, CT * k:CT * k + CT]
                    ins = A.activation(dst, src[:, c, :, :, :], ACT.Copy)
                ins.then_inc(freed(("take", k)), 1)
            used(ae, ("attT",))
            A.activation(aeT[0:32, :], asT[0:32, :], ACT.Exp, scale=SCALE1).then_inc(aexp_ready, 1)
            for k in range(NT // CT):
                src = full(ae, ("aoT", k))
                A.activation(ao[:, CT * k:CT * k + CT, :].rearrange("p j d -> p (j d)"), src[:, :], ACT.Copy).then_inc(freed(("aoT", k)), 1)

        @block.gpsimd
        def _(ge):
            G = nc.gpsimd
            norms = [0]

            def inverse_deviation(tiles):
                ge.wait_ge(var_ready, norms[0] + 1)
                norms[0] += 1
                G.tensor_tensor(rstd[:, 0:tiles], var_eps[:, 0:tiles], half_neg[:, 0:tiles], ALU.pow).then_inc(rstd_ready, 1)

            def low_copies(n):
                used(ge, ("Q", n))
                if n >= 1:
                    ge.wait_ge(scores_done, CB * n)
                G.tensor_copy(Qb[:, :, :, :], Qg[:, n % 2, :, :, :]).then_inc(qk_low_ready, 1)
                used(ge, ("K", n))
                G.tensor_copy(Kb[:, :, :, :], Ki[:, n % 2, :, :, :]).then_inc(qk_low_ready, 1)

            def add_bias(n):
                ge.wait_ge(normed, n + 1)
                ge.wait_ge(obias_ready, 1)
                part = xa[:, CT * n:CT * n + CT, :]
                G.tensor_tensor(part, part, obias[:, 0:1, :].broadcast_to([P, CT, D]), ALU.add).then_inc(bias_added, 1)

            def mask_bias():
                ge.wait_ge(rstd_ready, norms[0])
                G.memset(maskb[S:P, :, :, :], 0.0).then_inc(mask_ready, 1)
                ge.wait_ge(mask_ready, 1)
                ge.wait_ge(d_mask, 16)
                for k in range(2):
                    G.tensor_scalar(maskb[0:S, :, k, :], mask[:, :].rearrange("p (b t) -> p b t", b=B), 0.0, BIG,
                                    ALU.is_equal, ALU.mult).then_inc(mask_ready, 1)
                ge.wait_ge(mask_ready, 3)

            G.memset(half_neg[:, :], -0.5).then_inc(pool_step, 1)
            ge.wait_ge(pool_step, 1)
            inverse_deviation(CT)
            G.memset(V2[:, 0, :, :, :], 0.0).then_inc(zeros_ready, 1)
            G.memset(V2[:, 1, :, :, :], 0.0).then_inc(zeros_ready, 1)
            G.memset(cwT[:, :], 0.0).then_inc(pools_ready, 1)
            low_copies(0)
            add_bias(0)
            inverse_deviation(CT)
            add_bias(1)
            low_copies(1)
            inverse_deviation(CT)
            add_bias(2)
            for n in range(NA):
                if n + 2 < NA:
                    low_copies(n + 2)
                if n < NC:
                    inverse_deviation(CT)
                if n == 0:
                    inverse_deviation(CT)
                    add_bias(3)
                if 1 <= n <= NC:
                    inverse_deviation(CT)
                if n == 1:
                    mask_bias()
            ge.wait_ge(d_xr, 16 * NQ)
            ge.wait_ge(obias_ready, 2)
            G.tensor_tensor(xr[:, :, :], xr[:, :, :], obias[:, 1:2, :].broadcast_to([P, SP, D]), ALU.add).then_inc(bias_added, 1)
            filled(ge, ("Y", NC - 1))
            G.memset(takeT, 0.0).then_inc(tail_zero, 1)
            G.memset(putT, 0.0).then_inc(tail_zero, 1)
            ge.wait_ge(scoresT_done, CB * NA)
            G.memset(avT, 0.0).then_inc(tail_zero, 1)
            for k in range(NT // CT):
                inverse_deviation(CT)
            ge.wait_ge(d_wl, 16)
            ge.wait_ge(hn_ready, NT // CT)
            g = gated[:, 3:4]
            G.tensor_scalar(col(wl, WL, "ln_b"), col(wl, WL, "ln_b"), g, None, ALU.mult).then_inc(pool_step, 1)
            ge.wait_ge(pool_step, 2)
            G.tensor_scalar(col(wl, WL, "ln_g"), col(wl, WL, "ln_g"), g, None, ALU.mult).then_inc(pool_step, 1)
            G.tensor_tensor(xr[:, :, :], xr[:, :, :], col(wl, WL, "ln_b").unsqueeze(1).broadcast_to([P, SP, D]),
                            ALU.add).then_inc(out_bias, 1)
            ge.wait_ge(pool_step, 3)
            for k in range(NT // CT):
                inverse_deviation(CT)


def shape_constants():
    row = np.arange(P)
    cf = np.zeros((P, CF_N), np.float32)
    cb = np.zeros((P, CBF_N), np.float32)

    def f(name):
        a, w = CF[name]
        return cf[:, a:a + w]

    def b(name):
        a, w = CBF[name]
        return cb[:, a:a + w]
    f("ident")[:] = np.eye(P)
    f("gmask")[:] = (row[:, None] // 32) == np.arange(NG)
    f("imask")[:] = (row[:, None] // DH % NI) == np.arange(NI)
    gp, i = row // 4 % 2, row % 4
    f("cmask")[:] = (i[:, None] // 2 == np.arange(4) // 2) & (gp[:, None] == np.arange(4) % 2)
    r = np.arange(64)
    f("ones_v")[:] = (r[None] % 32 // DH) == 2 * (r[None] // 32) + row[:, None] // 64
    f("first8")[:] = NE - np.arange(CT * NE) % NE
    f("first32")[:] = B - np.arange(B)
    b("ident")[:] = np.eye(P)
    seq = row // 8 % CB
    pick = (seq[:, None, None] == np.arange(CB)[None, :, None]) & (i[:, None, None] % 2 == row[None, None, :] // 64)
    b("pick")[:] = pick.reshape(P, -1)
    ex = (row[:, None] < 3 * NE) & (row[:, None] % NE == np.arange(NE * F)[None] // F)
    b("experts")[:] = ex
    b("twice")[:] = row[:, None] == row[None] % S
    return cf, cb


def kernel(**inputs):
    import ml_dtypes
    import concourse.bacc as bacc
    from concourse.bass_utils import run_bass_kernel_spmd

    a = {k: np.asarray(v) for k, v in inputs.items()}

    def pack(table, n, parts):
        t = np.zeros((P, n), np.float32)
        for name, v in parts.items():
            first, w = table[name]
            t[:v.shape[0], first:first + w] = v.reshape(v.shape[0], w)
        return t

    def diagonal(w):
        t = np.zeros((P, P), np.float32)
        for h in range(NG * NI):
            t[DH * h:DH * h + DH, DH * h:DH * h + DH] = w[h].T
        return t

    def rows(v):
        return np.broadcast_to(v, (P, v.size))

    cf, cb = shape_constants()
    w_a = pack(WA, WA_N, {
        "wq0": diagonal(a["L0_xattn_wq"]), "wk0": diagonal(a["L0_xattn_wk"]), "wv0": diagonal(a["L0_xattn_wv"]),
        "wo0": a["L0_xattn_wo"].T, "bo0": rows(a["L0_xattn_bo"]), "bq0": a["L0_xattn_bq"].reshape(P, 1),
        "bk0": a["L0_xattn_bk"].reshape(P, 1), "bv0": a["L0_xattn_bv"].reshape(P, 1),
        "gates": rows(np.stack([a["g_xattn"][0], a["g_ffn"][0], a["g_xattn"][1], a["g_ffn"][1]])),
        "gate_w": a["L0_ffn_gate_w"].T})
    w_b = pack(WB, WB_N, {
        "wq1": a["L1_xattn_W0"].T, "wk1": a["L1_xattn_W1"].T, "wv1": a["L1_xattn_W2"].T, "wo1": a["L1_xattn_W3"].T,
        "bo1": rows(a["L1_xattn_b3"]), "bq1": a["L1_xattn_b0"].reshape(P, 1),
        "bk1": a["L1_xattn_b1"].reshape(P, 1), "bv1": a["L1_xattn_b2"].reshape(P, 1)})
    w_f = pack(WF, WF_N, {
        "wg": a["L0_ffn_wg"].reshape(NE * F, D).T, "wu": a["L0_ffn_wu"].reshape(NE * F, D).T,
        "shared": np.concatenate([a["L0_ffn_sg"], a["L0_ffn_su"]], 0).T,
        "wd": a["L0_ffn_wd"].transpose(0, 2, 1).reshape(NP, 2 * F, D).transpose(1, 0, 2).reshape(P, -1),
        "sd": a["L0_ffn_sd"].T})
    wo = a["L1_ffn_Wo"].transpose(1, 0, 2).reshape(E1, -1)
    bqkv = np.concatenate([a["L1_ffn_bq"], a["L1_ffn_bkv"]], -1).reshape(H1 // 2, 2, 3 * E1)
    w_l = pack(WL, WL_N, {
        "Wg": a["L1_ffn_Wg"], "bo": a["L1_ffn_bo"].reshape(P, 1), "ln_g": rows(a["L1_ffn_ln_g"]),
        "ln_b": rows(a["L1_ffn_ln_b"]), "Wo": np.concatenate([wo, wo], 0),
        "Wqkv": np.concatenate([a["L1_ffn_Wq"], a["L1_ffn_Wkv"]], -1).transpose(1, 0, 2).reshape(D, -1),
        "bqkv": np.concatenate([np.broadcast_to(bqkv[:, k].reshape(1, -1), (S, H1 // 2 * 3 * E1)) for k in range(2)], 0)})
    arrays = {
        "x": np.ascontiguousarray(a["x"]),
        "ctxT": np.ascontiguousarray(a["ctx_1024"].reshape(B * S, D).T),
        "maskT": np.ascontiguousarray(a["mask_BxSxS2_if1"].transpose(1, 0, 2).reshape(S, B * S)),
        "const_f": cf, "const_b": cb.astype(ml_dtypes.bfloat16),
        "w_a": w_a, "w_b": w_b, "w_f": w_f, "w_l": w_l}
    nc = bacc.Bacc("TRN2", target_bir_lowering=False, num_devices=1)
    args = [nc.dram_tensor(f"in_{k}", v.shape, mybir.dt.from_np(v.dtype), kind="ExternalInput").ap()
            for k, v in arrays.items()]
    args.append(nc.dram_tensor("out", (B, S, D), F32, kind="ExternalOutput").ap())
    two_layers(nc, *args)
    r = run_bass_kernel_spmd(nc, [{f"in_{k}": v for k, v in arrays.items()}], core_ids=[0])
    return r.results[0]["out"]
```

```python
from contextlib import ExitStack

import numpy as np
import concourse.bass as bass
from concourse import mybir

ALU = mybir.AluOpType
ACT = mybir.ActivationFunctionType
AX = mybir.AxisListType
F32 = mybir.dt.float32
BF16 = mybir.dt.bfloat16
I32 = mybir.dt.int32

P = 128
B, S, D = 32, 64, 128
NG, NI, DH = 4, 4, 8
NT = B * S // P
CB = 8
CW = CB * S
CT = CW // P
VECTOR_PAIRS = (slice(0, 4), slice(4, 6))
POOL_PAIRS = slice(6, 8)
SPLIT = 6
NC = B // CB
NA = 2 * NC
NE, F = 8, 64
NP = NE // 2
H1, E1, CAP = 16, 64, 2
NQ, SP = 4, S // 4
SCALE = float(DH) ** -0.5
SCALE1 = float(E1) ** -0.5
BIG = -(2.0 ** 100)
EPS = 1e-5


def columns(widths):
    at, out = 0, {}
    for name, w in widths:
        out[name] = (at, w)
        at += w
    return out, at


CF, CF_N = columns([("ident", P), ("gmask", NG), ("imask", NI), ("cmask", 4), ("ones_v", 64),
                    ("first8", CT * NE), ("sequence", B)])
CBF, CBF_N = columns([("ident", P), ("pick", CB * P), ("experts", NP * P), ("twice", P)])
WA, WA_N = columns([("wq0", P), ("wk0", P), ("wv0", P), ("wo0", P), ("bo0", P), ("bq0", 1), ("bk0", 1),
                    ("bv0", 1), ("gates", 4), ("gate_w", NE)])
WB, WB_N = columns([("wq1", P), ("wk1", P), ("wv1", P), ("wo1", P), ("bo1", P), ("bq1", 1), ("bk1", 1),
                    ("bv1", 1)])
WF, WF_N = columns([("wg", NE * F), ("wu", NE * F), ("shared", 2 * F), ("wd", NP * D), ("sd", D)])
WL, WL_N = columns([("Wg", H1), ("bo", 1), ("ln_g", D), ("ln_b", D), ("Wo", H1 * D),
                    ("Wqkv", H1 * 3 * E1), ("bqkv", H1 // 2 * 3 * E1)])


def schedule():
    plan = [("measure", 0), ("norm", 0), ("bias", 0), ("clear",), ("xT", 0), ("K", 0), ("Q", 0), ("K2", 0), ("Q2", 0), ("round", 0, 1),
             ("V", 0, 0), ("V", 0, 1)]
    plan += [("low", 0, b) for b in range(CB)]
    plan += [("split", 0), ("maxT", 0), ("measure", 1), ("norm", 1)]
    for n in range(NA):
        after = [[] for _ in range(CB)]
        c = n - 1
        here, rest = 0 <= c < NC, 0 <= c - 1 < NC
        if c >= 0:
            after[0] += [("evacuate", c), ("divide", c)]
        if n + 1 < NA:
            after[0] += [("xT", n + 1)]
        if rest:
            after[0] += [("U", c - 1, 1), ("G", c - 1, 2)]
        if n + 1 < NA:
            after[0] += [("K", n + 1)]
        if rest:
            after[1] += [("weightT", c - 1), ("U", c - 1, 2), ("G", c - 1, 3)]
        if n + 1 < NA:
            after[1] += [("Q", n + 1)]
            after[2] += [("V", n + 1, 0)]
        if rest:
            after[2] += [("U", c - 1, 3), ("shared", c - 1)]
        if n + 1 < NA:
            after[3] += [("round", n + 1, 1)]
        if rest:
            after[3] += [("gated", c - 1)]
        if n + 1 < NA:
            after[3] += [("V", n + 1, 1)]
            for b in range(4):
                after[3 + b] += [("low", n + 1, 2 * b + 1)]
        if here:
            after[3] += [("O", c)]
        if here:
            after[4] += [("fnorm", c)]
        if rest:
            after[4] += [("W", c - 1, p) for p in range(3)]
        if here:
            after[5] += [("fT", c)]
        if rest:
            after[5] += [("W", c - 1, 3)]
        if n + 1 < NA:
            after[6] += [("split", n + 1)]
        if here:
            after[6] += [("logits", c), ("G", c, 0), ("route", c)]
        if rest:
            after[6] += [("Y", c - 1)]
        if n + 2 < NA:
            after[6] += [("measure", n + 2)]
        if n + 1 < NA:
            after[7] += [("maxT", n + 1)]
        if here:
            after[7] += [("U", c, 0), ("G", c, 1)]
        if n + 2 < NA:
            after[7] += [("norm", n + 2)]
        if n == 0:
            after[5] += [("mask",)]
        if n == 1:
            after[5] += [("bias", 1)]
        if n == NA - 1:
            after[3] += [("last_bias",)]
        for b in range(CB):
            plan += [("scores", n, b)]
            if b == 1 and n + 1 < NA:
                plan += [("K2", n + 1)]
            if b == 2 and n + 1 < NA:
                plan += [("Q2", n + 1)]
            if 3 <= b < 7 and n + 1 < NA:
                plan += [("low", n + 1, 2 * (b - 3))]
            if b >= 1:
                plan += [("values", n, b - 1)]
            plan += after[b]
            if n == NA - 1 and b == SPLIT:
                plan += [("evacuate", n, 0), ("divide", n, 0)]
        plan += [("values", n, CB - 1)]
    plan += [("evacuate", NA - 1, 1), ("divide", NA - 1, 1)]
    last = range(NT // CT)
    plan += [("O1", k) for k in last]
    for k in last:
        plan += [("hnorm", k), ("hT", k), ("head_logits", k)]
    plan += [("head_logits_done",), ("probT",), ("hotT",)]
    plan += [("take", k) for k in last]
    plan += [("qkv", k) for k in range(H1 // 2)]
    plan += [("attT",), ("attB",)]
    plan += [("avT", k) for k in range(2)]
    plan += [("ao", k) for k in last]
    plan += [("aoT", k) for k in last]
    plan += [("back", 0)]
    for k in last:
        if k + 1 < len(last):
            plan += [("back", k + 1)]
        plan += [("finish", k)]
    return plan


def turns(plan):
    held, place, k = [0] * 5, {}, 0
    last_block = plan.index(("O1", 0))
    for at, stage in enumerate(plan):
        if stage[0] in GENERAL:
            bank = k % (3 if at < last_block else 5)
            place[stage] = (bank, held[bank])
            held[bank] += 1
            k += 1
    return place


GENERAL = {"bias", "xT", "Q", "K", "V", "maxT", "O", "fT", "logits", "G", "U", "shared", "weightT", "W", "Y",
           "O1", "hT", "probT", "hotT", "take", "qkv", "attT", "attB", "avT", "ao", "aoT", "back"}


def two_layers(nc, x, ctxT, maskT, const_f, const_b, w_a, w_b, w_f, w_l, out):
    plan = schedule()
    place = turns(plan)
    stack = ExitStack()
    with stack:
        def sb(name, shape, dt=F32):
            return stack.enter_context(nc.sbuf_tensor(name, shape, dt))

        def bank(name):
            return stack.enter_context(nc.psum_tensor(name, [P, 512], F32))

        def sem(name):
            return stack.enter_context(nc.semaphore(name))

        cf = sb("cf", [P, CF_N])
        cb = sb("cb", [P, CBF_N], BF16)
        wa = sb("wa", [P, WA_N])
        wb = sb("wb", [P, WB_N])
        wf = sb("wf", [P, WF_N])
        wl = sb("wl", [P, WL_N])
        xa = sb("xa", [P, NT, D])
        xn = sb("xn", [P, CT, D])
        fn = sb("fn", [P, CT, D])
        stats = sb("stats", [P, 16, 6])
        mean_var = sb("mean_var", [P, 16, 2])
        var_eps = sb("var_eps", [P, 16])
        rstd = sb("rstd", [P, 16])
        neg_mean = sb("neg_mean", [P, 16])
        offset = sb("offset", [P, 16])
        half_neg = sb("half_neg", [P, 16])
        xT = sb("xT", [P, 2, CW])
        fT = sb("fT", [P, CW])
        cT = sb("cT", [P, B * S])
        Qg = sb("Qg", [P, 2, CB, NG, S])
        Ki = sb("Ki", [P, 2, CB, NI, S])
        Qb = sb("Qb", [P, 2, CB, NG, S], BF16)
        Kb = sb("Kb", [P, 2, CB, NI, S], BF16)
        V2 = sb("V2", [P, 2, CB, 2, P])
        pT = sb("pT", [P, 3, 512])
        nmax = sb("nmax", [P, 2, CB * 8])
        nmax2 = sb("nmax2", [P, 2, CB * 8], BF16)
        shift = sb("shift", [P, 2, 512], BF16)
        den = sb("den", [P, 512])
        raw = sb("raw", [P, 512])
        oT = sb("oT", [P, B * S])
        maskb = sb("maskb", [P, B, 2, S], BF16)
        gated = sb("gated", [P, 4])
        bqg = sb("bqg", [P, 2, NG])
        bki = sb("bki", [P, 2, NI])
        obias = sb("obias", [P, 2, D])
        lg = sb("lg", [P, CT, NE])
        lw = sb("lw", [P, CT, NE])
        hot1 = sb("hot1", [P, CT, NE])
        hot2 = sb("hot2", [P, CT, NE])
        pr = sb("pr", [P, CT, NE])
        r4 = sb("r4", [P, 4, CT])
        cw3 = sb("cw3", [P, CT, 3, NE], BF16)
        cwT = sb("cwT", [P, CW], BF16)
        halves = sb("halves", [P, 2, 2, CW])
        th, gh = halves[:, 0, :, :], halves[:, 1, :, :]
        sil = sb("sil", [P, 2, CW])
        top8 = sb("top8", [P, 8, 8])
        top8_at = sb("top8_at", [P, 8, 8], mybir.dt.uint32)
        gu = sb("gu", [P, NP + 1, CW])
        hid = sb("hid", [P, NP, CW])
        xr = halves[:, :, :, :].rearrange("p k a w -> p (k a w)").rearrange("p (s d) -> p s d", s=SP)
        hn = sb("hn", [P, SP, D])
        mask = hn[0:S, :, :].bitcast(I32).rearrange("p s d -> p (s d)")
        at = Qg[:, :, :, :, :].rearrange("p a b g s -> p (a b g s)")
        hT = at[:, 0:2048].rearrange("p (h c s) -> p h c s", h=H1, c=CAP)
        avT = at[:, 2048:4096].rearrange("p (h c s) -> p h c s", h=H1, c=CAP)
        at = Ki[:, :, :, :, :].rearrange("p a b g s -> p (a b g s)")
        qkv = at[:, 0:3072].rearrange("p (h c e) -> p h c e", h=8, c=CAP)
        av = at[:, 3072:4096].rearrange("p (h c e) -> p h c e", h=8, c=CAP)
        at = V2[:, :, :, :, :].rearrange("p a b g s -> p (a b g s)")
        aoT = at[:, 0:2048].rearrange("p (s q r) -> p s q r", s=SP, q=NQ)
        ao = at[:, 2048:4096].rearrange("p (s d) -> p s d", s=SP)
        y = oT[:, :].rearrange("p (s d) -> p s d", s=SP)
        at = gu[:, :, :].rearrange("p a b -> p (a b)")
        takeT = at[:, 0:2048].rearrange("p (s q r) -> p s q r", s=SP, q=NQ)
        prod = at[:, 0:2048]
        at = hid[:, :, :].rearrange("p a b -> p (a b)")
        putT = at[:, 0:2048].rearrange("p (s q t) -> p s q t", s=SP, q=NQ)
        xnT = cT[:, :].rearrange("p (s r) -> p s r", s=SP)
        at = fT[:, :]
        sm = at[:, 0:256].rearrange("p (s h) -> p s h", s=SP)
        smr = at[:, 256:320].rearrange("p (k s) -> p k s", k=4)
        at = xT[:, :, :].rearrange("p a b -> p (a b)")
        pt = at[:, 0:256].rearrange("p (a q t) -> p a q t", a=2, q=NQ)
        w0 = at[:, 256:512].rearrange("p (a q t) -> p a q t", a=2, q=NQ)
        o1 = at[:, 512:768].rearrange("p (a q t) -> p a q t", a=2, q=NQ)
        o2 = at[:, 768:1024].rearrange("p (a q t) -> p a q t", a=2, q=NQ)
        at = xn[:, :, :].rearrange("p a b -> p (a b)")
        tm = at[:, 0:64].rearrange("p (k a q) -> p k a q", k=8, a=2)
        hot = at[:, 64:320].rearrange("p (a q t) -> p a q t", a=2, q=NQ)
        att = at[:, 320:352]
        attn = at[:, 352:384]
        at = fn[:, :, :].rearrange("p a b -> p (a b)")
        asT = at[:, 0:128]
        aeT = at[:, 128:256]
        ar = at[:, 256:272]

        bS = bank("scores")
        bT = [bank(f"scoresT{i}") for i in range(2)]
        bC = bank("context")
        bD = bank("denominators")
        bG = [bank(f"general{i}") for i in range(3)] + bT

        d_cf, d_cb, d_wa, d_wb, d_wf, d_wl, d_mask = (sem(f"loaded_{k}") for k in
                                                      ("cf", "cb", "wa", "wb", "wf", "wl", "mask"))
        d_x = [sem(f"loaded_x{c}") for c in range(NC)]
        d_c = [sem(f"loaded_ctx{c}") for c in range(NC)]
        general_full = [sem(f"general_full{i}") for i in range(5)]
        general_free = [sem(f"general_free{i}") for i in range(5)]
        vector_step, scalar_step, pool_step = sem("vector_step"), sem("scalar_step"), sem("pool_step")
        gates_ready, biases_ready, pools_ready = sem("gates_ready"), sem("biases_ready"), sem("pools_ready")
        zeros_ready, mask_ready = sem("zeros_ready"), sem("mask_ready")
        normed, var_ready, rstd_ready = sem("normed"), sem("var_ready"), sem("rstd_ready")
        fnormed = sem("fnormed")
        obias_ready, bias_added = sem("obias_ready"), sem("bias_added")
        xT_ready, fT_ready = sem("xT_ready"), sem("fT_ready")
        q_ready, k_ready, v_ready = sem("q_ready"), sem("k_ready"), sem("v_ready")
        qk_low_ready = sem("qk_low_ready")
        scores_done, max_done = sem("scores_done"), sem("max_done")
        nmax_ready, shift_ready = sem("nmax_ready"), sem("shift_ready")
        scoresT_done, exp_done, pv_done = sem("scoresT_done"), sem("exp_done"), sem("pv_done")
        context_ready, residual_ready, layer_ready = (sem("context_ready"), sem("residual_ready"),
                                                      sem("layer_ready"))
        logits_ready, route_exp, cw_ready, cwT_ready = (sem("logits_ready"), sem("route_exp"),
                                                        sem("cw_ready"), sem("cwT_ready"))
        tanh_done, silu_done, shared_done = sem("tanh_done"), sem("silu_done"), sem("shared_done")
        context_out, den_out = sem("context_out"), sem("den_out")
        gate_logits, gate_exp = sem("gate_logits"), sem("gate_exp")
        tops_ready, low_q, low_k = sem("tops_ready"), sem("low_q"), sem("low_k")
        parts_ready = sem("parts_ready")
        take_v, take_a = sem("take_v"), sem("take_a")
        cleared = sem("cleared")
        spilled, d_xr, stored = sem("spilled"), sem("loaded_xr"), sem("stored")
        hn_ready, hnT_ready, tl_ready, tl_exp = (sem("hn_ready"), sem("hnT_ready"), sem("tl_ready"),
                                                 sem("tl_exp"))
        probs_ready, hot_ready, take_ready = sem("probs_ready"), sem("hot_ready"), sem("take_ready")
        put_ready, hT_ready, qkv_ready = sem("put_ready"), sem("hT_ready"), sem("qkv_ready")
        att_ready, ash_ready, aexp_ready, attn_ready = (sem("att_ready"), sem("ash_ready"),
                                                        sem("aexp_ready"), sem("attn_ready"))
        av_ready, avT_ready, aoT_ready, ao_ready = (sem("av_ready"), sem("avT_ready"),
                                                    sem("aoT_ready"), sem("ao_ready"))
        out_bias, tail_zero, out_ready = sem("out_bias"), sem("tail_zero"), sem("out_ready")
        yn_ready, offset_ready, scaled = sem("yn_ready"), sem("offset_ready"), sem("scaled")
        prod_ready, av_pool_ready = sem("prod_ready"), sem("av_pool_ready")

        def col(tile, table, name):
            a, w = table[name]
            return tile[:, a:a + w]

        ident = col(cf, CF, "ident")
        identb = col(cb, CBF, "ident")

        spill = nc.dram_tensor("x_by_position", [B, S, D], F32).ap()
        spill_tiles = spill.rearrange("(j b) s d -> (b s) j d", b=2)

        def sequences(n, part):
            assert (part is not None) == (n == NA - 1)
            return {None: (0, CB), 0: (0, SPLIT), 1: (SPLIT, CB)}[part]

        def head_product(k, j):
            hs = slice(k - 3, k + 1)
            return (prod[:, 512 * j:512 * j + 512].rearrange("p (h i e) -> p h i e", h=4, i=2), qkv[:, hs, :, 0:E1],
                    qkv[:, hs, j:j + 1, E1:2 * E1].broadcast_to([P, 4, 2, E1]), ALU.mult)

        def weighted_values(hs, at):
            an = attn.rearrange("p (h i j) -> p h i j", i=2, j=2)
            n = hs.stop - hs.start
            terms = [prod[:, at + 128 * n * j:at + 128 * n * (j + 1)].rearrange("p (h i e) -> p h i e", h=n, i=2)
                     for j in range(2)]
            products = [(terms[j], qkv[:, hs, j:j + 1, 2 * E1:3 * E1].broadcast_to([P, n, 2, E1]),
                         an[:, hs, :, j].unsqueeze(3).broadcast_to([P, n, 2, E1]), ALU.mult) for j in range(2)]
            return products, (av[:, hs, :, :], terms[0], terms[1], ALU.add)

        def average_part(bank, k, i):
            src = bank[:, :].rearrange("p (j h s) -> p (j h) s", j=4, h=2)
            return avT[64 * i:64 * i + 64, 8 * k:8 * k + 8, i, :], src[64 * i:64 * i + 64, :, :]

        def output_part(bank, k, c):
            src = bank[:, :].rearrange("p (h c q s) -> p c h q s", h=CT, c=CAP, q=NQ)[:, c, :, :, :]
            return aoT[:, :, :, H1 * c + CT * k:H1 * c + CT * k + CT].rearrange("p s q h -> p h q s"), src

        def low_bank(n, b):
            return bC if n == 0 and b % 2 else bS

        def sum_banks(n, b):
            return (bS, bG[2]) if n == NA - 1 and b >= SPLIT else (bC, bD)

        def by_position(ap):
            return ap.rearrange("b (q s) d -> q b s d", q=NQ)

        def filled(engine, job):
            bank, before = place[job]
            engine.wait_ge(general_full[bank], before + 1)

        def full(engine, job):
            filled(engine, job)
            return bG[place[job][0]]

        def freed(job):
            return general_free[place[job][0]]

        def used(engine, job):
            bank, before = place[job]
            engine.wait_ge(general_free[bank], before + 1)

        block = stack.enter_context(nc.Block())

        @block.sync
        def _(sp):
            x_tiles = x.rearrange("(j b) s d -> (b s) j d", b=2)
            sp.dma_start(xa[:, 0:CT, :], x_tiles[:, 0:CT, :]).then_inc(d_x[0], 16)
            sp.dma_start(cf[:, :], const_f).then_inc(d_cf, 16)
            sp.dma_start(wa[:, :], w_a).then_inc(d_wa, 16)
            for c in range(NC):
                if c:
                    sp.dma_start(xa[:, CT * c:CT * c + CT, :], x_tiles[:, CT * c:CT * c + CT, :]).then_inc(d_x[c], 16)
                sp.dma_start(cT[:, CW * c:CW * c + CW], ctxT[:, CW * c:CW * c + CW]).then_inc(d_c[c], 16)
                if c == 0:
                    sp.dma_start(cb[:, :], const_b).then_inc(d_cb, 16)
            sp.dma_start(wf[:, :], w_f).then_inc(d_wf, 16)
            sp.dma_start(mask, maskT).then_inc(d_mask, 16)
            sp.dma_start(wb[:, :], w_b).then_inc(d_wb, 16)
            sp.dma_start(wl[:, :], w_l).then_inc(d_wl, 16)
            for c in range(NC):
                used(sp, ("Y", c))
                sp.dma_start(spill_tiles[:, CT * c:CT * c + CT, :], xa[:, CT * c:CT * c + CT, :]).then_inc(spilled, 16)
            sp.wait_ge(spilled, 16 * NC)
            for q in range(NQ):
                sp.dma_start(xr[32 * q:32 * q + 32, :, :], by_position(spill)[q]).then_inc(d_xr, 16)
            for k in range(NT // CT):
                sp.wait_ge(out_ready, k + 1)
                for q in range(NQ):
                    sp.dma_start(by_position(out)[q][:, CT * k:CT * k + CT, :],
                                 y[32 * q:32 * q + 32, CT * k:CT * k + CT, :]).then_inc(stored, 16)
            sp.wait_ge(stored, 16 * NQ * (NT // CT))

        @block.tensor
        def _(pe):
            def take(job):
                bank, before = place[job]
                if before:
                    pe.wait_ge(general_free[bank], before)
                elif bG[bank] in bT:
                    pe.wait_ge(exp_done, CB * NA)
                return bG[bank], general_full[bank]

            def out_bias_product(l):
                w, table = ((wa, WA), (wb, WB))[l]
                pe.wait_ge(d_wb if l else d_wa, 16)
                dst, done = take(("bias", l))
                bv = col(w, table, f"bv{l}")
                nc.tensor.matmul(dst[:, 0:D], bv.broadcast_to([P, P]), col(w, table, f"wo{l}"),
                                 start=True, stop=True).then_inc(done, 1)

            def transpose_tiles(job, tiles):
                dst, done = take(job)
                for j in range(CT):
                    last = nc.tensor.transpose(dst[:, P * j:P * j + P], tiles[:, j, :], ident)
                last.then_inc(done, 1)

            def queries(n):
                l = n // NC
                w, table = ((wa, WA), (wb, WB))[l]
                dst, done = take(("Q", n))
                used(pe, ("xT", n))
                nc.tensor.matmul(dst[:, :], col(w, table, f"wq{l}"), xT[:, n % 2, :],
                                 start=True, stop=True).then_inc(done, 1)

            def keys(n):
                l, c = divmod(n, NC)
                w, table = ((wa, WA), (wb, WB))[l]
                if l == 0:
                    pe.wait_ge(d_c[c], 16)
                dst, done = take(("K", n))
                nc.tensor.matmul(dst[:, :], col(w, table, f"wk{l}"), cT[:, CW * c:CW * c + CW],
                                 start=True, stop=True).then_inc(done, 1)

            def value_rows(n, half):
                l, c = divmod(n, NC)
                w, table = ((wa, WA), (wb, WB))[l]
                dst, done = take(("V", n, half))
                for b in range(4):
                    first = CW * c + S * (4 * half + b)
                    for i2 in range(2):
                        last = nc.tensor.matmul(dst[S * i2:S * i2 + S, P * b:P * b + P], cT[:, first:first + S],
                                                col(w, table, f"wv{l}"), start=True, stop=True)
                last.then_inc(done, 1)

            def low_scores(n, b):
                k = CB * n + b
                if k == 0:
                    pe.wait_ge(d_cb, 16)
                if b == 0:
                    pe.wait_ge(low_q, 2 * n + 1)
                    pe.wait_ge(low_k, 2 * n + 1)
                elif b == CB // 2:
                    pe.wait_ge(low_q, 2 * n + 2)
                    pe.wait_ge(low_k, 2 * n + 2)
                in_turns = 1 if n else 2
                if k >= in_turns:
                    pe.wait_ge(max_done, k - in_turns + 1)
                dst = low_bank(n, b)
                masked = n >= NC
                if masked:
                    if n == NC and b == 0:
                        pe.wait_ge(mask_ready, 3)
                    seq = CB * (n - NC) + b
                    nc.tensor.matmul(dst[:, :], col(cb, CBF, "twice"),
                                     maskb[:, seq, 0:1, :].broadcast_to([P, 8, S]),
                                     start=True, stop=False, skip_group_check=True)
                for gp in range(2):
                    last = nc.tensor.matmul(dst[:, 256 * gp:256 * gp + 256],
                                            Qb[:, n % 2, b, 2 * gp:2 * gp + 2, :].rearrange("p g s -> p (g s)"),
                                            Kb[:, n % 2, b, :, :].rearrange("p i t -> p (i t)"),
                                            start=not masked, stop=not masked or gp == 1,
                                            skip_group_check=masked)
                last.then_inc(scores_done, 1)

            def transpose_maxima(n):
                dst, done = take(("maxT", n))
                pe.wait_ge(nmax_ready, n + 1)
                nc.tensor.transpose(dst[:, :].bitcast(BF16)[:, 0:P],
                                    nmax2[:, :, :].rearrange("p a b -> p (a b)"), identb).then_inc(done, 1)

            def scores_transposed(n, b):
                k = CB * n + b
                if b == 0:
                    used(pe, ("maxT", n))
                if k >= 2:
                    pe.wait_ge(exp_done, k - 1)
                dst = bT[k % 2]
                masked = n >= NC
                pick = col(cb, CBF, "pick")[:, P * b:P * b + P]
                if masked:
                    seq = CB * (n - NC) + b
                    nc.tensor.matmul(dst[:, :], maskb[:, seq, :, :].rearrange("p a t -> p (a t)"),
                                     identb[:, 0:S].unsqueeze(1).broadcast_to([P, 8, S]),
                                     start=True, stop=False, skip_group_check=True)
                else:
                    nc.tensor.matmul(dst[:, :], pick, shift[:, n % 2, :], start=True, stop=False,
                                     skip_group_check=True)
                for ip in range(2):
                    last = nc.tensor.matmul(dst[:, 256 * ip:256 * ip + 256],
                                            Ki[:, n % 2, b, 2 * ip:2 * ip + 2, :].rearrange("p i t -> p (i t)"),
                                            Qg[:, n % 2, b, :, :].rearrange("p g s -> p (g s)"),
                                            start=False, stop=not masked and ip == 1, skip_group_check=True)
                if masked:
                    last = nc.tensor.matmul(dst[:, :], pick, shift[:, n % 2, :], start=False, stop=True,
                                            skip_group_check=True)
                last.then_inc(scoresT_done, 1)

            def values(n, b):
                k = CB * n + b
                if b == 0:
                    used(pe, ("V", n, 1))
                    if n >= 1:
                        pe.wait_ge(context_out, n)
                        pe.wait_ge(den_out, n)
                pe.wait_ge(exp_done, k + 1)
                ones = col(cf, CF, "ones_v").rearrange("p (a r) -> p a r", a=2)
                context, sums = sum_banks(n, b)
                for dst, w in ((context, None), (sums, ones)):
                    for ip in range(2):
                        for g in range(NG):
                            lhs = V2[:, n % 2, b, ip, 32 * g:32 * g + 32] if w is None else w[:, ip, :]
                            at = 256 * ip + S * g
                            last = nc.tensor.matmul(dst[32 * g:32 * g + 32, S * b:S * b + S], lhs,
                                                    pT[:, k % 3, at:at + S],
                                                    start=ip == 0, stop=ip == 1)
                last.then_inc(pv_done, 1)

            def project_out(n):
                dst, done = take(("O", n))
                pe.wait_ge(context_ready, n + 1)
                for j in range(CT):
                    first = CW * n + P * j
                    last = nc.tensor.matmul(dst[:, P * j:P * j + P], oT[:, first:first + P],
                                            col(wa, WA, "wo0"), start=True, stop=True)
                last.then_inc(done, 1)

            def expert_logits(c):
                if c == 0:
                    pe.wait_ge(d_wf, 16)
                dst, done = take(("logits", c))
                used(pe, ("fT", c))
                for j in range(CT):
                    last = nc.tensor.matmul(dst[:, NE * j:NE * j + NE], fT[:, P * j:P * j + P],
                                            col(wa, WA, "gate_w"), start=True, stop=True)
                last.then_inc(done, 1)

            def expert_in(job, w):
                def product(c, p):
                    dst, done = take((job, c, p))
                    nc.tensor.matmul(dst[:, :], col(wf, WF, w)[:, P * p:P * p + P], fT[:, :],
                                     start=True, stop=True).then_inc(done, 1)
                return product

            def shared_in(c):
                dst, done = take(("shared", c))
                nc.tensor.matmul(dst[:, :], col(wf, WF, "shared"), fT[:, :], start=True, stop=True).then_inc(done, 1)

            def weights_transposed(c):
                dst, done = take(("weightT", c))
                pe.wait_ge(cw_ready, c + 1)
                for j in range(CT):
                    last = nc.tensor.transpose(dst[0:3 * NE, :].bitcast(BF16)[:, P * j:P * j + P],
                                               cw3[:, j, :, :].rearrange("p a b -> p (a b)"), identb)
                last.then_inc(done, 1)

            def weights_spread(c, p):
                dst, done = take(("W", c, p))
                used(pe, ("weightT", c))
                nc.tensor.matmul(dst[:, :], col(cb, CBF, "experts")[:, P * p:P * p + P], cwT[:, :],
                                 start=True, stop=True).then_inc(done, 1)

            def expert_out(c):
                dst, done = take(("Y", c))
                used(pe, ("W", c, NP - 1))
                if c == 0:
                    pe.wait_ge(cleared, 4)
                for j in range(CT):
                    for p in range(NP + 1):
                        if p < NP:
                            lhs, rhs = hid[:, p, P * j:P * j + P], col(wf, WF, "wd")[:, D * p:D * p + D]
                        else:
                            lhs, rhs = gu[:, NP, P * j:P * j + P], col(wf, WF, "sd")
                        last = nc.tensor.matmul(dst[:, P * j:P * j + P], lhs, rhs, start=p == 0, stop=p == NP)
                last.then_inc(done, 1)

            def out_by_position(k):
                dst, done = take(("O1", k))
                if k == 0:
                    pe.wait_ge(context_ready, NA + 1)
                for j in range(CT):
                    last = nc.tensor.matmul(dst[:, P * j:P * j + P], oT[:, P * (CT * k + j):P * (CT * k + j) + P],
                                            col(wb, WB, "wo1"), start=True, stop=True)
                last.then_inc(done, 1)

            def head_logits(k):
                used(pe, ("hT", k))
                if k == 0:
                    pe.wait_ge(d_wl, 16)
                for j in range(CT * k, CT * k + CT):
                    nc.tensor.matmul(bS[:, H1 * j:H1 * j + H1], xnT[:, j, :], col(wl, WL, "Wg"),
                                     start=True, stop=True).then_inc(gate_logits, 1)

            def probabilities_transposed():
                dst, done = take(("probT",))
                pe.wait_ge(probs_ready, 1)
                for a in range(2):
                    last = nc.tensor.transpose(dst[:, P * a:P * a + P],
                                               sm[:, 8 * a:8 * a + 8, :].rearrange("p s h -> p (s h)"), ident)
                last.then_inc(done, 1)

            def choices_transposed():
                dst, done = take(("hotT",))
                pe.wait_ge(hot_ready, 1)
                for c in range(CAP):
                    for a in range(2):
                        src = (o1 if c == 0 else o2)[:, a, :, :].rearrange("p q t -> p (q t)")
                        last = nc.tensor.transpose(dst[:, 256 * c + P * a:256 * c + P * a + P], src, ident)
                last.then_inc(done, 1)

            def take_tokens(k):
                dst, done = take(("take", k))
                if k == 0:
                    pe.wait_ge(take_v, 1)
                    pe.wait_ge(take_a, 1)
                for j in range(CT):
                    s = CT * k + j
                    last = nc.tensor.matmul(dst[:, P * j:P * j + P], hn[:, s, :],
                                            takeT[:, s, :, :].rearrange("p q r -> p (q r)"),
                                            start=True, stop=True)
                last.then_inc(done, 1)

            def head_projections(k):
                dst, done = take(("qkv", k))
                if k == 0:
                    used(pe, ("take", NT // CT - 1))
                for c in range(CAP):
                    for h2 in range(2):
                        h = 2 * k + h2
                        last = nc.tensor.matmul(dst[64 * h2:64 * h2 + 64, 192 * c:192 * c + 192],
                                                hT[:, h, c, :], col(wl, WL, "Wqkv")[:, 192 * h:192 * h + 192],
                                                start=True, stop=True)
                last.then_inc(done, 1)

            def head_scores_transposed():
                dst, done = take(("attT",))
                pe.wait_ge(att_ready, 4)
                nc.tensor.transpose(dst[0:32, 0:P], att, ident).then_inc(done, 1)

            def head_weights_back():
                dst, done = take(("attB",))
                pe.wait_ge(attn_ready, 1)
                nc.tensor.transpose(dst[:, 0:32], asT[0:32, :], ident[0:32, 0:32]).then_inc(done, 1)

            def head_values_transposed(k):
                dst, done = take(("avT", k))
                pe.wait_ge(av_ready, k + 1)
                if k:
                    pe.wait_ge(av_pool_ready, 1)
                for j in range(4):
                    last = nc.tensor.transpose(dst[:, P * j:P * j + P],
                                               av[:, 4 * k + j, :, :].rearrange("p c e -> p (c e)"), ident)
                last.then_inc(done, 1)

            def head_outputs(k):
                dst, done = take(("ao", k))
                if k % 2 == 0:
                    used(pe, ("avT", k // 2))
                for j in range(CT):
                    h = CT * k + j
                    last = nc.tensor.matmul(dst[:, P * j:P * j + P], col(wl, WL, "Wo")[:, D * h:D * h + D],
                                            avT[:, h, :, :].rearrange("p c s -> p (c s)"), start=True, stop=True)
                last.then_inc(done, 1)

            def head_outputs_transposed(k):
                dst, done = take(("aoT", k))
                if k == 0:
                    used(pe, ("ao", NT // CT - 2))
                    used(pe, ("ao", NT // CT - 1))
                for j in range(CT):
                    last = nc.tensor.transpose(dst[:, P * j:P * j + P],
                                               aoT[:, CT * k + j, :, :].rearrange("p q r -> p (q r)"), ident)
                last.then_inc(done, 1)

            def put_back(k):
                dst, done = take(("back", k))
                used(pe, ("aoT", k))
                if k == 0:
                    pe.wait_ge(put_ready, 1)
                for j in range(CT):
                    s = CT * k + j
                    nc.tensor.matmul(dst[:, P * j:P * j + P], ident, hn[:, s, :], start=True, stop=False)
                    last = nc.tensor.matmul(dst[:, P * j:P * j + P],
                                            putT[:, s, :, :].rearrange("p q t -> p (q t)"), ao[:, s, :],
                                            start=False, stop=True)
                last.then_inc(done, 1)

            def tokens_transposed(n):
                pe.wait_ge(normed, n + 1)
                if n == 0:
                    pe.wait_ge(d_cf, 16)
                transpose_tiles(("xT", n), xn)

            def expert_tokens_transposed(c):
                pe.wait_ge(fnormed, c + 1)
                transpose_tiles(("fT", c), fn)

            def last_tokens_transposed(k):
                pe.wait_ge(hn_ready, k + 1)
                transpose_tiles(("hT", k), hn[:, CT * k:CT * k + CT, :])

            part = {"bias": out_bias_product, "xT": tokens_transposed, "Q": queries, "K": keys, "V": value_rows,
                    "low": low_scores, "maxT": transpose_maxima, "scores": scores_transposed, "values": values,
                    "O": project_out, "fT": expert_tokens_transposed, "logits": expert_logits,
                    "G": expert_in("G", "wg"), "U": expert_in("U", "wu"), "shared": shared_in,
                    "weightT": weights_transposed, "W": weights_spread, "Y": expert_out,
                    "O1": out_by_position, "hT": last_tokens_transposed, "head_logits": head_logits,
                    "probT": probabilities_transposed, "hotT": choices_transposed, "take": take_tokens,
                    "qkv": head_projections, "attT": head_scores_transposed, "attB": head_weights_back,
                    "avT": head_values_transposed, "ao": head_outputs, "aoT": head_outputs_transposed,
                    "back": put_back}
            for stage, *where in plan:
                if stage in part:
                    part[stage](*where)

        @block.vector
        def _(ve):
            V = nc.vector
            steps = [0]

            def settled(ins):
                steps[0] += 1
                ins.then_inc(vector_step, 1)
                ve.wait_ge(vector_step, steps[0])

            def spread(src, slot):
                for j in range(CT):
                    last = V.bn_stats(stats[:, CT * slot + j, :], src[:, j, :])
                settled(last)
                for j in range(CT):
                    last = V.bn_aggr(mean_var[:, CT * slot + j, :], stats[:, CT * slot + j, :])
                settled(last)
                tiles = slice(CT * slot, CT * slot + CT)
                V.tensor_scalar(neg_mean[:, tiles], mean_var[:, tiles, 0], -1.0, None, ALU.mult)
                V.tensor_scalar(var_eps[:, tiles], mean_var[:, tiles, 1], EPS, None, ALU.add).then_inc(var_ready, 1)

            measures = [0]
            measured = {}

            def measure(src, slot):
                for j in range(CT):
                    last = V.bn_stats(stats[:, CT * slot + j, :], src[:, j, :])
                settled(last)
                for j in range(CT):
                    last = V.bn_aggr(mean_var[:, CT * slot + j, :], stats[:, CT * slot + j, :])
                settled(last)
                V.tensor_scalar(var_eps[:, CT * slot:CT * slot + CT], mean_var[:, CT * slot:CT * slot + CT, 1],
                                EPS, None, ALU.add).then_inc(var_ready, 1)
                measures[0] += 1
                measured[slot] = measures[0]

            def normalise(src, dst, slot, done):
                ve.wait_ge(rstd_ready, measured[slot])
                for j in range(CT):
                    ins = V.tensor_scalar(dst[:, j, :], src[:, j, :], mean_var[:, CT * slot + j, 0:1],
                                          rstd[:, CT * slot + j:CT * slot + j + 1], ALU.subtract, ALU.mult)
                ins.then_inc(done, 1)

            def measure_tokens(n):
                c = n % NC
                if n < NC:
                    ve.wait_ge(d_x[c], 16)
                else:
                    used(ve, ("Y", c))
                measure(xa[:, CT * c:CT * c + CT, :], n % 2)

            def norm_tokens(n):
                c = n % NC
                if n >= 1:
                    filled(ve, ("xT", n - 1))
                normalise(xa[:, CT * c:CT * c + CT, :], xn, n % 2, normed)

            def norm_for_experts(c):
                if c >= 1:
                    filled(ve, ("fT", c - 1))
                normalise(xa[:, CT * c:CT * c + CT, :], fn, 2 + c % 2, fnormed)

            def spread_some(n, groups):
                l = n // NC
                ve.wait_ge(biases_ready, l + 1)
                src = full(ve, ("Q", n))
                for g in range(*groups):
                    ins = V.tensor_scalar(Qg[:, n % 2, :, g, :], src[:, :].rearrange("p (b s) -> p b s", b=CB),
                                          col(cf, CF, "gmask")[:, g:g + 1], bqg[:, l, g:g + 1], ALU.mult, ALU.add)
                return ins

            def spread_queries(n):
                spread_some(n, (0, NG // 2))

            def spread_other_queries(n):
                spread_some(n, (NG // 2, NG)).then_inc(freed(("Q", n)), 1)
                used(ve, ("Q", n))
                round_queries(n, 0)

            def round_queries(n, half):
                part = slice(CB // 2 * half, CB // 2 * (half + 1))
                V.tensor_copy(Qb[:, n % 2, part, :, :], Qg[:, n % 2, part, :, :]).then_inc(low_q, 1)

            def row_maximum(n, b):
                k = CB * n + b
                ve.wait_ge(scores_done, k + 1)
                V.tensor_reduce(nmax[:, n % 2, 8 * b:8 * b + 8], low_bank(n, b)[:, :].rearrange("p (r t) -> p r t", r=8),
                                AX.X, ALU.max, negate=True).then_inc(max_done, 1)

            def split_maxima(n):
                ve.wait_ge(max_done, CB * (n + 1))
                if n >= 1:
                    filled(ve, ("maxT", n - 1))
                settled(V.tensor_copy(nmax2[:, 0, :], nmax[:, n % 2, :]))
                V.tensor_tensor(nmax2[:, 1, :], nmax[:, n % 2, :], nmax2[:, 0, :], ALU.subtract).then_inc(nmax_ready, 1)

            def spread_shift(n):
                src = full(ve, ("maxT", n))
                if n >= 2:
                    ve.wait_ge(scoresT_done, CB * (n - 1))
                V.tensor_tensor(shift[:, n % 2, :].rearrange("p (a r) -> p a r", a=4),
                                src[:, :].bitcast(BF16)[:, 0:P].unsqueeze(1).broadcast_to([P, 4, P]),
                                col(cf, CF, "cmask").unsqueeze(2).broadcast_to([P, 4, P]),
                                ALU.mult).then_inc(freed(("maxT", n)), 1)

            def evacuate(n, part=None):
                first, end = sequences(n, part)
                ve.wait_ge(pv_done, CB * n + end)
                if n >= 1:
                    ve.wait_ge(context_ready, n)
                cols = slice(S * first, S * end)
                V.tensor_copy(raw[:, cols], sum_banks(n, first)[0][:, cols]).then_inc(context_out, 1)

            def divide(n, part=None):
                c = n % NC
                first, end = sequences(n, part)
                cols = slice(S * first, S * end)
                ve.wait_ge(den_out, n + 1 + (part or 0))
                settled(V.reciprocal(den[:, cols], den[:, cols]))
                dst, parts = oT[:, CW * c:CW * c + CW], [raw[:, cols], den[:, cols]]
                if n >= NC:
                    dst = oT[:, :].rearrange("p (s q b) -> p b q s", s=SP, q=NQ)[:, CB * c + first:CB * c + end, :, :]
                    parts = [ap.rearrange("p (b q s) -> p b q s", q=NQ, s=SP) for ap in parts]
                V.tensor_tensor(dst, *parts, ALU.mult).then_inc(context_ready, 1)

            def add_attention(n):
                src = full(ve, ("O", n))
                ve.wait_ge(bias_added, n + 1)
                part = xa[:, CT * n:CT * n + CT, :]
                flat = part.rearrange("p j d -> p (j d)")
                V.scalar_tensor_tensor(flat, src[:, :], gated[:, 0:1], flat, ALU.mult, ALU.add).then_inc(freed(("O", n)), 1)
                used(ve, ("O", n))
                measure(part, 2 + n % 2)

            def route_logits(c):
                src = full(ve, ("logits", c))[:, 0:CT * NE].rearrange("p (j e) -> p j e", e=NE)
                settled(V.tensor_reduce(r4[:, 0, :], src, AX.X, ALU.max))
                V.tensor_tensor(lg[:, :, :], src, r4[:, 0, :].unsqueeze(2).broadcast_to([P, CT, NE]),
                                ALU.subtract).then_inc(freed(("logits", c)), 1)

            def route(c):
                def bc(ap):
                    return ap.unsqueeze(2).broadcast_to([P, CT, NE])
                ve.wait_ge(route_exp, c + 1)
                settled(V.tensor_reduce(r4[:, 1, :], pr[:, :, :], AX.X, ALU.add))
                settled(V.reciprocal(r4[:, 2, :], r4[:, 1, :]))
                settled(V.tensor_tensor(pr[:, :, :], pr[:, :, :], bc(r4[:, 2, :]), ALU.mult))
                order = col(cf, CF, "first8").rearrange("p (j e) -> p j e", e=NE)
                for hot_, src_ in ((hot1, pr), (hot2, lw)):
                    settled(V.tensor_reduce(r4[:, 0, :], src_[:, :, :], AX.X, ALU.max))
                    settled(V.tensor_tensor(hot_[:, :, :], src_[:, :, :], bc(r4[:, 0, :]), ALU.is_equal))
                    settled(V.tensor_tensor(hot_[:, :, :], hot_[:, :, :], order, ALU.mult))
                    settled(V.tensor_reduce(r4[:, 1, :], hot_[:, :, :], AX.X, ALU.max))
                    settled(V.tensor_tensor(hot_[:, :, :], hot_[:, :, :], bc(r4[:, 1, :]), ALU.is_equal))
                    if hot_ is hot1:
                        settled(V.scalar_tensor_tensor(lw[:, :, :], hot1[:, :, :], -4.0, pr[:, :, :], ALU.mult, ALU.add))
                settled(V.tensor_tensor(hot1[:, :, :], hot1[:, :, :], hot2[:, :, :], ALU.add))
                settled(V.tensor_tensor(lw[:, :, :], hot1[:, :, :], pr[:, :, :], ALU.mult))
                if c >= 1:
                    filled(ve, ("weightT", c - 1))
                settled(V.tensor_copy(cw3[:, :, 0, :], lw[:, :, :]))
                settled(V.tensor_tensor(lw[:, :, :], lw[:, :, :], cw3[:, :, 0, :], ALU.subtract))
                settled(V.tensor_copy(cw3[:, :, 1, :], lw[:, :, :]))
                V.tensor_tensor(cw3[:, :, 2, :], lw[:, :, :], cw3[:, :, 1, :], ALU.subtract).then_inc(cw_ready, 1)

            def gate_up(c, p):
                ve.wait_ge(silu_done, (NP + 1) * c + p + 1)
                src = full(ve, ("U", c, p))
                V.tensor_tensor(gu[:, p, :], sil[:, ((NP + 1) * c + p) % 2, :], src[:, :], ALU.mult).then_inc(freed(("U", c, p)), 1)

            def gate_shared(c):
                ve.wait_ge(silu_done, (NP + 1) * (c + 1))
                src = full(ve, ("shared", c))
                V.tensor_tensor(gu[0:F, NP, :], sil[0:F, ((NP + 1) * c + NP) % 2, :], src[F:2 * F, :], ALU.mult).then_inc(freed(("shared", c)), 1)

            def weigh(c, p):
                src = full(ve, ("W", c, p))
                if p == 0:
                    used(ve, ("U", c, NP - 1))
                V.tensor_tensor(hid[:, p, :], gu[:, p, :], src[:, :], ALU.mult).then_inc(freed(("W", c, p)), 1)

            def add_experts(c):
                src = full(ve, ("Y", c))
                part = xa[:, CT * c:CT * c + CT, :].rearrange("p j d -> p (j d)")
                V.scalar_tensor_tensor(part, src[:, :], gated[:, 1:2], part, ALU.mult, ALU.add).then_inc(freed(("Y", c)), 1)

            def mask_bias():
                ve.wait_ge(d_mask, 16)
                ve.wait_ge(mask_ready, 1)
                for k in range(2):
                    V.tensor_scalar(maskb[0:S, :, k, :], mask.rearrange("p (b t) -> p b t", b=B), 0.0, BIG,
                                    ALU.is_equal, ALU.mult).then_inc(mask_ready, 1)

            def biases(l):
                w, table = ((wa, WA), (wb, WB))[l]
                if l:
                    ve.wait_ge(d_wb, 16)
                else:
                    ve.wait_ge(d_wa, 16)
                    ve.wait_ge(d_cf, 16)
                    ve.wait_ge(gates_ready, 1)
                V.tensor_scalar(bqg[:, l, :], col(cf, CF, "gmask"), col(w, table, f"bq{l}"), None, ALU.mult)
                V.tensor_scalar(bki[:, l, :], col(cf, CF, "imask"), col(w, table, f"bk{l}"), None,
                                ALU.mult).then_inc(biases_ready, 1)
                src = full(ve, ("bias", l))
                V.tensor_tensor(obias[:, l, :], src[:, 0:D], col(w, table, f"bo{l}"), ALU.add).then_inc(freed(("bias", l)), 1)
                used(ve, ("bias", l))
                V.tensor_scalar(obias[:, l, :], obias[:, l, :], gated[:, 2 * l:2 * l + 1], None,
                                ALU.mult).then_inc(obias_ready, 1)


            def add_last_attention(k):
                if k == 0:
                    ve.wait_ge(d_xr, 16 * NQ)
                    ve.wait_ge(bias_added, NC + 1)
                part = xr[:, CT * k:CT * k + CT, :]
                flat = part.rearrange("p j d -> p (j d)")
                src = full(ve, ("O1", k))
                V.scalar_tensor_tensor(flat, src[:, :], gated[:, 2:3], flat, ALU.mult, ALU.add).then_inc(freed(("O1", k)), 1)
                used(ve, ("O1", k))
                spread(part, k)

            def head_probabilities():
                ve.wait_ge(gate_logits, SP)
                src = bS[:, 0:SP * H1].rearrange("p (s h) -> p s h", h=H1)

                def over(ap):
                    return ap.unsqueeze(2).broadcast_to([P, SP, H1])
                settled(V.tensor_reduce(smr[:, 0, :], src, AX.X, ALU.max))
                V.tensor_tensor(sm, src, over(smr[:, 0, :]), ALU.subtract).then_inc(gate_exp, 1)
                ve.wait_ge(tl_exp, 1)
                settled(V.tensor_reduce(smr[:, 1, :], sm, AX.X, ALU.add))
                settled(V.reciprocal(smr[:, 2, :], smr[:, 1, :]))
                V.tensor_tensor(sm, sm, over(smr[:, 2, :]), ALU.mult).then_inc(probs_ready, 1)

            def choose():
                src = full(ve, ("probT",))[:, 0:256]
                V.tensor_copy(pt.rearrange("p a q t -> p (a q t)"), src).then_inc(freed(("probT",)), 1)
                used(ve, ("probT",))
                rows_ = pt.rearrange("p a q t -> p (a q) t")
                for r in range(8):
                    last = V.max(top8[:, r, :], rows_[:, r, :])
                settled(last)
                for r in range(8):
                    last = V.max_index(top8_at[:, r, :], top8[:, r, :], rows_[:, r, :])
                settled(last)
                sequence = col(cf, CF, "sequence").unsqueeze(1).broadcast_to([P, 8, B])
                first, second = (tm[:, r, :, :].rearrange("p a q -> p (a q)") for r in range(2))
                V.tensor_tensor(first, top8_at[:, :, 0], top8_at[:, :, 1], ALU.min)
                settled(V.tensor_tensor(second, top8_at[:, :, 0], top8_at[:, :, 1], ALU.max))
                for at, hot_ in ((first, o1), (second, o2)):
                    last = V.tensor_tensor(hot_.rearrange("p a q t -> p (a q) t"), sequence,
                                           at.unsqueeze(2).broadcast_to([P, 8, B]), ALU.is_equal)
                last.then_inc(hot_ready, 1)

            def place_choices(q):
                src = bG[place[("hotT",)][0]][32 * q:32 * q + 32, :].rearrange("p (c s h) -> p c s h", c=CAP, s=SP)
                return takeT[32 * q:32 * q + 32, :, q, :].rearrange("p s (c h) -> p c s h", c=CAP), src

            def choices_placed():
                ve.wait_ge(cleared, 6)
                full(ve, ("hotT",))
                for q in (0, 1):
                    last = V.tensor_copy(*place_choices(q))
                last.then_inc(take_v, 1)
                ve.wait_ge(take_a, 1)
                ve.wait_ge(take_v, 1)
                for q in range(NQ):
                    last = V.transpose(putT[32 * q:32 * q + 32, :, q, :], takeT[32 * q:32 * q + 32, :, q, :])
                last.then_inc(put_ready, 1)
                ve.wait_ge(put_ready, 1)
                V.tensor_copy(tm[:, 2, :, :], tm[:, 0, :, :]).then_inc(freed(("hotT",)), 1)

            def head_features(k):
                if k == 0:
                    ve.wait_ge(d_wl, 16)
                bias = col(wl, WL, "bqkv").rearrange("p (h e) -> p h e", e=3 * E1)
                src = full(ve, ("qkv", k))[:, 0:2 * 192].rearrange("p (c e) -> p c e", c=CAP)
                V.tensor_tensor(qkv[:, k, :, :], src, bias[:, k:k + 1, :].broadcast_to([P, CAP, 3 * E1]),
                                ALU.add).then_inc(freed(("qkv", k)), 1)
                if k % 4 == 3:
                    used(ve, ("qkv", k))
                    if k > 3:
                        ve.wait_ge(att_ready, 2)
                    settled(V.tensor_tensor(*head_product(k, 0)))
                    att_v = att.rearrange("p (h i j) -> p h i j", i=2, j=2)
                    for j in range(2):
                        if j:
                            ve.wait_ge(prod_ready, k // 4 + 1)
                        V.tensor_reduce(att_v[:, k - 3:k + 1, :, j], head_product(k, j)[0], AX.X,
                                        ALU.add).then_inc(att_ready, 1)

            def head_softmax():
                src = full(ve, ("attT",))[0:32, 0:P].rearrange("p (b s) -> p b s", b=2)
                settled(V.tensor_reduce(ar[0:32, 0:2], src, AX.X, ALU.max))
                V.tensor_tensor(asT[0:32, :].rearrange("p (b s) -> p b s", b=2), src,
                                ar[0:32, 0:2].unsqueeze(2).broadcast_to([32, 2, S]), ALU.subtract).then_inc(freed(("attT",)), 1)
                ve.wait_ge(aexp_ready, 1)
                ex = aeT[0:32, :].rearrange("p (b s) -> p b s", b=2)
                settled(V.tensor_reduce(ar[0:32, 2:4], ex, AX.X, ALU.add))
                settled(V.reciprocal(ar[0:32, 4:6], ar[0:32, 2:4]))
                V.tensor_tensor(asT[0:32, :].rearrange("p (b s) -> p b s", b=2), ex,
                                ar[0:32, 4:6].unsqueeze(2).broadcast_to([32, 2, S]), ALU.mult).then_inc(attn_ready, 1)

            def head_averages():
                src = full(ve, ("attB",))
                V.tensor_copy(attn, src[:, 0:32]).then_inc(freed(("attB",)), 1)
                used(ve, ("attB",))
                at = 512
                for pairs in VECTOR_PAIRS:
                    products, total = weighted_values(pairs, at)
                    for operands in products:
                        last = V.tensor_tensor(*operands)
                    settled(last)
                    V.tensor_tensor(*total).then_inc(av_ready, 1)
                    at += 2 * 128 * (pairs.stop - pairs.start)

            def place_averages(k):
                if k % 2:
                    return
                ve.wait_ge(cleared, 7)
                src = full(ve, ("avT", k))
                for i in range(2):
                    last = V.tensor_copy(*average_part(src, k, i))
                last.then_inc(freed(("avT", k)), 1)

            def place_outputs(k):
                if k % 2:
                    return
                src = full(ve, ("ao", k))
                for c in range(CAP):
                    last = V.tensor_scalar(*output_part(src, k, c), col(wl, WL, "bo"), None, ALU.add)
                last.then_inc(freed(("ao", k)), 1)

            def add_heads(k):
                src = full(ve, ("back", k))
                spread(src[:, :].rearrange("p (j d) -> p j d", d=D), k)

            def finish(k):
                used(ve, ("back", k))
                if k == 0:
                    ve.wait_ge(out_bias, 1)
                part = slice(CT * k, CT * k + CT)
                V.tensor_tensor(y[:, part, :], y[:, part, :],
                                col(wl, WL, "ln_g").unsqueeze(1).broadcast_to([P, CT, D]), ALU.mult).then_inc(scaled, 1)

            part = {"bias": biases, "mask": mask_bias, "measure": measure_tokens, "norm": norm_tokens, "Q": spread_queries, "Q2": spread_other_queries, "round": round_queries,
                    "low": row_maximum, "split": split_maxima, "maxT": spread_shift, "evacuate": evacuate,
                    "divide": divide, "O": add_attention, "fnorm": norm_for_experts, "logits": route_logits,
                    "route": route, "U": gate_up, "gated": gate_shared, "W": weigh, "Y": add_experts,
                    "O1": add_last_attention, "head_logits_done": head_probabilities,
                    "probT": choose, "hotT": choices_placed, "qkv": head_features, "attT": head_softmax,
                    "attB": head_averages, "avT": place_averages, "ao": place_outputs, "back": add_heads,
                    "finish": finish}
            for stage, *where in plan:
                if stage in part:
                    part[stage](*where)

        @block.scalar
        def _(ae):
            A = nc.scalar

            def spread_some(n, heads):
                l = n // NC
                ae.wait_ge(biases_ready, l + 1)
                src = full(ae, ("K", n))
                for i in range(*heads):
                    ins = A.activation(Ki[:, n % 2, :, i, :], src[:, :].rearrange("p (b s) -> p b s", b=CB),
                                       ACT.Identity, bias=bki[:, l, i:i + 1], scale=col(cf, CF, "imask")[:, i:i + 1])
                return ins

            def spread_keys(n):
                spread_some(n, (0, NI // 2))

            def spread_other_keys(n):
                spread_some(n, (NI // 2, NI)).then_inc(freed(("K", n)), 1)
                used(ae, ("K", n))
                round_keys(n, 0)

            def round_keys(n, half):
                part = slice(CB // 2 * half, CB // 2 * (half + 1))
                A.activation(Kb[:, n % 2, part, :, :], Ki[:, n % 2, part, :, :], ACT.Copy).then_inc(low_k, 1)

            def place_values(n, half):
                if n < 2:
                    ae.wait_ge(cleared, n + 1)
                src = full(ae, ("V", n, half))[:, :].rearrange("p (b g r) -> p b g r", b=4, g=NG)
                for i in range(NI):
                    ip, i2 = divmod(i, 2)
                    rows = slice(64 * i2, 64 * i2 + 64)
                    dst = V2[rows, n % 2, 4 * half:4 * half + 4, ip, :].rearrange("p b (g r) -> p b g r", g=NG)
                    ins = A.activation(dst[:, :, :, DH * i:DH * i + DH], src[rows, :, :, DH * i:DH * i + DH], ACT.Copy)
                ins.then_inc(freed(("V", n, half)), 1)

            def copy_xT(n):
                src = full(ae, ("xT", n))
                A.activation(xT[:, n % 2, :], src[:, :], ACT.Copy).then_inc(freed(("xT", n)), 1)

            def exponentials(n, b):
                k = CB * n + b
                ae.wait_ge(scoresT_done, k + 1)
                if k >= 3:
                    ae.wait_ge(pv_done, k - 2)
                A.activation(pT[:, k % 3, :], bT[k % 2][:, :], ACT.Exp, scale=SCALE).then_inc(exp_done, 1)

            def evacuate(n, part=None):
                first, end = sequences(n, part)
                ae.wait_ge(pv_done, CB * n + end)
                if n >= 1:
                    ae.wait_ge(context_ready, n)
                cols = slice(S * first, S * end)
                A.activation(den[:, cols], sum_banks(n, first)[1][:, cols], ACT.Copy).then_inc(den_out, 1)

            def route_exponentials(c):
                used(ae, ("logits", c))
                A.activation(pr[:, :, :], lg[:, :, :], ACT.Exp).then_inc(route_exp, 1)

            def silu_parts(job, c, p):
                src = full(ae, job)
                k = (NP + 1) * c + p
                if k >= 2:
                    ae.wait_ge(silu_done, k - 1)
                A.activation(th[:, k % 2, :], src[:, :], ACT.Tanh, scale=0.5).then_inc(tanh_done, 1)
                copy = A.activation(gh[:, k % 2, :], src[:, :], ACT.Copy, scale=0.5)
                if p < NP:
                    copy.then_inc(freed(job), 1)
                ae.wait_ge(tanh_done, k + 1)
                A.activation(th[:, k % 2, :], th[:, k % 2, :], ACT.Copy, bias=1.0).then_inc(parts_ready, 1)

            def silu_gate(c, p):
                silu_parts(("G", c, p), c, p)

            def silu_shared(c):
                silu_parts(("shared", c), c, NP)

            def copy_weights(c):
                src = full(ae, ("weightT", c))
                if c == 0:
                    ae.wait_ge(cleared, 3)
                A.activation(cwT[0:3 * NE, :], src[0:3 * NE, :].bitcast(BF16)[:, 0:CW], ACT.Copy).then_inc(freed(("weightT", c)), 1)

            def copy_fT(n):
                src = full(ae, ("fT", n))
                A.activation(fT[:, :], src[:, :], ACT.Copy).then_inc(freed(("fT", n)), 1)

            def normalise(src, dst, slot, turn, done):
                ae.wait_ge(offset_ready, turn + 1)
                for j in range(CT):
                    t = CT * slot + j
                    ins = A.activation(dst[:, j, :], src[:, j, :], ACT.Identity, scale=rstd[:, t:t + 1],
                                       bias=offset[:, t:t + 1])
                ins.then_inc(done, 1)

            def norm_last(k):
                tiles = slice(CT * k, CT * k + CT)
                normalise(xr[:, tiles, :], hn[:, tiles, :], k, k, hn_ready)

            def norm_out(k):
                src = full(ae, ("back", k))[:, :].rearrange("p (j d) -> p j d", d=D)
                normalise(src, y[:, CT * k:CT * k + CT, :], k, NT // CT + k, freed(("back", k)))

            def copy_hT(k):
                src = full(ae, ("hT", k))
                A.activation(cT[:, CW * k:CW * k + CW], src[:, :], ACT.Copy).then_inc(freed(("hT", k)), 1)

            def head_exponentials():
                ae.wait_ge(gate_exp, 1)
                A.activation(sm, sm, ACT.Exp).then_inc(tl_exp, 1)

            def place_choices():
                ae.wait_ge(cleared, 6)
                src = full(ae, ("hotT",))
                for q in (2, 3):
                    rows_ = slice(32 * q, 32 * q + 32)
                    last = A.activation(takeT[rows_, :, q, :].rearrange("p s (c h) -> p c s h", c=CAP),
                                        src[rows_, :].rearrange("p (c s h) -> p c s h", c=CAP, s=SP), ACT.Copy)
                last.then_inc(take_a, 1)

            def place_tokens(k):
                src = full(ae, ("take", k))[:, :].rearrange("p (s q c h) -> p c h q s", s=CT, q=NQ, c=CAP)
                for c in range(CAP):
                    dst = hT[:, :, c, :].rearrange("p h (q s) -> p h q s", q=NQ)[:, :, :, CT * k:CT * k + CT]
                    ins = A.activation(dst, src[:, c, :, :, :], ACT.Copy)
                ins.then_inc(freed(("take", k)), 1)

            def place_averages(k):
                if k % 2 == 0:
                    return
                ae.wait_ge(cleared, 7)
                src = full(ae, ("avT", k))
                for i in range(2):
                    last = A.activation(*average_part(src, k, i), ACT.Copy)
                last.then_inc(freed(("avT", k)), 1)

            def place_outputs(k):
                if k % 2 == 0:
                    return
                src = full(ae, ("ao", k))
                for c in range(CAP):
                    last = A.activation(*output_part(src, k, c), ACT.Identity, bias=col(wl, WL, "bo"))
                last.then_inc(freed(("ao", k)), 1)

            def head_score_exponentials():
                used(ae, ("attT",))
                A.activation(aeT[0:32, :], asT[0:32, :], ACT.Exp, scale=SCALE1).then_inc(aexp_ready, 1)

            def copy_outputs(k):
                src = full(ae, ("aoT", k))
                A.activation(ao[:, CT * k:CT * k + CT, :].rearrange("p j d -> p (j d)"), src[:, :],
                             ACT.Copy).then_inc(freed(("aoT", k)), 1)

            ae.wait_ge(d_wa, 16)
            A.activation(gated[:, :], col(wa, WA, "gates"), ACT.Tanh).then_inc(gates_ready, 1)
            part = {"xT": copy_xT, "K": spread_keys, "K2": spread_other_keys, "round": round_keys, "V": place_values, "scores": exponentials,
                    "evacuate": evacuate, "fT": copy_fT, "logits": route_exponentials, "G": silu_gate,
                    "shared": silu_shared, "weightT": copy_weights, "hnorm": norm_last, "hT": copy_hT,
                    "head_logits_done": head_exponentials, "hotT": place_choices, "take": place_tokens,
                    "attT": head_score_exponentials, "avT": place_averages, "ao": place_outputs,
                    "aoT": copy_outputs, "finish": norm_out}
            for stage, *where in plan:
                if stage in part:
                    part[stage](*where)

        @block.gpsimd
        def _(ge):
            G = nc.gpsimd
            roots = [0]

            def inverse_deviation(slot):
                ge.wait_ge(var_ready, roots[0] + 1)
                roots[0] += 1
                part = slice(CT * slot, CT * slot + CT)
                G.tensor_tensor(rstd[:, part], var_eps[:, part], half_neg[:, part], ALU.pow).then_inc(rstd_ready, 1)

            def last_deviation(k):
                inverse_deviation(k)
                ge.wait_ge(rstd_ready, roots[0])
                tiles = slice(CT * k, CT * k + CT)
                G.tensor_tensor(offset[:, tiles], neg_mean[:, tiles], rstd[:, tiles], ALU.mult).then_inc(offset_ready, 1)

            def token_deviation(n):
                inverse_deviation(n % 2)

            def expert_deviation(c):
                inverse_deviation(2 + c % 2)

            def add_bias(n):
                if n >= NC:
                    return
                ge.wait_ge(normed, n + 1)
                ge.wait_ge(obias_ready, 1)
                part = xa[:, CT * n:CT * n + CT, :]
                G.tensor_tensor(part, part, obias[:, 0:1, :].broadcast_to([P, CT, D]), ALU.add).then_inc(bias_added, 1)

            def clear():
                G.memset(V2[:, 0, :, :, :], 0.0).then_inc(cleared, 1)
                G.memset(V2[:, 1, :, :, :], 0.0).then_inc(cleared, 1)
                G.memset(cwT[:, :], 0.0).then_inc(cleared, 1)
                G.memset(gu[:, NP, :], 0.0).then_inc(cleared, 1)
                ge.wait_ge(cleared, 4)
                G.memset(maskb[S:P, :, :, :], 0.0).then_inc(mask_ready, 1)
                ge.wait_ge(mask_ready, 1)

            def silu(c, p):
                turn = (NP + 1) * c + p
                ge.wait_ge(parts_ready, turn + 1)
                if p >= 2:
                    used(ge, ("U", c, p - 2))
                elif c >= 1:
                    used(ge, ("shared", c - 1) if p else ("U", c - 1, NP - 1))
                G.tensor_tensor(sil[:, turn % 2, :], th[:, turn % 2, :], gh[:, turn % 2, :],
                                ALU.mult).then_inc(silu_done, 1)

            def silu_shared(c):
                silu(c, NP)

            pool_steps = [1]

            def ge_step(ins):
                pool_steps[0] += 1
                ins.then_inc(pool_step, 1)
                ge.wait_ge(pool_step, pool_steps[0])

            def last_bias():
                ge.wait_ge(d_xr, 16 * NQ)
                ge.wait_ge(obias_ready, 2)
                G.tensor_tensor(xr[:, :, :], xr[:, :, :], obias[:, 1:2, :].broadcast_to([P, SP, D]),
                                ALU.add).then_inc(bias_added, 1)
                filled(ge, ("Y", NC - 1))
                G.memset(takeT, 0.0).then_inc(cleared, 1)
                G.memset(putT, 0.0).then_inc(cleared, 1)

            def head_products(k):
                if k % 4 == 3:
                    used(ge, ("qkv", k))
                    if k > 3:
                        ge.wait_ge(att_ready, 2)
                    G.tensor_tensor(*head_product(k, 1)).then_inc(prod_ready, 1)

            def head_averages():
                used(ge, ("attB",))
                products, total = weighted_values(POOL_PAIRS, 0)
                for operands in products:
                    last = G.tensor_tensor(*operands)
                ge_step(last)
                G.tensor_tensor(*total).then_inc(av_pool_ready, 1)

            def add_residual(k):
                tiles = slice(CT * k, CT * k + CT)
                ge.wait_ge(scaled, k + 1)
                G.tensor_tensor(y[:, tiles, :], y[:, tiles, :], xr[:, tiles, :], ALU.add).then_inc(out_ready, 1)

            def out_share(k):
                if k != NT // CT - 1:
                    return
                ge.wait_ge(hn_ready, NT // CT)
                G.memset(avT, 0.0).then_inc(cleared, 1)
                ge.wait_ge(d_wl, 16)
                g = gated[:, 3:4]
                ge_step(G.tensor_scalar(col(wl, WL, "ln_b"), col(wl, WL, "ln_b"), g, None, ALU.mult))
                ge_step(G.tensor_scalar(col(wl, WL, "ln_g"), col(wl, WL, "ln_g"), g, None, ALU.mult))
                G.tensor_tensor(xr[:, :, :], xr[:, :, :], col(wl, WL, "ln_b").unsqueeze(1).broadcast_to([P, SP, D]),
                                ALU.add).then_inc(out_bias, 1)

            G.memset(half_neg[:, :], -0.5).then_inc(pool_step, 1)
            ge.wait_ge(pool_step, 1)
            part = {"measure": token_deviation, "norm": add_bias, "clear": clear,
                    "O": expert_deviation, "G": silu,
                    "shared": silu_shared, "last_bias": last_bias,
                    "O1": last_deviation, "hnorm": out_share, "qkv": head_products, "attB": head_averages,
                    "back": last_deviation, "finish": add_residual}
            for stage, *where in plan:
                if stage in part:
                    part[stage](*where)


def shape_constants():
    row = np.arange(P)
    cf = np.zeros((P, CF_N), np.float32)
    cb = np.zeros((P, CBF_N), np.float32)

    def f(name):
        a, w = CF[name]
        return cf[:, a:a + w]

    def b(name):
        a, w = CBF[name]
        return cb[:, a:a + w]
    f("ident")[:] = np.eye(P)
    f("gmask")[:] = (row[:, None] // 32) == np.arange(NG)
    f("imask")[:] = (row[:, None] // DH % NI) == np.arange(NI)
    gp, i = row // 4 % 2, row % 4
    f("cmask")[:] = (i[:, None] // 2 == np.arange(4) // 2) & (gp[:, None] == np.arange(4) % 2)
    r = np.arange(64)
    f("ones_v")[:] = (r[None] % 32 // DH) == 2 * (r[None] // 32) + row[:, None] // 64
    f("first8")[:] = NE - np.arange(CT * NE) % NE
    f("sequence")[:] = np.arange(B)
    b("ident")[:] = np.eye(P)
    seq = row // 8 % CB
    pick = (seq[:, None, None] == np.arange(CB)[None, :, None]) & (i[:, None, None] % 2 == row[None, None, :] // 64)
    b("pick")[:] = pick.reshape(P, -1)
    ex = (row[:, None] < 3 * NE) & (row[:, None] % NE == np.arange(NE * F)[None] // F)
    b("experts")[:] = ex
    b("twice")[:] = row[:, None] == row[None] % S
    return cf, cb


def kernel(**inputs):
    import ml_dtypes
    import concourse.bacc as bacc
    from concourse.bass_utils import run_bass_kernel_spmd

    a = {k: np.asarray(v) for k, v in inputs.items()}

    def pack(table, n, parts):
        t = np.zeros((P, n), np.float32)
        for name, v in parts.items():
            first, w = table[name]
            t[:v.shape[0], first:first + w] = v.reshape(v.shape[0], w)
        return t

    def diagonal(w):
        t = np.zeros((P, P), np.float32)
        for h in range(NG * NI):
            t[DH * h:DH * h + DH, DH * h:DH * h + DH] = w[h].T
        return t

    def rows(v):
        return np.broadcast_to(v, (P, v.size))

    cf, cb = shape_constants()
    w_a = pack(WA, WA_N, {
        "wq0": diagonal(a["L0_xattn_wq"]), "wk0": diagonal(a["L0_xattn_wk"]), "wv0": diagonal(a["L0_xattn_wv"]),
        "wo0": a["L0_xattn_wo"].T, "bo0": rows(a["L0_xattn_bo"]), "bq0": a["L0_xattn_bq"].reshape(P, 1),
        "bk0": a["L0_xattn_bk"].reshape(P, 1), "bv0": a["L0_xattn_bv"].reshape(P, 1),
        "gates": rows(np.stack([a["g_xattn"][0], a["g_ffn"][0], a["g_xattn"][1], a["g_ffn"][1]])),
        "gate_w": a["L0_ffn_gate_w"].T})
    w_b = pack(WB, WB_N, {
        "wq1": a["L1_xattn_W0"].T, "wk1": a["L1_xattn_W1"].T, "wv1": a["L1_xattn_W2"].T, "wo1": a["L1_xattn_W3"].T,
        "bo1": rows(a["L1_xattn_b3"]), "bq1": a["L1_xattn_b0"].reshape(P, 1),
        "bk1": a["L1_xattn_b1"].reshape(P, 1), "bv1": a["L1_xattn_b2"].reshape(P, 1)})
    w_f = pack(WF, WF_N, {
        "wg": a["L0_ffn_wg"].reshape(NE * F, D).T, "wu": a["L0_ffn_wu"].reshape(NE * F, D).T,
        "shared": np.concatenate([a["L0_ffn_sg"], a["L0_ffn_su"]], 0).T,
        "wd": a["L0_ffn_wd"].transpose(0, 2, 1).reshape(NP, 2 * F, D).transpose(1, 0, 2).reshape(P, -1),
        "sd": a["L0_ffn_sd"].T})
    wo = a["L1_ffn_Wo"].transpose(1, 0, 2).reshape(E1, -1)
    bqkv = np.concatenate([a["L1_ffn_bq"], a["L1_ffn_bkv"]], -1).reshape(H1 // 2, 2, 3 * E1)
    w_l = pack(WL, WL_N, {
        "Wg": a["L1_ffn_Wg"], "bo": a["L1_ffn_bo"].reshape(P, 1), "ln_g": rows(a["L1_ffn_ln_g"]),
        "ln_b": rows(a["L1_ffn_ln_b"]), "Wo": np.concatenate([wo, wo], 0),
        "Wqkv": np.concatenate([a["L1_ffn_Wq"], a["L1_ffn_Wkv"]], -1).transpose(1, 0, 2).reshape(D, -1),
        "bqkv": np.concatenate([np.broadcast_to(bqkv[:, k].reshape(1, -1), (S, H1 // 2 * 3 * E1)) for k in range(2)], 0)})
    arrays = {
        "x": np.ascontiguousarray(a["x"]),
        "ctxT": np.ascontiguousarray(a["ctx_1024"].reshape(B * S, D).T),
        "maskT": np.ascontiguousarray(a["mask_BxSxS2_if1"].transpose(1, 0, 2).reshape(S, B * S)),
        "const_f": cf, "const_b": cb.astype(ml_dtypes.bfloat16),
        "w_a": w_a, "w_b": w_b, "w_f": w_f, "w_l": w_l}
    nc = bacc.Bacc("TRN2", target_bir_lowering=False, num_devices=1)
    args = [nc.dram_tensor(f"in_{k}", v.shape, mybir.dt.from_np(v.dtype), kind="ExternalInput").ap()
            for k, v in arrays.items()]
    args.append(nc.dram_tensor("out", (B, S, D), F32, kind="ExternalOutput").ap())
    two_layers(nc, *args)
    r = run_bass_kernel_spmd(nc, [{f"in_{k}": v for k, v in arrays.items()}], core_ids=[0])
    return r.results[0]["out"]
```

```python
from contextlib import ExitStack

import numpy as np
import concourse.bass as bass
from concourse import mybir

ALU = mybir.AluOpType
ACT = mybir.ActivationFunctionType
AX = mybir.AxisListType
F32 = mybir.dt.float32
BF16 = mybir.dt.bfloat16
I32 = mybir.dt.int32

P = 128
B, S, D = 32, 64, 128
NG, NI, DH = 4, 4, 8
NT = B * S // P
CB = 8
CW = CB * S
CT = CW // P
LAST = NT // CT - 1
VECTOR_PAIRS = (slice(0, 4), slice(4, 6))
POOL_PAIRS = slice(6, 8)
POOL_FEATURES = (1, 3, 5)
SPLIT = 6
NC = B // CB
NA = 2 * NC
NE, F = 8, 64
NP = NE // 2
H1, E1, CAP = 16, 64, 2
NQ, SP = 4, S // 4
SCALE = float(DH) ** -0.5
SCALE1 = float(E1) ** -0.5
BIG = -(2.0 ** 100)
EPS = 1e-5


def columns(widths):
    at, out = 0, {}
    for name, w in widths:
        out[name] = (at, w)
        at += w
    return out, at


CF, CF_N = columns([("ident", P), ("gmask", NG), ("imask", NI), ("cmask", 4), ("ones_v", 64),
                    ("first8", CT * NE), ("sequence", B)])
CBF, CBF_N = columns([("ident", P), ("pick", CB * P), ("experts", NP * P), ("twice", P)])
WA, WA_N = columns([("wq0", P), ("wk0", P), ("wv0", P), ("wo0", P), ("bo0", P), ("bq0", 1), ("bk0", 1),
                    ("bv0", 1), ("gates", 4), ("gate_w", NE)])
WB, WB_N = columns([("wq1", P), ("wk1", P), ("wv1", P), ("wo1", P), ("bo1", P), ("bq1", 1), ("bk1", 1),
                    ("bv1", 1)])
WF, WF_N = columns([("wg", NE * F), ("wu", NE * F), ("shared", 2 * F), ("wd", NP * D), ("sd", D)])
WL, WL_N = columns([("Wg", H1), ("bo", 1), ("ln_g", D), ("ln_b", D), ("Wo", H1 * D),
                    ("Wqkv", H1 * 3 * E1), ("bqkv", H1 // 2 * 3 * E1)])


def schedule():
    plan = [("measure", 0), ("norm", 0), ("bias", 0), ("clear",), ("xT", 0), ("K", 0), ("Q", 0), ("K2", 0), ("Q2", 0),
             ("round", 0, 1), ("V", 0, 0), ("V", 0, 1)]
    plan += [("low", 0, b) for b in range(CB)]
    plan += [("split", 0), ("maxT", 0), ("measure", 1), ("norm", 1)]
    for n in range(NA):
        after = [[] for _ in range(CB)]
        c = n - 1
        here, rest = 0 <= c < NC, 0 <= c - 1 < NC
        if c >= 0:
            after[0] += [("evacuate", c), ("divide", c)]
        if n + 1 < NA:
            after[0] += [("xT", n + 1)]
        if rest:
            after[0] += [("U", c - 1, 1), ("G", c - 1, 2)]
        if n + 1 < NA:
            after[0] += [("K", n + 1)]
        if rest:
            after[1] += [("weightT", c - 1), ("U", c - 1, 2), ("G", c - 1, 3)]
        if n + 1 < NA:
            after[1] += [("Q", n + 1)]
            after[2] += [("V", n + 1, 0)]
        if rest:
            after[2] += [("U", c - 1, 3), ("shared", c - 1)]
        if n + 1 < NA:
            after[3] += [("round", n + 1, 1)]
        if rest:
            after[3] += [("gated", c - 1)]
        if n + 1 < NA:
            after[3] += [("V", n + 1, 1)]
            for b in range(4):
                after[3 + b] += [("low", n + 1, 2 * b + 1)]
        if here:
            after[3] += [("O", c)]
        if here:
            after[4] += [("fnorm", c)]
        if rest:
            after[4] += [("W", c - 1, p) for p in range(3)]
        if here:
            after[5] += [("fT", c)]
        if rest:
            after[5] += [("W", c - 1, 3)]
        if n + 1 < NA:
            after[6] += [("split", n + 1)]
        if here:
            after[6] += [("logits", c), ("G", c, 0), ("route", c)]
        if rest:
            after[6] += [("Y", c - 1)]
        if n + 2 < NA:
            after[6] += [("measure", n + 2)]
        if n + 1 < NA:
            after[7] += [("maxT", n + 1)]
        if here:
            after[7] += [("U", c, 0), ("G", c, 1)]
        if n + 2 < NA:
            after[7] += [("norm", n + 2)]
        if n == 0:
            after[5] += [("mask",)]
        if n == 1:
            after[5] += [("bias", 1)]
        if n == NA - 1:
            after[3] += [("last_bias",)]
        for b in range(CB):
            plan += [("scores", n, b)]
            if b == 1 and n + 1 < NA:
                plan += [("K2", n + 1)]
            if b == 2 and n + 1 < NA:
                plan += [("Q2", n + 1)]
            if 3 <= b < 7 and n + 1 < NA:
                plan += [("low", n + 1, 2 * (b - 3))]
            if b >= 1:
                plan += [("values", n, b - 1)]
            plan += after[b]
            if n == NA - 1 and b == SPLIT:
                plan += [("evacuate", n, 0), ("divide", n, 0)]
        plan += [("values", n, CB - 1)]
    plan += [("evacuate", NA - 1, 1), ("divide", NA - 1, 1)]
    last = range(NT // CT)
    plan += [("stream", k) for k in last[:-1]] + [("O1", k) for k in last[:-1]]
    plan += [("stream", LAST), ("O1", LAST)] + [("keep", k) for k in last]
    plan += [("hnorm", 0)]
    for k in last:
        if k + 1 < len(last):
            plan += [("hnorm", k + 1)]
        plan += [("hT", k)]
        if k >= 1:
            plan += [("head_logits", k - 1)]
        if k == len(last) - 1:
            plan += [("probs", 0), ("probT", 0), ("head_logits", k), ("choose", 0)]
    plan += [("probs", 1), ("probT", 1), ("choose", 1), ("hotT",)]
    plan += [("take", k) for k in last]
    plan += [("qkv", k) for k in range(H1 // 2)]
    plan += [("residual", 0), ("residual", 1), ("attT",), ("attB",), ("residual", 2), ("residual", 3)]
    plan += [("avT", k) for k in range(2)]
    plan += [("ao", k) for k in last]
    plan += [("aoT", k) for k in last]
    plan += [("back", 0), ("back", 1)]
    for k in last:
        if k + 2 < len(last):
            plan += [("back", k + 2)]
        plan += [("finish", k)]
    return plan


def turns(plan):
    held, place, k = [0] * 8, {}, 0
    last_block = plan.index(("evacuate", NA - 1, 1))
    for at, (stage, *where) in enumerate(plan):
        if stage in GENERAL:
            if stage == "O1" and where[0] == 0:
                k = 0
            if stage == "back":
                bank = 4 + where[0]
            elif stage == "hT":
                bank = (4, 6)[where[0] % 2]
            else:
                bank = k % 3 if at < last_block else (0, 1, 3, 2)[k % 4]
                k += 1
            place[(stage, *where)] = (bank, held[bank])
            held[bank] += 1
    return place


GENERAL = {"bias", "xT", "Q", "K", "V", "maxT", "O", "fT", "logits", "G", "U", "shared", "weightT", "W", "Y",
           "O1", "hT", "probT", "hotT", "take", "qkv", "attT", "attB", "avT", "ao", "aoT", "back"}


def two_layers(nc, x, ctxT, maskT, const_f, const_b, w_a, w_b, w_f, w_l, out):
    plan = schedule()
    place = turns(plan)
    stack = ExitStack()
    with stack:
        def sb(name, shape, dt=F32):
            return stack.enter_context(nc.sbuf_tensor(name, shape, dt))

        def bank(name):
            return stack.enter_context(nc.psum_tensor(name, [P, 512], F32))

        def sem(name):
            return stack.enter_context(nc.semaphore(name))

        cf = sb("cf", [P, CF_N])
        cb = sb("cb", [P, CBF_N], BF16)
        wa = sb("wa", [P, WA_N])
        wb = sb("wb", [P, WB_N])
        wf = sb("wf", [P, WF_N])
        wl = sb("wl", [P, WL_N])
        xa = sb("xa", [P, NT, D])
        xn = sb("xn", [P, CT, D])
        fn = sb("fn", [P, CT, D])
        stats = sb("stats", [P, 16, 6])
        mean_var = sb("mean_var", [P, 16, 2])
        var_eps = sb("var_eps", [P, 16])
        rstd = sb("rstd", [P, 16])
        neg_mean = sb("neg_mean", [P, 16])
        offset = sb("offset", [P, 16])
        half_neg = sb("half_neg", [P, 16])
        xT = sb("xT", [P, 2, CW])
        fT = sb("fT", [P, CW])
        cT = sb("cT", [P, B * S])
        Qg = sb("Qg", [P, 2, CB, NG, S])
        Ki = sb("Ki", [P, 2, CB, NI, S])
        Qb = sb("Qb", [P, 2, CB, NG, S], BF16)
        Kb = sb("Kb", [P, 2, CB, NI, S], BF16)
        V2 = sb("V2", [P, 2, CB, 2, P])
        pT = sb("pT", [P, 3, 512])
        nmax = sb("nmax", [P, 2, CB * 8])
        nmax2 = sb("nmax2", [P, 2, CB * 8], BF16)
        shift = sb("shift", [P, 2, 512], BF16)
        den = sb("den", [P, 512])
        raw = sb("raw", [P, 512])
        oT = sb("oT", [P, B * S])
        maskb = sb("maskb", [P, B, 2, S], BF16)
        gated = sb("gated", [P, 4])
        bqg = sb("bqg", [P, 2, NG])
        bki = sb("bki", [P, 2, NI])
        obias = sb("obias", [P, 2, D])
        lg = sb("lg", [P, CT, NE])
        lw = sb("lw", [P, CT, NE])
        hot1 = sb("hot1", [P, CT, NE])
        hot2 = sb("hot2", [P, CT, NE])
        pr = sb("pr", [P, CT, NE])
        r4 = sb("r4", [P, 4, CT])
        cw3 = sb("cw3", [P, CT, 3, NE], BF16)
        cwT = sb("cwT", [P, CW], BF16)
        halves = sb("halves", [P, 2, 2, CW])
        th, gh = halves[:, 0, :, :], halves[:, 1, :, :]
        sil = sb("sil", [P, 2, CW])
        top8 = sb("top8", [P, 8, 8])
        top8_at = sb("top8_at", [P, 8, 8], mybir.dt.uint32)
        gu = sb("gu", [P, NP + 1, CW])
        hid = sb("hid", [P, NP, CW])
        xr = halves[:, :, :, :].rearrange("p k a w -> p (k a w)").rearrange("p (s d) -> p s d", s=SP)
        hn = sb("hn", [P, SP, D])
        mask = hn[0:S, :, :].bitcast(I32).rearrange("p s d -> p (s d)")
        at = Qg[:, :, :, :, :].rearrange("p a b g s -> p (a b g s)")
        hT = at[:, 0:2048].rearrange("p (h c s) -> p h c s", h=H1, c=CAP)
        avT = at[:, 2048:4096].rearrange("p (h c s) -> p h c s", h=H1, c=CAP)
        at = Ki[:, :, :, :, :].rearrange("p a b g s -> p (a b g s)")
        qkv = at[:, 0:3072].rearrange("p (h c e) -> p h c e", h=8, c=CAP)
        av = at[:, 3072:4096].rearrange("p (h c e) -> p h c e", h=8, c=CAP)
        at = V2[:, :, :, :, :].rearrange("p a b g s -> p (a b g s)")
        aoT = at[:, 0:2048].rearrange("p (s q r) -> p s q r", s=SP, q=NQ)
        ao = at[:, 2048:4096].rearrange("p (s d) -> p s d", s=SP)
        y = oT[:, :].rearrange("p (s d) -> p s d", s=SP)
        at = gu[:, :, :].rearrange("p a b -> p (a b)")
        takeT = at[:, 0:2048].rearrange("p (s q r) -> p s q r", s=SP, q=NQ)
        prod = at[:, 0:2048]
        at = hid[:, :, :].rearrange("p a b -> p (a b)")
        putT = at[:, 0:2048].rearrange("p (s q t) -> p s q t", s=SP, q=NQ)
        xnT = cT[:, :].rearrange("p (s r) -> p s r", s=SP)
        at = fT[:, :]
        sm = at[:, 0:256].rearrange("p (s h) -> p s h", s=SP)
        smr = at[:, 256:320].rearrange("p (k s) -> p k s", k=4)
        at = xT[:, :, :].rearrange("p a b -> p (a b)")
        pt = at[:, 0:256].rearrange("p (a q t) -> p a q t", a=2, q=NQ)
        o1 = at[:, 512:768].rearrange("p (a q t) -> p a q t", a=2, q=NQ)
        o2 = at[:, 768:1024].rearrange("p (a q t) -> p a q t", a=2, q=NQ)
        at = xn[:, :, :].rearrange("p a b -> p (a b)")
        tm = at[:, 0:64].rearrange("p (k a q) -> p k a q", k=8, a=2)
        hot = at[:, 64:320].rearrange("p (a q t) -> p a q t", a=2, q=NQ)
        att = at[:, 320:352]
        attn = at[:, 352:384]
        at = fn[:, :, :].rearrange("p a b -> p (a b)")
        asT = at[:, 0:128]
        aeT = at[:, 128:256]
        ar = at[:, 256:272]

        bS = bank("scores")
        bT = [bank(f"scoresT{i}") for i in range(2)]
        bC = bank("context")
        bD = bank("denominators")
        bG = [bank(f"general{i}") for i in range(3)] + bT + [bC, bD, bS]

        d_cf, d_cb, d_wa, d_wb, d_wf, d_wl, d_mask = (sem(f"loaded_{k}") for k in
                                                      ("cf", "cb", "wa", "wb", "wf", "wl", "mask"))
        d_x = [sem(f"loaded_x{c}") for c in range(NC)]
        d_c = [sem(f"loaded_ctx{c}") for c in range(NC)]
        spilled, d_xr, stored = sem("spilled"), sem("loaded_xr"), sem("stored")
        general_full = [sem(f"general_full{i}") for i in range(8)]
        general_free = [sem(f"general_free{i}") for i in range(8)]
        vector_step, pool_step, tanh_done = sem("vector_step"), sem("pool_step"), sem("tanh_done")
        gates_ready, biases_ready, obias_ready = sem("gates_ready"), sem("biases_ready"), sem("obias_ready")
        mask_ready, cleared, wo_gated = sem("mask_ready"), sem("cleared"), sem("wo_gated")
        normed, fnormed, hn_ready = sem("normed"), sem("fnormed"), sem("hn_ready")
        var_ready, rstd_ready, offset_ready = sem("var_ready"), sem("rstd_ready"), sem("offset_ready")
        low_q, low_k, scores_done, max_done = sem("low_q"), sem("low_k"), sem("scores_done"), sem("max_done")
        nmax_ready, scoresT_done, exp_done = sem("nmax_ready"), sem("scoresT_done"), sem("exp_done")
        pv_done, context_out, den_out = sem("pv_done"), sem("context_out"), sem("den_out")
        context_ready, bias_added = sem("context_ready"), sem("bias_added")
        route_exp, cw_ready, parts_ready = sem("route_exp"), sem("cw_ready"), sem("parts_ready")
        silu_done = sem("silu_done")
        gate_logits, gate_exp, tl_exp = sem("gate_logits"), sem("gate_exp"), sem("head_probs_exp")
        probs_ready, hot_ready = sem("probs_ready"), sem("hot_ready")
        take_v, take_a, put_ready = sem("take_placed_v"), sem("take_placed_a"), sem("put_ready")
        biased, prod_ready, att_ready = sem("features_biased"), sem("prod_ready"), sem("att_ready")
        aexp_ready, attn_ready = sem("aexp_ready"), sem("attn_ready")
        av_ready, av_pool_ready = sem("av_ready"), sem("av_pool_ready")
        out_bias, scaled, centred = sem("out_bias"), sem("scaled"), sem("centred")
        out_ready, last_out_ready = sem("out_ready"), sem("last_out_ready")

        def col(tile, table, name):
            a, w = table[name]
            return tile[:, a:a + w]

        ident = col(cf, CF, "ident")
        identb = col(cb, CBF, "ident")

        spill = nc.dram_tensor("x_by_position", [B, S, D], F32).ap()
        spill_tiles = spill.rearrange("(j b) s d -> (b s) j d", b=2)

        def sequences(n, part):
            assert (part is not None) == (n == NA - 1)
            return {None: (0, CB), 0: (0, SPLIT), 1: (SPLIT, CB)}[part]

        def feature_bias(k):
            bias = col(wl, WL, "bqkv").rearrange("p (h e) -> p h e", e=3 * E1)
            return bias[:, k:k + 1, :].broadcast_to([P, CAP, 3 * E1])

        def head_product(k, j):
            hs = slice(k - 3, k + 1)
            return (prod[:, 512 * j:512 * j + 512].rearrange("p (h i e) -> p h i e", h=4, i=2), qkv[:, hs, :, 0:E1],
                    qkv[:, hs, j:j + 1, E1:2 * E1].broadcast_to([P, 4, 2, E1]), ALU.mult)

        def weighted_values(hs, at):
            an = attn.rearrange("p (h i j) -> p h i j", i=2, j=2)
            n = hs.stop - hs.start
            terms = [prod[:, at + 128 * n * j:at + 128 * n * (j + 1)].rearrange("p (h i e) -> p h i e", h=n, i=2)
                     for j in range(2)]
            products = [(terms[j], qkv[:, hs, j:j + 1, 2 * E1:3 * E1].broadcast_to([P, n, 2, E1]),
                         an[:, hs, :, j].unsqueeze(3).broadcast_to([P, n, 2, E1]), ALU.mult) for j in range(2)]
            return products, (av[:, hs, :, :], terms[0], terms[1], ALU.add)

        def average_part(bank, k, i):
            src = bank[:, :].rearrange("p (j h s) -> p (j h) s", j=4, h=2)
            return avT[64 * i:64 * i + 64, 8 * k:8 * k + 8, i, :], src[64 * i:64 * i + 64, :, :]

        def output_part(bank, k, c):
            src = bank[:, :].rearrange("p (h c q s) -> p c h q s", h=CT, c=CAP, q=NQ)[:, c, :, :, :]
            return aoT[:, :, :, H1 * c + CT * k:H1 * c + CT * k + CT].rearrange("p s q h -> p h q s"), src

        def low_bank(n, b):
            return bC if n == 0 and b % 2 else bS

        def sum_banks(n, b):
            return (bS, bG[2]) if n == NA - 1 and b >= SPLIT else (bC, bD)

        def by_position(ap):
            return ap.rearrange("b (q s) d -> q b s d", q=NQ)

        def filled(engine, job):
            bank, before = place[job]
            engine.wait_ge(general_full[bank], before + 1)

        def full(engine, job):
            filled(engine, job)
            return bG[place[job][0]]

        def freed(job):
            return general_free[place[job][0]]

        def used(engine, job):
            bank, before = place[job]
            engine.wait_ge(general_free[bank], before + 1)

        block = stack.enter_context(nc.Block())

        @block.sync
        def _(sp):
            x_tiles = x.rearrange("(j b) s d -> (b s) j d", b=2)
            sp.dma_start(xa[:, 0:CT, :], x_tiles[:, 0:CT, :]).then_inc(d_x[0], 16)
            sp.dma_start(cf[:, :], const_f).then_inc(d_cf, 16)
            sp.dma_start(wa[:, :], w_a).then_inc(d_wa, 16)
            for c in range(NC):
                if c:
                    sp.dma_start(xa[:, CT * c:CT * c + CT, :], x_tiles[:, CT * c:CT * c + CT, :]).then_inc(d_x[c], 16)
                sp.dma_start(cT[:, CW * c:CW * c + CW], ctxT[:, CW * c:CW * c + CW]).then_inc(d_c[c], 16)
                if c == 0:
                    sp.dma_start(cb[:, :], const_b).then_inc(d_cb, 16)
            sp.dma_start(wf[:, :], w_f).then_inc(d_wf, 16)
            sp.dma_start(mask, maskT).then_inc(d_mask, 16)
            sp.dma_start(wb[:, :], w_b).then_inc(d_wb, 16)
            sp.dma_start(wl[:, :], w_l).then_inc(d_wl, 16)
            for c in range(NC):
                used(sp, ("Y", c))
                sp.dma_start(spill_tiles[:, CT * c:CT * c + CT, :], xa[:, CT * c:CT * c + CT, :]).then_inc(spilled, 16)
            sp.wait_ge(spilled, 16 * NC)
            for q in range(NQ):
                sp.dma_start(xr[32 * q:32 * q + 32, :, :], by_position(spill)[q]).then_inc(d_xr, 16)
            for k in range(NT // CT):
                if k == LAST:
                    sp.wait_ge(last_out_ready, 1)
                else:
                    sp.wait_ge(out_ready, k + 1)
                sp.dma_start(by_position(out)[:, :, CT * k:CT * k + CT, :],
                             y[:, CT * k:CT * k + CT, :]).then_inc(stored, 16)
            sp.wait_ge(stored, 16 * (NT // CT))

        @block.tensor
        def _(pe):
            def take(job):
                bank, before = place[job]
                if before:
                    pe.wait_ge(general_free[bank], before)
                elif bG[bank] in bT:
                    pe.wait_ge(exp_done, CB * NA)
                return bG[bank], general_full[bank]

            def out_bias_product(l):
                w, table = ((wa, WA), (wb, WB))[l]
                pe.wait_ge(d_wb if l else d_wa, 16)
                dst, done = take(("bias", l))
                bv = col(w, table, f"bv{l}")
                nc.tensor.matmul(dst[:, 0:D], bv.broadcast_to([P, P]), col(w, table, f"wo{l}"),
                                 start=True, stop=True).then_inc(done, 1)

            def transpose_tiles(job, tiles):
                dst, done = take(job)
                for j in range(CT):
                    last = nc.tensor.transpose(dst[:, P * j:P * j + P], tiles[:, j, :], ident)
                last.then_inc(done, 1)

            def queries(n):
                l = n // NC
                w, table = ((wa, WA), (wb, WB))[l]
                dst, done = take(("Q", n))
                used(pe, ("xT", n))
                nc.tensor.matmul(dst[:, :], col(w, table, f"wq{l}"), xT[:, n % 2, :],
                                 start=True, stop=True).then_inc(done, 1)

            def keys(n):
                l, c = divmod(n, NC)
                w, table = ((wa, WA), (wb, WB))[l]
                if l == 0:
                    pe.wait_ge(d_c[c], 16)
                dst, done = take(("K", n))
                nc.tensor.matmul(dst[:, :], col(w, table, f"wk{l}"), cT[:, CW * c:CW * c + CW],
                                 start=True, stop=True).then_inc(done, 1)

            def value_rows(n, half):
                l, c = divmod(n, NC)
                w, table = ((wa, WA), (wb, WB))[l]
                dst, done = take(("V", n, half))
                for b in range(4):
                    first = CW * c + S * (4 * half + b)
                    for i2 in range(2):
                        last = nc.tensor.matmul(dst[S * i2:S * i2 + S, P * b:P * b + P], cT[:, first:first + S],
                                                col(w, table, f"wv{l}"), start=True, stop=True)
                last.then_inc(done, 1)

            def low_scores(n, b):
                k = CB * n + b
                if k == 0:
                    pe.wait_ge(d_cb, 16)
                if b == 0:
                    pe.wait_ge(low_q, 2 * n + 1)
                    pe.wait_ge(low_k, 2 * n + 1)
                elif b == CB // 2:
                    pe.wait_ge(low_q, 2 * n + 2)
                    pe.wait_ge(low_k, 2 * n + 2)
                in_turns = 1 if n else 2
                if k >= in_turns:
                    pe.wait_ge(max_done, k - in_turns + 1)
                dst = low_bank(n, b)
                masked = n >= NC
                if masked:
                    if n == NC and b == 0:
                        pe.wait_ge(mask_ready, 3)
                    seq = CB * (n - NC) + b
                    nc.tensor.matmul(dst[:, :], col(cb, CBF, "twice"),
                                     maskb[:, seq, 0:1, :].broadcast_to([P, 8, S]),
                                     start=True, stop=False, skip_group_check=True)
                for gp in range(2):
                    last = nc.tensor.matmul(dst[:, 256 * gp:256 * gp + 256],
                                            Qb[:, n % 2, b, 2 * gp:2 * gp + 2, :].rearrange("p g s -> p (g s)"),
                                            Kb[:, n % 2, b, :, :].rearrange("p i t -> p (i t)"),
                                            start=not masked, stop=not masked or gp == 1,
                                            skip_group_check=masked)
                last.then_inc(scores_done, 1)

            def transpose_maxima(n):
                dst, done = take(("maxT", n))
                pe.wait_ge(nmax_ready, n + 1)
                nc.tensor.transpose(dst[:, :].bitcast(BF16)[:, 0:P],
                                    nmax2[:, :, :].rearrange("p a b -> p (a b)"), identb).then_inc(done, 1)

            def scores_transposed(n, b):
                k = CB * n + b
                if b == 0:
                    used(pe, ("maxT", n))
                if k >= 2:
                    pe.wait_ge(exp_done, k - 1)
                dst = bT[k % 2]
                masked = n >= NC
                pick = col(cb, CBF, "pick")[:, P * b:P * b + P]
                if masked:
                    seq = CB * (n - NC) + b
                    nc.tensor.matmul(dst[:, :], maskb[:, seq, :, :].rearrange("p a t -> p (a t)"),
                                     identb[:, 0:S].unsqueeze(1).broadcast_to([P, 8, S]),
                                     start=True, stop=False, skip_group_check=True)
                else:
                    nc.tensor.matmul(dst[:, :], pick, shift[:, n % 2, :], start=True, stop=False,
                                     skip_group_check=True)
                for ip in range(2):
                    last = nc.tensor.matmul(dst[:, 256 * ip:256 * ip + 256],
                                            Ki[:, n % 2, b, 2 * ip:2 * ip + 2, :].rearrange("p i t -> p (i t)"),
                                            Qg[:, n % 2, b, :, :].rearrange("p g s -> p (g s)"),
                                            start=False, stop=not masked and ip == 1, skip_group_check=True)
                if masked:
                    last = nc.tensor.matmul(dst[:, :], pick, shift[:, n % 2, :], start=False, stop=True,
                                            skip_group_check=True)
                last.then_inc(scoresT_done, 1)

            def values(n, b):
                k = CB * n + b
                if b == 0:
                    used(pe, ("V", n, 1))
                    if n >= 1:
                        pe.wait_ge(context_out, n)
                        pe.wait_ge(den_out, n)
                pe.wait_ge(exp_done, k + 1)
                ones = col(cf, CF, "ones_v").rearrange("p (a r) -> p a r", a=2)
                context, sums = sum_banks(n, b)
                for dst, w in ((context, None), (sums, ones)):
                    for ip in range(2):
                        for g in range(NG):
                            lhs = V2[:, n % 2, b, ip, 32 * g:32 * g + 32] if w is None else w[:, ip, :]
                            at = 256 * ip + S * g
                            last = nc.tensor.matmul(dst[32 * g:32 * g + 32, S * b:S * b + S], lhs,
                                                    pT[:, k % 3, at:at + S],
                                                    start=ip == 0, stop=ip == 1)
                last.then_inc(pv_done, 1)

            def project_out(n):
                dst, done = take(("O", n))
                pe.wait_ge(context_ready, n + 1)
                for j in range(CT):
                    first = CW * n + P * j
                    last = nc.tensor.matmul(dst[:, P * j:P * j + P], oT[:, first:first + P],
                                            col(wa, WA, "wo0"), start=True, stop=True)
                last.then_inc(done, 1)

            def expert_logits(c):
                if c == 0:
                    pe.wait_ge(d_wf, 16)
                dst, done = take(("logits", c))
                used(pe, ("fT", c))
                for j in range(CT):
                    last = nc.tensor.matmul(dst[:, NE * j:NE * j + NE], fT[:, P * j:P * j + P],
                                            col(wa, WA, "gate_w"), start=True, stop=True)
                last.then_inc(done, 1)

            def expert_in(job, w):
                def product(c, p):
                    dst, done = take((job, c, p))
                    nc.tensor.matmul(dst[:, :], col(wf, WF, w)[:, P * p:P * p + P], fT[:, :],
                                     start=True, stop=True).then_inc(done, 1)
                return product

            def shared_in(c):
                dst, done = take(("shared", c))
                nc.tensor.matmul(dst[:, :], col(wf, WF, "shared"), fT[:, :], start=True, stop=True).then_inc(done, 1)

            def weights_transposed(c):
                dst, done = take(("weightT", c))
                pe.wait_ge(cw_ready, c + 1)
                for j in range(CT):
                    last = nc.tensor.transpose(dst[0:3 * NE, :].bitcast(BF16)[:, P * j:P * j + P],
                                               cw3[:, j, :, :].rearrange("p a b -> p (a b)"), identb)
                last.then_inc(done, 1)

            def weights_spread(c, p):
                dst, done = take(("W", c, p))
                used(pe, ("weightT", c))
                nc.tensor.matmul(dst[:, :], col(cb, CBF, "experts")[:, P * p:P * p + P], cwT[:, :],
                                 start=True, stop=True).then_inc(done, 1)

            def expert_out(c):
                dst, done = take(("Y", c))
                used(pe, ("W", c, NP - 1))
                if c == 0:
                    pe.wait_ge(cleared, 4)
                for j in range(CT):
                    for p in range(NP + 1):
                        if p < NP:
                            lhs, rhs = hid[:, p, P * j:P * j + P], col(wf, WF, "wd")[:, D * p:D * p + D]
                        else:
                            lhs, rhs = gu[:, NP, P * j:P * j + P], col(wf, WF, "sd")
                        last = nc.tensor.matmul(dst[:, P * j:P * j + P], lhs, rhs, start=p == 0, stop=p == NP)
                last.then_inc(done, 1)

            def residual_stream(k):
                if k == 0:
                    pe.wait_ge(bias_added, NC + 1)
                dst, _ = take(("O1", k))
                nc.tensor.matmul(dst[:, :], ident, xr[:, CT * k:CT * k + CT, :].rearrange("p j d -> p (j d)"),
                                 start=True, stop=False, skip_group_check=True)

            def out_by_position(k):
                bank, _ = place[("O1", k)]
                dst, done = bG[bank], general_full[bank]
                if k == 0:
                    pe.wait_ge(wo_gated, 1)
                    pe.wait_ge(context_ready, NA + 1)
                for j in range(CT):
                    last = nc.tensor.matmul(dst[:, P * j:P * j + P], oT[:, P * (CT * k + j):P * (CT * k + j) + P],
                                            col(wb, WB, "wo1"), start=False, stop=True, skip_group_check=True)
                last.then_inc(done, 1)

            def head_logits(k):
                used(pe, ("hT", k))
                if k == 0:
                    pe.wait_ge(d_wl, 16)
                for j in range(CT * k, CT * k + CT):
                    nc.tensor.matmul((bS, bC)[k // 2][:, H1 * j:H1 * j + H1], xnT[:, j, :], col(wl, WL, "Wg"),
                                     start=True, stop=True).then_inc(gate_logits, 1)

            def probabilities_transposed(a):
                dst, done = take(("probT", a))
                pe.wait_ge(probs_ready, a + 1)
                nc.tensor.transpose(dst[:, 0:P], sm[:, 8 * a:8 * a + 8, :].rearrange("p s h -> p (s h)"),
                                    ident).then_inc(done, 1)

            def choices_transposed():
                dst, done = take(("hotT",))
                pe.wait_ge(hot_ready, 2)
                for c in range(CAP):
                    for a in range(2):
                        src = (o1 if c == 0 else o2)[:, a, :, :].rearrange("p q t -> p (q t)")
                        last = nc.tensor.transpose(dst[:, 256 * c + P * a:256 * c + P * a + P], src, ident)
                last.then_inc(done, 1)

            def take_tokens(k):
                dst, done = take(("take", k))
                if k == 0:
                    pe.wait_ge(take_v, 1)
                    pe.wait_ge(take_a, 1)
                for j in range(CT):
                    s = CT * k + j
                    last = nc.tensor.matmul(dst[:, P * j:P * j + P], hn[:, s, :],
                                            takeT[:, s, :, :].rearrange("p q r -> p (q r)"),
                                            start=True, stop=True)
                last.then_inc(done, 1)

            def head_projections(k):
                dst, done = take(("qkv", k))
                if k == 0:
                    used(pe, ("take", NT // CT - 1))
                for c in range(CAP):
                    for h2 in range(2):
                        h = 2 * k + h2
                        last = nc.tensor.matmul(dst[64 * h2:64 * h2 + 64, 192 * c:192 * c + 192],
                                                hT[:, h, c, :], col(wl, WL, "Wqkv")[:, 192 * h:192 * h + 192],
                                                start=True, stop=True)
                last.then_inc(done, 1)

            def head_scores_transposed():
                dst, done = take(("attT",))
                pe.wait_ge(att_ready, 4)
                nc.tensor.transpose(dst[0:32, 0:P], att, ident).then_inc(done, 1)

            def head_weights_back():
                dst, done = take(("attB",))
                pe.wait_ge(attn_ready, 1)
                nc.tensor.transpose(dst[:, 0:32], asT[0:32, :], ident[0:32, 0:32]).then_inc(done, 1)

            def head_values_transposed(k):
                dst, done = take(("avT", k))
                pe.wait_ge(av_ready, k + 1)
                if k:
                    pe.wait_ge(av_pool_ready, 1)
                for j in range(4):
                    last = nc.tensor.transpose(dst[:, P * j:P * j + P],
                                               av[:, 4 * k + j, :, :].rearrange("p c e -> p (c e)"), ident)
                last.then_inc(done, 1)

            def head_outputs(k):
                dst, done = take(("ao", k))
                if k % 2 == 0:
                    used(pe, ("avT", k // 2))
                for j in range(CT):
                    h = CT * k + j
                    last = nc.tensor.matmul(dst[:, P * j:P * j + P], col(wl, WL, "Wo")[:, D * h:D * h + D],
                                            avT[:, h, :, :].rearrange("p c s -> p (c s)"), start=True, stop=True)
                last.then_inc(done, 1)

            def head_outputs_transposed(k):
                dst, done = take(("aoT", k))
                if k == 0:
                    used(pe, ("ao", NT // CT - 2))
                    used(pe, ("ao", NT // CT - 1))
                for j in range(CT):
                    last = nc.tensor.transpose(dst[:, P * j:P * j + P],
                                               aoT[:, CT * k + j, :, :].rearrange("p q r -> p (q r)"), ident)
                last.then_inc(done, 1)

            def residual(k):
                dst, _ = take(("back", k))
                nc.tensor.matmul(dst[:, :], ident, hn[:, CT * k:CT * k + CT, :].rearrange("p j d -> p (j d)"),
                                 start=True, stop=False, skip_group_check=True)

            def put_back(k):
                bank, _ = place[("back", k)]
                dst, done = bG[bank], general_full[bank]
                used(pe, ("aoT", k))
                if k == 0:
                    pe.wait_ge(put_ready, 1)
                for j in range(CT):
                    s = CT * k + j
                    last = nc.tensor.matmul(dst[:, P * j:P * j + P],
                                            putT[:, s, :, :].rearrange("p q t -> p (q t)"), ao[:, s, :],
                                            start=False, stop=True, skip_group_check=True)
                last.then_inc(done, 1)

            def tokens_transposed(n):
                pe.wait_ge(normed, n + 1)
                if n == 0:
                    pe.wait_ge(d_cf, 16)
                transpose_tiles(("xT", n), xn)

            def expert_tokens_transposed(c):
                pe.wait_ge(fnormed, c + 1)
                transpose_tiles(("fT", c), fn)

            def last_tokens_transposed(k):
                pe.wait_ge(hn_ready, k + 1)
                transpose_tiles(("hT", k), hn[:, CT * k:CT * k + CT, :])

            part = {"bias": out_bias_product, "xT": tokens_transposed, "Q": queries, "K": keys, "V": value_rows,
                    "low": low_scores, "maxT": transpose_maxima, "scores": scores_transposed, "values": values,
                    "O": project_out, "fT": expert_tokens_transposed, "logits": expert_logits,
                    "G": expert_in("G", "wg"), "U": expert_in("U", "wu"), "shared": shared_in,
                    "weightT": weights_transposed, "W": weights_spread, "Y": expert_out,
                    "stream": residual_stream, "O1": out_by_position, "hT": last_tokens_transposed, "head_logits": head_logits,
                    "probT": probabilities_transposed, "hotT": choices_transposed, "take": take_tokens,
                    "qkv": head_projections, "attT": head_scores_transposed, "attB": head_weights_back,
                    "avT": head_values_transposed, "ao": head_outputs, "aoT": head_outputs_transposed,
                    "residual": residual, "back": put_back}
            for stage, *where in plan:
                if stage in part:
                    part[stage](*where)

        @block.vector
        def _(ve):
            V = nc.vector
            steps = [0]

            def settled(ins):
                steps[0] += 1
                ins.then_inc(vector_step, 1)
                ve.wait_ge(vector_step, steps[0])

            measures = [0]
            measured = {}

            def measure(src, slot, for_scalar=False):
                for j in range(CT):
                    last = V.bn_stats(stats[:, CT * slot + j, :], src[:, j, :])
                settled(last)
                for j in range(CT):
                    last = V.bn_aggr(mean_var[:, CT * slot + j, :], stats[:, CT * slot + j, :])
                settled(last)
                tiles = slice(CT * slot, CT * slot + CT)
                if for_scalar:
                    V.tensor_scalar(neg_mean[:, tiles], mean_var[:, tiles, 0], -1.0, None, ALU.mult)
                V.tensor_scalar(var_eps[:, tiles], mean_var[:, tiles, 1], EPS, None, ALU.add).then_inc(var_ready, 1)
                measures[0] += 1
                measured[slot] = measures[0]

            def normalise(src, dst, slot, done):
                ve.wait_ge(rstd_ready, measured[slot])
                for j in range(CT):
                    ins = V.tensor_scalar(dst[:, j, :], src[:, j, :], mean_var[:, CT * slot + j, 0:1],
                                          rstd[:, CT * slot + j:CT * slot + j + 1], ALU.subtract, ALU.mult)
                ins.then_inc(done, 1)

            def measure_tokens(n):
                c = n % NC
                if n < NC:
                    ve.wait_ge(d_x[c], 16)
                else:
                    used(ve, ("Y", c))
                measure(xa[:, CT * c:CT * c + CT, :], n % 2)

            def norm_tokens(n):
                c = n % NC
                if n >= 1:
                    filled(ve, ("xT", n - 1))
                normalise(xa[:, CT * c:CT * c + CT, :], xn, n % 2, normed)

            def norm_for_experts(c):
                if c >= 1:
                    filled(ve, ("fT", c - 1))
                normalise(xa[:, CT * c:CT * c + CT, :], fn, 2 + c % 2, fnormed)

            def spread_some(n, groups):
                l = n // NC
                ve.wait_ge(biases_ready, l + 1)
                src = full(ve, ("Q", n))
                for g in range(*groups):
                    ins = V.tensor_scalar(Qg[:, n % 2, :, g, :], src[:, :].rearrange("p (b s) -> p b s", b=CB),
                                          col(cf, CF, "gmask")[:, g:g + 1], bqg[:, l, g:g + 1], ALU.mult, ALU.add)
                return ins

            def spread_queries(n):
                spread_some(n, (0, NG // 2))

            def spread_other_queries(n):
                spread_some(n, (NG // 2, NG)).then_inc(freed(("Q", n)), 1)
                used(ve, ("Q", n))
                round_queries(n, 0)

            def round_queries(n, half):
                part = slice(CB // 2 * half, CB // 2 * (half + 1))
                V.tensor_copy(Qb[:, n % 2, part, :, :], Qg[:, n % 2, part, :, :]).then_inc(low_q, 1)

            def row_maximum(n, b):
                k = CB * n + b
                ve.wait_ge(scores_done, k + 1)
                V.tensor_reduce(nmax[:, n % 2, 8 * b:8 * b + 8], low_bank(n, b)[:, :].rearrange("p (r t) -> p r t", r=8),
                                AX.X, ALU.max, negate=True).then_inc(max_done, 1)

            def split_maxima(n):
                ve.wait_ge(max_done, CB * (n + 1))
                if n >= 1:
                    filled(ve, ("maxT", n - 1))
                settled(V.tensor_copy(nmax2[:, 0, :], nmax[:, n % 2, :]))
                V.tensor_tensor(nmax2[:, 1, :], nmax[:, n % 2, :], nmax2[:, 0, :], ALU.subtract).then_inc(nmax_ready, 1)

            def spread_shift(n):
                src = full(ve, ("maxT", n))
                if n >= 2:
                    ve.wait_ge(scoresT_done, CB * (n - 1))
                V.tensor_tensor(shift[:, n % 2, :].rearrange("p (a r) -> p a r", a=4),
                                src[:, :].bitcast(BF16)[:, 0:P].unsqueeze(1).broadcast_to([P, 4, P]),
                                col(cf, CF, "cmask").unsqueeze(2).broadcast_to([P, 4, P]),
                                ALU.mult).then_inc(freed(("maxT", n)), 1)

            def evacuate(n, part=None):
                first, end = sequences(n, part)
                ve.wait_ge(pv_done, CB * n + end)
                if n >= 1:
                    ve.wait_ge(context_ready, n)
                cols = slice(S * first, S * end)
                V.tensor_copy(raw[:, cols], sum_banks(n, first)[0][:, cols]).then_inc(context_out, 1)

            def divide(n, part=None):
                c = n % NC
                first, end = sequences(n, part)
                cols = slice(S * first, S * end)
                ve.wait_ge(den_out, n + 1 + (part or 0))
                settled(V.reciprocal(den[:, cols], den[:, cols]))
                dst, parts = oT[:, CW * c:CW * c + CW], [raw[:, cols], den[:, cols]]
                if n >= NC:
                    dst = oT[:, :].rearrange("p (s q b) -> p b q s", s=SP, q=NQ)[:, CB * c + first:CB * c + end, :, :]
                    parts = [ap.rearrange("p (b q s) -> p b q s", q=NQ, s=SP) for ap in parts]
                V.tensor_tensor(dst, *parts, ALU.mult).then_inc(context_ready, 1)

            def add_attention(n):
                src = full(ve, ("O", n))
                ve.wait_ge(bias_added, n + 1)
                part = xa[:, CT * n:CT * n + CT, :]
                flat = part.rearrange("p j d -> p (j d)")
                V.scalar_tensor_tensor(flat, src[:, :], gated[:, 0:1], flat, ALU.mult, ALU.add).then_inc(freed(("O", n)), 1)
                used(ve, ("O", n))
                measure(part, 2 + n % 2)

            def route_logits(c):
                src = full(ve, ("logits", c))[:, 0:CT * NE].rearrange("p (j e) -> p j e", e=NE)
                settled(V.tensor_reduce(r4[:, 0, :], src, AX.X, ALU.max))
                V.tensor_tensor(lg[:, :, :], src, r4[:, 0, :].unsqueeze(2).broadcast_to([P, CT, NE]),
                                ALU.subtract).then_inc(freed(("logits", c)), 1)

            def route(c):
                def bc(ap):
                    return ap.unsqueeze(2).broadcast_to([P, CT, NE])
                ve.wait_ge(route_exp, c + 1)
                settled(V.tensor_reduce(r4[:, 1, :], pr[:, :, :], AX.X, ALU.add))
                settled(V.reciprocal(r4[:, 2, :], r4[:, 1, :]))
                settled(V.tensor_tensor(pr[:, :, :], pr[:, :, :], bc(r4[:, 2, :]), ALU.mult))
                order = col(cf, CF, "first8").rearrange("p (j e) -> p j e", e=NE)
                for hot_, src_ in ((hot1, pr), (hot2, lw)):
                    settled(V.tensor_reduce(r4[:, 0, :], src_[:, :, :], AX.X, ALU.max))
                    settled(V.tensor_tensor(hot_[:, :, :], src_[:, :, :], bc(r4[:, 0, :]), ALU.is_equal))
                    settled(V.tensor_tensor(hot_[:, :, :], hot_[:, :, :], order, ALU.mult))
                    settled(V.tensor_reduce(r4[:, 1, :], hot_[:, :, :], AX.X, ALU.max))
                    settled(V.tensor_tensor(hot_[:, :, :], hot_[:, :, :], bc(r4[:, 1, :]), ALU.is_equal))
                    if hot_ is hot1:
                        settled(V.scalar_tensor_tensor(lw[:, :, :], hot1[:, :, :], -4.0, pr[:, :, :], ALU.mult, ALU.add))
                settled(V.tensor_tensor(hot1[:, :, :], hot1[:, :, :], hot2[:, :, :], ALU.add))
                settled(V.tensor_tensor(lw[:, :, :], hot1[:, :, :], pr[:, :, :], ALU.mult))
                if c >= 1:
                    filled(ve, ("weightT", c - 1))
                settled(V.tensor_copy(cw3[:, :, 0, :], lw[:, :, :]))
                settled(V.tensor_tensor(lw[:, :, :], lw[:, :, :], cw3[:, :, 0, :], ALU.subtract))
                settled(V.tensor_copy(cw3[:, :, 1, :], lw[:, :, :]))
                V.tensor_tensor(cw3[:, :, 2, :], lw[:, :, :], cw3[:, :, 1, :], ALU.subtract).then_inc(cw_ready, 1)

            def gate_up(c, p):
                ve.wait_ge(silu_done, (NP + 1) * c + p + 1)
                src = full(ve, ("U", c, p))
                turn = (NP + 1) * c + p
                V.tensor_tensor(gu[:, p, :], sil[:, turn % 2, :], src[:, :], ALU.mult).then_inc(freed(("U", c, p)), 1)

            def gate_shared(c):
                ve.wait_ge(silu_done, (NP + 1) * (c + 1))
                src = full(ve, ("shared", c))
                turn = (NP + 1) * c + NP
                V.tensor_tensor(gu[0:F, NP, :], sil[0:F, turn % 2, :], src[F:2 * F, :],
                                ALU.mult).then_inc(freed(("shared", c)), 1)

            def weigh(c, p):
                src = full(ve, ("W", c, p))
                if p == 0:
                    used(ve, ("U", c, NP - 1))
                V.tensor_tensor(hid[:, p, :], gu[:, p, :], src[:, :], ALU.mult).then_inc(freed(("W", c, p)), 1)

            def add_experts(c):
                src = full(ve, ("Y", c))
                part = xa[:, CT * c:CT * c + CT, :].rearrange("p j d -> p (j d)")
                V.scalar_tensor_tensor(part, src[:, :], gated[:, 1:2], part, ALU.mult, ALU.add).then_inc(freed(("Y", c)), 1)

            def mask_bias():
                ve.wait_ge(d_mask, 16)
                ve.wait_ge(mask_ready, 1)
                for k in range(2):
                    V.tensor_scalar(maskb[0:S, :, k, :], mask.rearrange("p (b t) -> p b t", b=B), 0.0, BIG,
                                    ALU.is_equal, ALU.mult).then_inc(mask_ready, 1)

            def biases(l):
                w, table = ((wa, WA), (wb, WB))[l]
                if l:
                    ve.wait_ge(d_wb, 16)
                else:
                    ve.wait_ge(d_wa, 16)
                    ve.wait_ge(d_cf, 16)
                    ve.wait_ge(gates_ready, 1)
                V.tensor_scalar(bqg[:, l, :], col(cf, CF, "gmask"), col(w, table, f"bq{l}"), None, ALU.mult)
                V.tensor_scalar(bki[:, l, :], col(cf, CF, "imask"), col(w, table, f"bk{l}"), None,
                                ALU.mult).then_inc(biases_ready, 1)
                src = full(ve, ("bias", l))
                V.tensor_tensor(obias[:, l, :], src[:, 0:D], col(w, table, f"bo{l}"), ALU.add).then_inc(freed(("bias", l)), 1)
                used(ve, ("bias", l))
                V.tensor_scalar(obias[:, l, :], obias[:, l, :], gated[:, 2 * l:2 * l + 1], None,
                                ALU.mult).then_inc(obias_ready, 1)
                if l:
                    wo = col(wb, WB, "wo1")
                    V.tensor_scalar(wo, wo, gated[:, 2:3], None, ALU.mult).then_inc(wo_gated, 1)


            def measure_residual(k):
                src = full(ve, ("O1", k))
                measure(src[:, :].rearrange("p (j d) -> p j d", d=D), k, True)

            def keep_residual(k):
                ve.wait_ge(hn_ready, k + 1)
                V.tensor_copy(xr[:, CT * k:CT * k + CT, :].rearrange("p j d -> p (j d)"),
                              full(ve, ("O1", k))[:, :]).then_inc(freed(("O1", k)), 1)

            def head_probabilities(a):
                half = slice(SP // 2 * a, SP // 2 * (a + 1))
                ve.wait_ge(gate_logits, SP // 2 * (a + 1))
                src = (bS, bC)[a][:, 0:SP * H1].rearrange("p (s h) -> p s h", h=H1)[:, half, :]

                def over(k):
                    return smr[:, k, half].unsqueeze(2).broadcast_to([P, SP // 2, H1])
                settled(V.tensor_reduce(smr[:, 0, half], src, AX.X, ALU.max))
                V.tensor_tensor(sm[:, half, :], src, over(0), ALU.subtract).then_inc(gate_exp, 1)
                ve.wait_ge(tl_exp, a + 1)
                settled(V.tensor_reduce(smr[:, 1, half], sm[:, half, :], AX.X, ALU.add))
                settled(V.reciprocal(smr[:, 2, half], smr[:, 1, half]))
                V.tensor_tensor(sm[:, half, :], sm[:, half, :], over(2), ALU.mult).then_inc(probs_ready, 1)

            def choose(a):
                src = full(ve, ("probT", a))[:, 0:P]
                V.tensor_copy(pt[:, a, :, :].rearrange("p q t -> p (q t)"), src).then_inc(freed(("probT", a)), 1)
                used(ve, ("probT", a))
                for q in range(NQ):
                    last = V.max(top8[:, NQ * a + q, :], pt[:, a, q, :])
                settled(last)
                for q in range(NQ):
                    last = V.max_index(top8_at[:, NQ * a + q, :], top8[:, NQ * a + q, :], pt[:, a, q, :])
                settled(last)
                sequence = col(cf, CF, "sequence").unsqueeze(1).broadcast_to([P, NQ, B])
                found = top8_at[:, NQ * a:NQ * a + NQ, :]
                first, second = (tm[:, r, a, :] for r in range(2))
                V.tensor_tensor(first, found[:, :, 0], found[:, :, 1], ALU.min)
                settled(V.tensor_tensor(second, found[:, :, 0], found[:, :, 1], ALU.max))
                for at, hot_ in ((first, o1), (second, o2)):
                    last = V.tensor_tensor(hot_[:, a, :, :], sequence,
                                           at.unsqueeze(2).broadcast_to([P, NQ, B]), ALU.is_equal)
                last.then_inc(hot_ready, 1)

            def place_choices(q):
                src = bG[place[("hotT",)][0]][32 * q:32 * q + 32, :].rearrange("p (c s h) -> p c s h", c=CAP, s=SP)
                return takeT[32 * q:32 * q + 32, :, q, :].rearrange("p s (c h) -> p c s h", c=CAP), src

            def choices_placed():
                ve.wait_ge(cleared, 6)
                full(ve, ("hotT",))
                for q in (0, 1):
                    last = V.tensor_copy(*place_choices(q))
                last.then_inc(take_v, 1)
                ve.wait_ge(take_a, 1)
                ve.wait_ge(take_v, 1)
                for q in range(NQ):
                    last = V.transpose(putT[32 * q:32 * q + 32, :, q, :], takeT[32 * q:32 * q + 32, :, q, :])
                last.then_inc(put_ready, 1)
                ve.wait_ge(put_ready, 1)
                V.tensor_copy(tm[:, 2, :, :], tm[:, 0, :, :]).then_inc(freed(("hotT",)), 1)

            def head_features(k):
                if k == 0:
                    ve.wait_ge(d_wl, 16)
                if k not in POOL_FEATURES:
                    src = full(ve, ("qkv", k))[:, 0:2 * 192].rearrange("p (c e) -> p c e", c=CAP)
                    V.tensor_tensor(qkv[:, k, :, :], src, feature_bias(k), ALU.add).then_inc(freed(("qkv", k)), 1)
                if k % 4 == 3:
                    used(ve, ("qkv", k))
                    used(ve, ("qkv", k - 1))
                    ve.wait_ge(biased, sum(p <= k for p in POOL_FEATURES))
                    if k > 3:
                        ve.wait_ge(att_ready, 2)
                    settled(V.tensor_tensor(*head_product(k, 0)))
                    att_v = att.rearrange("p (h i j) -> p h i j", i=2, j=2)
                    for j in range(2):
                        if j:
                            ve.wait_ge(prod_ready, k // 4 + 1)
                        V.tensor_reduce(att_v[:, k - 3:k + 1, :, j], head_product(k, j)[0], AX.X,
                                        ALU.add).then_inc(att_ready, 1)

            def head_softmax():
                src = full(ve, ("attT",))[0:32, 0:P].rearrange("p (b s) -> p b s", b=2)
                settled(V.tensor_reduce(ar[0:32, 0:2], src, AX.X, ALU.max))
                V.tensor_tensor(asT[0:32, :].rearrange("p (b s) -> p b s", b=2), src,
                                ar[0:32, 0:2].unsqueeze(2).broadcast_to([32, 2, S]), ALU.subtract).then_inc(freed(("attT",)), 1)
                ve.wait_ge(aexp_ready, 1)
                ex = aeT[0:32, :].rearrange("p (b s) -> p b s", b=2)
                settled(V.tensor_reduce(ar[0:32, 2:4], ex, AX.X, ALU.add))
                settled(V.reciprocal(ar[0:32, 4:6], ar[0:32, 2:4]))
                V.tensor_tensor(asT[0:32, :].rearrange("p (b s) -> p b s", b=2), ex,
                                ar[0:32, 4:6].unsqueeze(2).broadcast_to([32, 2, S]), ALU.mult).then_inc(attn_ready, 1)

            def head_averages():
                src = full(ve, ("attB",))
                V.tensor_copy(attn, src[:, 0:32]).then_inc(freed(("attB",)), 1)
                used(ve, ("attB",))
                at = 512
                for pairs in VECTOR_PAIRS:
                    products, total = weighted_values(pairs, at)
                    for operands in products:
                        last = V.tensor_tensor(*operands)
                    settled(last)
                    V.tensor_tensor(*total).then_inc(av_ready, 1)
                    at += 2 * 128 * (pairs.stop - pairs.start)

            def place_averages(k):
                if k % 2:
                    return
                ve.wait_ge(cleared, 7)
                src = full(ve, ("avT", k))
                for i in range(2):
                    last = V.tensor_copy(*average_part(src, k, i))
                last.then_inc(freed(("avT", k)), 1)

            def place_outputs(k):
                if k % 2:
                    return
                src = full(ve, ("ao", k))
                for c in range(CAP):
                    last = V.tensor_scalar(*output_part(src, k, c), col(wl, WL, "bo"), None, ALU.add)
                last.then_inc(freed(("ao", k)), 1)

            def add_heads(k):
                src = full(ve, ("back", k))
                tokens = src[:, :].rearrange("p (j d) -> p j d", d=D)
                measure(tokens, k, True)
                if k == LAST:
                    ln_g = col(wl, WL, "ln_g")
                    for j in range(CT):
                        t = CT * k + j
                        last = V.scalar_tensor_tensor(y[:, t, :], tokens[:, j, :], mean_var[:, t, 0:1], ln_g,
                                                      ALU.subtract, ALU.mult)
                    last.then_inc(centred, 1)

            def finish(k):
                part = slice(CT * k, CT * k + CT)
                if k == LAST:
                    ve.wait_ge(centred, 1)
                    ve.wait_ge(rstd_ready, measured[k])
                    for j in range(CT):
                        t = CT * k + j
                        last = V.scalar_tensor_tensor(y[:, t, :], y[:, t, :], rstd[:, t:t + 1], xr[:, t, :],
                                                      ALU.mult, ALU.add)
                    last.then_inc(last_out_ready, 1)
                    return
                used(ve, ("back", k))
                if k == 0:
                    ve.wait_ge(out_bias, 1)
                V.tensor_tensor(y[:, part, :], y[:, part, :],
                                col(wl, WL, "ln_g").unsqueeze(1).broadcast_to([P, CT, D]), ALU.mult).then_inc(scaled, 1)

            part = {"bias": biases, "mask": mask_bias, "measure": measure_tokens, "norm": norm_tokens, "Q": spread_queries,
                    "Q2": spread_other_queries, "round": round_queries,
                    "low": row_maximum, "split": split_maxima, "maxT": spread_shift, "evacuate": evacuate,
                    "divide": divide, "O": add_attention, "fnorm": norm_for_experts, "logits": route_logits,
                    "route": route, "U": gate_up, "gated": gate_shared, "W": weigh, "Y": add_experts,
                    "O1": measure_residual, "keep": keep_residual, "probs": head_probabilities,
                    "choose": choose, "hotT": choices_placed, "qkv": head_features, "attT": head_softmax,
                    "attB": head_averages, "avT": place_averages, "ao": place_outputs, "back": add_heads,
                    "finish": finish}
            for stage, *where in plan:
                if stage in part:
                    part[stage](*where)

        @block.scalar
        def _(ae):
            A = nc.scalar

            def spread_some(n, heads):
                l = n // NC
                ae.wait_ge(biases_ready, l + 1)
                src = full(ae, ("K", n))
                for i in range(*heads):
                    ins = A.activation(Ki[:, n % 2, :, i, :], src[:, :].rearrange("p (b s) -> p b s", b=CB),
                                       ACT.Identity, bias=bki[:, l, i:i + 1], scale=col(cf, CF, "imask")[:, i:i + 1])
                return ins

            def spread_keys(n):
                spread_some(n, (0, NI // 2))

            def spread_other_keys(n):
                spread_some(n, (NI // 2, NI)).then_inc(freed(("K", n)), 1)
                used(ae, ("K", n))
                round_keys(n, 0)

            def round_keys(n, half):
                part = slice(CB // 2 * half, CB // 2 * (half + 1))
                A.activation(Kb[:, n % 2, part, :, :], Ki[:, n % 2, part, :, :], ACT.Copy).then_inc(low_k, 1)

            def place_values(n, half):
                if n < 2:
                    ae.wait_ge(cleared, n + 1)
                src = full(ae, ("V", n, half))[:, :].rearrange("p (b g r) -> p b g r", b=4, g=NG)
                for i in range(NI):
                    ip, i2 = divmod(i, 2)
                    rows = slice(64 * i2, 64 * i2 + 64)
                    dst = V2[rows, n % 2, 4 * half:4 * half + 4, ip, :].rearrange("p b (g r) -> p b g r", g=NG)
                    ins = A.activation(dst[:, :, :, DH * i:DH * i + DH], src[rows, :, :, DH * i:DH * i + DH], ACT.Copy)
                ins.then_inc(freed(("V", n, half)), 1)

            def copy_xT(n):
                src = full(ae, ("xT", n))
                A.activation(xT[:, n % 2, :], src[:, :], ACT.Copy).then_inc(freed(("xT", n)), 1)

            def exponentials(n, b):
                k = CB * n + b
                ae.wait_ge(scoresT_done, k + 1)
                if k >= 3:
                    ae.wait_ge(pv_done, k - 2)
                A.activation(pT[:, k % 3, :], bT[k % 2][:, :], ACT.Exp, scale=SCALE).then_inc(exp_done, 1)

            def evacuate(n, part=None):
                first, end = sequences(n, part)
                ae.wait_ge(pv_done, CB * n + end)
                if n >= 1:
                    ae.wait_ge(context_ready, n)
                cols = slice(S * first, S * end)
                A.activation(den[:, cols], sum_banks(n, first)[1][:, cols], ACT.Copy).then_inc(den_out, 1)

            def route_exponentials(c):
                used(ae, ("logits", c))
                A.activation(pr[:, :, :], lg[:, :, :], ACT.Exp).then_inc(route_exp, 1)

            def silu_parts(job, c, p):
                src = full(ae, job)
                k = (NP + 1) * c + p
                if k >= 2:
                    ae.wait_ge(silu_done, k - 1)
                A.activation(th[:, k % 2, :], src[:, :], ACT.Tanh, scale=0.5).then_inc(tanh_done, 1)
                copy = A.activation(gh[:, k % 2, :], src[:, :], ACT.Copy, scale=0.5)
                if p < NP:
                    copy.then_inc(freed(job), 1)
                ae.wait_ge(tanh_done, k + 1)
                A.activation(th[:, k % 2, :], th[:, k % 2, :], ACT.Copy, bias=1.0).then_inc(parts_ready, 1)

            def silu_gate(c, p):
                silu_parts(("G", c, p), c, p)

            def silu_shared(c):
                silu_parts(("shared", c), c, NP)

            def copy_weights(c):
                src = full(ae, ("weightT", c))
                if c == 0:
                    ae.wait_ge(cleared, 3)
                A.activation(cwT[0:3 * NE, :], src[0:3 * NE, :].bitcast(BF16)[:, 0:CW],
                             ACT.Copy).then_inc(freed(("weightT", c)), 1)

            def copy_fT(n):
                src = full(ae, ("fT", n))
                A.activation(fT[:, :], src[:, :], ACT.Copy).then_inc(freed(("fT", n)), 1)

            def normalise(src, dst, slot, turn, done):
                ae.wait_ge(offset_ready, turn + 1)
                for j in range(CT):
                    t = CT * slot + j
                    ins = A.activation(dst[:, j, :], src[:, j, :], ACT.Identity, scale=rstd[:, t:t + 1],
                                       bias=offset[:, t:t + 1])
                ins.then_inc(done, 1)

            def norm_last(k):
                src = full(ae, ("O1", k))[:, :].rearrange("p (j d) -> p j d", d=D)
                normalise(src, hn[:, CT * k:CT * k + CT, :], k, k, hn_ready)

            def norm_out(k):
                if k == LAST:
                    return
                src = full(ae, ("back", k))[:, :].rearrange("p (j d) -> p j d", d=D)
                normalise(src, y[:, CT * k:CT * k + CT, :], k, NT // CT + k, freed(("back", k)))

            def copy_hT(k):
                src = full(ae, ("hT", k))
                A.activation(cT[:, CW * k:CW * k + CW], src[:, :], ACT.Copy).then_inc(freed(("hT", k)), 1)

            def head_exponentials(a):
                half = sm[:, SP // 2 * a:SP // 2 * (a + 1), :]
                ae.wait_ge(gate_exp, a + 1)
                A.activation(half, half, ACT.Exp).then_inc(tl_exp, 1)

            def place_choices():
                ae.wait_ge(cleared, 6)
                src = full(ae, ("hotT",))
                for q in (2, 3):
                    rows_ = slice(32 * q, 32 * q + 32)
                    last = A.activation(takeT[rows_, :, q, :].rearrange("p s (c h) -> p c s h", c=CAP),
                                        src[rows_, :].rearrange("p (c s h) -> p c s h", c=CAP, s=SP), ACT.Copy)
                last.then_inc(take_a, 1)

            def place_tokens(k):
                src = full(ae, ("take", k))[:, :].rearrange("p (s q c h) -> p c h q s", s=CT, q=NQ, c=CAP)
                for c in range(CAP):
                    dst = hT[:, :, c, :].rearrange("p h (q s) -> p h q s", q=NQ)[:, :, :, CT * k:CT * k + CT]
                    ins = A.activation(dst, src[:, c, :, :, :], ACT.Copy)
                ins.then_inc(freed(("take", k)), 1)

            def copy_features(k):
                if k in POOL_FEATURES:
                    src = full(ae, ("qkv", k))[:, 0:2 * 192].rearrange("p (c e) -> p c e", c=CAP)
                    A.activation(qkv[:, k, :, :], src, ACT.Copy).then_inc(freed(("qkv", k)), 1)

            def place_averages(k):
                if k % 2 == 0:
                    return
                ae.wait_ge(cleared, 7)
                src = full(ae, ("avT", k))
                for i in range(2):
                    last = A.activation(*average_part(src, k, i), ACT.Copy)
                last.then_inc(freed(("avT", k)), 1)

            def place_outputs(k):
                if k % 2 == 0:
                    return
                src = full(ae, ("ao", k))
                for c in range(CAP):
                    last = A.activation(*output_part(src, k, c), ACT.Identity, bias=col(wl, WL, "bo"))
                last.then_inc(freed(("ao", k)), 1)

            def head_score_exponentials():
                used(ae, ("attT",))
                A.activation(aeT[0:32, :], asT[0:32, :], ACT.Exp, scale=SCALE1).then_inc(aexp_ready, 1)

            def copy_outputs(k):
                src = full(ae, ("aoT", k))
                A.activation(ao[:, CT * k:CT * k + CT, :].rearrange("p j d -> p (j d)"), src[:, :],
                             ACT.Copy).then_inc(freed(("aoT", k)), 1)

            ae.wait_ge(d_wa, 16)
            A.activation(gated[:, :], col(wa, WA, "gates"), ACT.Tanh).then_inc(gates_ready, 1)
            part = {"xT": copy_xT, "K": spread_keys, "K2": spread_other_keys, "round": round_keys,
                    "V": place_values, "scores": exponentials,
                    "evacuate": evacuate, "fT": copy_fT, "logits": route_exponentials, "G": silu_gate,
                    "shared": silu_shared, "weightT": copy_weights, "hnorm": norm_last, "hT": copy_hT,
                    "probs": head_exponentials, "hotT": place_choices, "take": place_tokens,
                    "qkv": copy_features, "attT": head_score_exponentials, "avT": place_averages, "ao": place_outputs,
                    "aoT": copy_outputs, "finish": norm_out}
            for stage, *where in plan:
                if stage in part:
                    part[stage](*where)

        @block.gpsimd
        def _(ge):
            G = nc.gpsimd
            roots = [0]

            def inverse_deviation(slot):
                ge.wait_ge(var_ready, roots[0] + 1)
                roots[0] += 1
                part = slice(CT * slot, CT * slot + CT)
                G.tensor_tensor(rstd[:, part], var_eps[:, part], half_neg[:, part], ALU.pow).then_inc(rstd_ready, 1)

            def last_deviation(k):
                inverse_deviation(k)
                ge.wait_ge(rstd_ready, roots[0])
                tiles = slice(CT * k, CT * k + CT)
                G.tensor_tensor(offset[:, tiles], neg_mean[:, tiles], rstd[:, tiles], ALU.mult).then_inc(offset_ready, 1)

            def token_deviation(n):
                inverse_deviation(n % 2)

            def expert_deviation(c):
                inverse_deviation(2 + c % 2)

            def add_bias(n):
                if n >= NC:
                    return
                ge.wait_ge(normed, n + 1)
                ge.wait_ge(obias_ready, 1)
                part = xa[:, CT * n:CT * n + CT, :]
                G.tensor_tensor(part, part, obias[:, 0:1, :].broadcast_to([P, CT, D]), ALU.add).then_inc(bias_added, 1)

            def clear():
                G.memset(V2[:, 0, :, :, :], 0.0).then_inc(cleared, 1)
                G.memset(V2[:, 1, :, :, :], 0.0).then_inc(cleared, 1)
                G.memset(cwT[:, :], 0.0).then_inc(cleared, 1)
                G.memset(gu[:, NP, :], 0.0).then_inc(cleared, 1)
                ge.wait_ge(cleared, 4)
                G.memset(maskb[S:P, :, :, :], 0.0).then_inc(mask_ready, 1)
                ge.wait_ge(mask_ready, 1)

            def silu(c, p):
                turn = (NP + 1) * c + p
                ge.wait_ge(parts_ready, turn + 1)
                if p >= 2:
                    used(ge, ("U", c, p - 2))
                elif c >= 1:
                    used(ge, ("shared", c - 1) if p else ("U", c - 1, NP - 1))
                G.tensor_tensor(sil[:, turn % 2, :], th[:, turn % 2, :], gh[:, turn % 2, :],
                                ALU.mult).then_inc(silu_done, 1)

            def silu_shared(c):
                silu(c, NP)

            pool_steps = [1]

            def ge_step(ins):
                pool_steps[0] += 1
                ins.then_inc(pool_step, 1)
                ge.wait_ge(pool_step, pool_steps[0])

            def last_bias():
                ge.wait_ge(d_xr, 16 * NQ)
                ge.wait_ge(obias_ready, 2)
                G.tensor_tensor(xr[:, :, :], xr[:, :, :], obias[:, 1:2, :].broadcast_to([P, SP, D]),
                                ALU.add).then_inc(bias_added, 1)
                filled(ge, ("Y", NC - 1))
                G.memset(takeT, 0.0).then_inc(cleared, 1)
                G.memset(putT, 0.0).then_inc(cleared, 1)

            def head_products(k):
                if k == 0:
                    ge.wait_ge(d_wl, 16)
                if k in POOL_FEATURES:
                    used(ge, ("qkv", k))
                    G.tensor_tensor(qkv[:, k, :, :], qkv[:, k, :, :], feature_bias(k), ALU.add).then_inc(biased, 1)
                if k % 4 == 3:
                    used(ge, ("qkv", k))
                    used(ge, ("qkv", k - 1))
                    ge.wait_ge(biased, sum(p <= k for p in POOL_FEATURES))
                    if k > 3:
                        ge.wait_ge(att_ready, 2)
                    G.tensor_tensor(*head_product(k, 1)).then_inc(prod_ready, 1)

            def head_averages():
                used(ge, ("attB",))
                products, total = weighted_values(POOL_PAIRS, 0)
                for operands in products:
                    last = G.tensor_tensor(*operands)
                ge_step(last)
                G.tensor_tensor(*total).then_inc(av_pool_ready, 1)

            def add_residual(k):
                tiles = slice(CT * k, CT * k + CT)
                if k == LAST:
                    return
                ge.wait_ge(scaled, k + 1)
                G.tensor_tensor(y[:, tiles, :], y[:, tiles, :], xr[:, tiles, :], ALU.add).then_inc(out_ready, 1)

            def out_share(k):
                if k != NT // CT - 1:
                    return
                ge.wait_ge(hn_ready, NT // CT)
                G.memset(avT, 0.0).then_inc(cleared, 1)
                ge.wait_ge(d_wl, 16)
                g = gated[:, 3:4]
                for tiles in range(NT // CT):
                    used(ge, ("O1", tiles))
                ge_step(G.tensor_scalar(col(wl, WL, "ln_b"), col(wl, WL, "ln_b"), g, None, ALU.mult))
                ge_step(G.tensor_scalar(col(wl, WL, "ln_g"), col(wl, WL, "ln_g"), g, None, ALU.mult))
                G.tensor_tensor(xr[:, :, :], xr[:, :, :], col(wl, WL, "ln_b").unsqueeze(1).broadcast_to([P, SP, D]),
                                ALU.add).then_inc(out_bias, 1)

            G.memset(half_neg[:, :], -0.5).then_inc(pool_step, 1)
            ge.wait_ge(pool_step, 1)
            part = {"measure": token_deviation, "norm": add_bias, "clear": clear,
                    "O": expert_deviation, "G": silu,
                    "shared": silu_shared, "last_bias": last_bias,
                    "O1": last_deviation, "hnorm": out_share, "qkv": head_products, "attB": head_averages,
                    "back": last_deviation, "finish": add_residual}
            for stage, *where in plan:
                if stage in part:
                    part[stage](*where)


def shape_constants():
    row = np.arange(P)
    cf = np.zeros((P, CF_N), np.float32)
    cb = np.zeros((P, CBF_N), np.float32)

    def f(name):
        a, w = CF[name]
        return cf[:, a:a + w]

    def b(name):
        a, w = CBF[name]
        return cb[:, a:a + w]
    f("ident")[:] = np.eye(P)
    f("gmask")[:] = (row[:, None] // 32) == np.arange(NG)
    f("imask")[:] = (row[:, None] // DH % NI) == np.arange(NI)
    gp, i = row // 4 % 2, row % 4
    f("cmask")[:] = (i[:, None] // 2 == np.arange(4) // 2) & (gp[:, None] == np.arange(4) % 2)
    r = np.arange(64)
    f("ones_v")[:] = (r[None] % 32 // DH) == 2 * (r[None] // 32) + row[:, None] // 64
    f("first8")[:] = NE - np.arange(CT * NE) % NE
    f("sequence")[:] = np.arange(B)
    b("ident")[:] = np.eye(P)
    seq = row // 8 % CB
    pick = (seq[:, None, None] == np.arange(CB)[None, :, None]) & (i[:, None, None] % 2 == row[None, None, :] // 64)
    b("pick")[:] = pick.reshape(P, -1)
    ex = (row[:, None] < 3 * NE) & (row[:, None] % NE == np.arange(NE * F)[None] // F)
    b("experts")[:] = ex
    b("twice")[:] = row[:, None] == row[None] % S
    return cf, cb


def kernel(**inputs):
    import ml_dtypes
    import concourse.bacc as bacc
    from concourse.bass_utils import run_bass_kernel_spmd

    a = {k: np.asarray(v) for k, v in inputs.items()}

    def pack(table, n, parts):
        t = np.zeros((P, n), np.float32)
        for name, v in parts.items():
            first, w = table[name]
            t[:v.shape[0], first:first + w] = v.reshape(v.shape[0], w)
        return t

    def diagonal(w):
        t = np.zeros((P, P), np.float32)
        for h in range(NG * NI):
            t[DH * h:DH * h + DH, DH * h:DH * h + DH] = w[h].T
        return t

    def rows(v):
        return np.broadcast_to(v, (P, v.size))

    cf, cb = shape_constants()
    w_a = pack(WA, WA_N, {
        "wq0": diagonal(a["L0_xattn_wq"]), "wk0": diagonal(a["L0_xattn_wk"]), "wv0": diagonal(a["L0_xattn_wv"]),
        "wo0": a["L0_xattn_wo"].T, "bo0": rows(a["L0_xattn_bo"]), "bq0": a["L0_xattn_bq"].reshape(P, 1),
        "bk0": a["L0_xattn_bk"].reshape(P, 1), "bv0": a["L0_xattn_bv"].reshape(P, 1),
        "gates": rows(np.stack([a["g_xattn"][0], a["g_ffn"][0], a["g_xattn"][1], a["g_ffn"][1]])),
        "gate_w": a["L0_ffn_gate_w"].T})
    w_b = pack(WB, WB_N, {
        "wq1": a["L1_xattn_W0"].T, "wk1": a["L1_xattn_W1"].T, "wv1": a["L1_xattn_W2"].T, "wo1": a["L1_xattn_W3"].T,
        "bo1": rows(a["L1_xattn_b3"]), "bq1": a["L1_xattn_b0"].reshape(P, 1),
        "bk1": a["L1_xattn_b1"].reshape(P, 1), "bv1": a["L1_xattn_b2"].reshape(P, 1)})
    w_f = pack(WF, WF_N, {
        "wg": a["L0_ffn_wg"].reshape(NE * F, D).T, "wu": a["L0_ffn_wu"].reshape(NE * F, D).T,
        "shared": np.concatenate([a["L0_ffn_sg"], a["L0_ffn_su"]], 0).T,
        "wd": a["L0_ffn_wd"].transpose(0, 2, 1).reshape(NP, 2 * F, D).transpose(1, 0, 2).reshape(P, -1),
        "sd": a["L0_ffn_sd"].T})
    wo = a["L1_ffn_Wo"].transpose(1, 0, 2).reshape(E1, -1)
    bqkv = np.concatenate([a["L1_ffn_bq"], a["L1_ffn_bkv"]], -1).reshape(H1 // 2, 2, 3 * E1)
    w_l = pack(WL, WL_N, {
        "Wg": a["L1_ffn_Wg"], "bo": a["L1_ffn_bo"].reshape(P, 1), "ln_g": rows(a["L1_ffn_ln_g"]),
        "ln_b": rows(a["L1_ffn_ln_b"]), "Wo": np.concatenate([wo, wo], 0),
        "Wqkv": np.concatenate([a["L1_ffn_Wq"], a["L1_ffn_Wkv"]], -1).transpose(1, 0, 2).reshape(D, -1),
        "bqkv": np.concatenate([np.broadcast_to(bqkv[:, k].reshape(1, -1), (S, H1 // 2 * 3 * E1)) for k in range(2)], 0)})
    arrays = {
        "x": np.ascontiguousarray(a["x"]),
        "ctxT": np.ascontiguousarray(a["ctx_1024"].reshape(B * S, D).T),
        "maskT": np.ascontiguousarray(a["mask_BxSxS2_if1"].transpose(1, 0, 2).reshape(S, B * S)),
        "const_f": cf, "const_b": cb.astype(ml_dtypes.bfloat16),
        "w_a": w_a, "w_b": w_b, "w_f": w_f, "w_l": w_l}
    nc = bacc.Bacc("TRN2", target_bir_lowering=False, num_devices=1)
    args = [nc.dram_tensor(f"in_{k}", v.shape, mybir.dt.from_np(v.dtype), kind="ExternalInput").ap()
            for k, v in arrays.items()]
    args.append(nc.dram_tensor("out", (B, S, D), F32, kind="ExternalOutput").ap())
    two_layers(nc, *args)
    r = run_bass_kernel_spmd(nc, [{f"in_{k}": v for k, v in arrays.items()}], core_ids=[0])
    return r.results[0]["out"]
```
